# Optimizing a Trainium2 kernel written in Bass

```python
import numpy as np
import jax
import jax.numpy as jnp

def _softmax(x, axis=-1):
    return jax.nn.softmax(x, axis=axis)

def _gelu(x):
    return jax.nn.gelu(x, approximate=True)

def _silu(x):
    return jax.nn.silu(x)

def _sigmoid(x):
    return jax.nn.sigmoid(x)

def _layernorm(x, axis=-1, eps=1e-05):
    m = jnp.mean(x, axis=axis, keepdims=True)
    v = jnp.var(x, axis=axis, keepdims=True)
    return (x - m) / jnp.sqrt(v + eps)

def _scatter_add(tgt, idx, src, axis=0):
    return tgt.at[idx].add(src)

def _segment_sum(src, seg, n):
    return jax.ops.segment_sum(src, seg, n)
kernel_name = 'mk_lm_tower_d1_tok_ids4096_r4_ce0cf0'

def setup_inputs(seed: int=0):
    np.random.seed(seed)
    _w = jnp.asarray

    def _rec_inputs():
        import jax
        import jax.numpy as jnp
        _rk = jax.random.key(seed)
        x = jax.random.randint(jax.random.fold_in(_rk, 1), (1, 2048), 0, 31993, jnp.int32)
        mask_BS_i1_0 = jnp.where(jnp.ones((1, 2048), dtype=bool), 1, 0).astype(jnp.int32)
        mask_BS_i0_1 = jnp.where(jnp.ones((1, 2048), dtype=bool), 0, 1).astype(jnp.int32)
        return (x, mask_BS_i1_0, mask_BS_i0_1)
    x, mask_BS_i1_0, mask_BS_i0_1 = _rec_inputs()

    def _L0_tok_setup():
        import jax, jax.numpy as jnp
        import numpy as np
        V, D, R = (8000, 1024, 128)
        B, S = (2, 1024)
        SCALE = 2.0
        PAD = 0
        key = jax.random.key(seed)
        ks = jax.random.split(key, 12)
        inp = {'x': jax.random.randint(ks[0], (B, S), 0, V, dtype=jnp.int32), 'cl_mask': jax.random.randint(ks[1], (B, S), 0, 2, dtype=jnp.int32), 'lm_mask': jax.random.randint(ks[2], (B, S), 0, 2, dtype=jnp.int32), 'cl_prime_mask': jax.random.randint(ks[3], (B, S), 0, 2, dtype=jnp.int32), 'weight': jax.random.normal(ks[4], (V, D), dtype=jnp.float32) * 0.02, 'lora_A_cl': jax.random.normal(ks[5], (V, R), dtype=jnp.float32) * 0.02, 'lora_B_cl': jax.random.normal(ks[6], (R, D), dtype=jnp.float32), 'lora_A_lm': jax.random.normal(ks[7], (V, R), dtype=jnp.float32) * 0.02, 'lora_B_lm': jax.random.normal(ks[8], (R, D), dtype=jnp.float32), 'lora_A_cl_prime': jax.random.normal(ks[9], (V, R), dtype=jnp.float32) * 0.02, 'lora_B_cl_prime': jax.random.normal(ks[10], (R, D), dtype=jnp.float32)}
        return inp
    _L0_tok_all = _L0_tok_setup()
    _L0_tok_in = {k: v for k, v in _L0_tok_all.items() if k in ('weight', 'lora_A_cl', 'lora_B_cl', 'lora_A_lm', 'lora_B_lm', 'lora_A_cl_prime', 'lora_B_cl_prime')}
    del _L0_tok_all

    def _L0_attn_setup():
        import jax, jax.numpy as jnp
        import numpy as np
        import math
        HIDDEN = 1024
        NUM_HEADS = 32
        HEAD_DIM = HIDDEN // NUM_HEADS
        SCALE = 1.0 / HEAD_DIM

        def _alibi_slopes(n_heads: int) -> np.ndarray:
            cp2 = 2 ** math.floor(math.log2(n_heads))
            base = 2 ** (-2 ** (-(math.log2(cp2) - 3)))
            slopes = base ** np.arange(1, cp2 + 1, dtype=np.float32)
            if cp2 != n_heads:
                extra_base = 2 ** (-2 ** (-(math.log2(2 * cp2) - 3)))
                n_rem = min(cp2, n_heads - cp2)
                extra = extra_base ** np.arange(1, 1 + 2 * n_rem, 2, dtype=np.float32)
                slopes = np.concatenate([slopes, extra])
            return slopes.astype(np.float32)
        key = jax.random.key(seed)
        k1, k2, k3, k4, k5 = jax.random.split(key, 5)
        B, S = (2, 512)
        return {'hidden_states': jax.random.normal(k1, (B, S, HIDDEN), dtype=jnp.float32), 'w_attn': jax.random.normal(k2, (HIDDEN, 3 * HIDDEN), dtype=jnp.float32) * 0.02, 'b_attn': jnp.zeros((3 * HIDDEN,), dtype=jnp.float32), 'w_proj': jax.random.normal(k3, (HIDDEN, HIDDEN), dtype=jnp.float32) * 0.02, 'b_proj': jnp.zeros((HIDDEN,), dtype=jnp.float32)}
    _L0_attn_all = _L0_attn_setup()
    _L0_attn_in = {k: v for k, v in _L0_attn_all.items() if k in ('w_attn', 'b_attn', 'w_proj', 'b_proj')}
    del _L0_attn_all

    def _L0_ffn_setup():
        import jax, jax.numpy as jnp
        import numpy as np
        SCALING = 32.0 / 16.0
        key = jax.random.key(seed)
        ks = jax.random.split(key, 7)
        B, T, D, O, R, E = (4, 512, 1024, 1024, 16, 8)
        x = jax.random.normal(ks[0], (B, T, D), dtype=jnp.float32)
        base_W = jax.random.normal(ks[1], (O, D), dtype=jnp.float32) * D ** (-0.5)
        base_b = jax.random.normal(ks[2], (O,), dtype=jnp.float32) * 0.01
        router_W = jax.random.normal(ks[3], (2 * E - 1, D), dtype=jnp.float32) * D ** (-0.5)
        router_b = jax.random.normal(ks[4], (2 * E - 1,), dtype=jnp.float32) * 0.01
        A = jax.random.normal(ks[5], (E, R, D), dtype=jnp.float32) * D ** (-0.5)
        Bm = jax.random.normal(ks[6], (E, O, R), dtype=jnp.float32) * R ** (-0.5)
        assigned_idx = 0
        others = [i for i in range(E) if i != assigned_idx]
        expert_map = jnp.array([assigned_idx] * E + others, dtype=jnp.int32)
        return {'x': x, 'base_W': base_W, 'base_b': base_b, 'router_W': router_W, 'router_b': router_b, 'A': A, 'B': Bm, 'expert_map': expert_map}
    _L0_ffn_all = _L0_ffn_setup()
    _L0_ffn_in = {k: v for k, v in _L0_ffn_all.items() if k in ('base_W', 'base_b', 'router_W', 'router_b', 'A', 'B', 'expert_map')}
    del _L0_ffn_all
    return {'x': x, 'mask_BS_i1_0': mask_BS_i1_0, 'mask_BS_i0_1': mask_BS_i0_1, 'L0_tok_weight': _L0_tok_in['weight'], 'L0_tok_lora_A_cl': _L0_tok_in['lora_A_cl'], 'L0_tok_lora_B_cl': _L0_tok_in['lora_B_cl'], 'L0_tok_lora_A_lm': _L0_tok_in['lora_A_lm'], 'L0_tok_lora_B_lm': _L0_tok_in['lora_B_lm'], 'L0_tok_lora_A_cl_prime': _L0_tok_in['lora_A_cl_prime'], 'L0_tok_lora_B_cl_prime': _L0_tok_in['lora_B_cl_prime'], 'L0_attn_w_attn': _L0_attn_in['w_attn'], 'L0_attn_b_attn': _L0_attn_in['b_attn'], 'L0_attn_w_proj': _L0_attn_in['w_proj'], 'L0_attn_b_proj': _L0_attn_in['b_proj'], 'L0_ffn_base_W': _L0_ffn_in['base_W'], 'L0_ffn_base_b': _L0_ffn_in['base_b'], 'L0_ffn_router_W': _L0_ffn_in['router_W'], 'L0_ffn_router_b': _L0_ffn_in['router_b'], 'L0_ffn_A': _L0_ffn_in['A'], 'L0_ffn_B': _L0_ffn_in['B'], 'L0_ffn_expert_map': _L0_ffn_in['expert_map']}

def reference(x, mask_BS_i1_0, mask_BS_i0_1, L0_tok_weight, L0_tok_lora_A_cl, L0_tok_lora_B_cl, L0_tok_lora_A_lm, L0_tok_lora_B_lm, L0_tok_lora_A_cl_prime, L0_tok_lora_B_cl_prime, L0_attn_w_attn, L0_attn_b_attn, L0_attn_w_proj, L0_attn_b_proj, L0_ffn_base_W, L0_ffn_base_b, L0_ffn_router_W, L0_ffn_router_b, L0_ffn_A, L0_ffn_B, L0_ffn_expert_map):
    import jax
    import jax.numpy as jnp

    def _L0_tok_ref(x, cl_mask, lm_mask, cl_prime_mask, weight, lora_A_cl, lora_B_cl, lora_A_lm, lora_B_lm, lora_A_cl_prime, lora_B_cl_prime):
        import jax, jax.numpy as jnp
        import numpy as np
        V, D, R = (8000, 1024, 128)
        B, S = (2, 1024)
        SCALE = 2.0
        PAD = 0
        result = weight[x]
        for A, Bm, m in ((lora_A_cl, lora_B_cl, cl_mask), (lora_A_lm, lora_B_lm, lm_mask), (lora_A_cl_prime, lora_B_cl_prime, cl_prime_mask)):
            after_A = A[x * m]
            result = result + SCALE * jnp.einsum('bsr,rd->bsd', after_A, Bm)
        return result

    def _L0_attn_ref(hidden_states, w_attn, b_attn, w_proj, b_proj):
        import jax, jax.numpy as jnp
        import numpy as np
        import math
        HIDDEN = 1024
        NUM_HEADS = 32
        HEAD_DIM = HIDDEN // NUM_HEADS
        SCALE = 1.0 / HEAD_DIM

        def _alibi_slopes(n_heads: int) -> np.ndarray:
            cp2 = 2 ** math.floor(math.log2(n_heads))
            base = 2 ** (-2 ** (-(math.log2(cp2) - 3)))
            slopes = base ** np.arange(1, cp2 + 1, dtype=np.float32)
            if cp2 != n_heads:
                extra_base = 2 ** (-2 ** (-(math.log2(2 * cp2) - 3)))
                n_rem = min(cp2, n_heads - cp2)
                extra = extra_base ** np.arange(1, 1 + 2 * n_rem, 2, dtype=np.float32)
                slopes = np.concatenate([slopes, extra])
            return slopes.astype(np.float32)
        B, S, _ = hidden_states.shape
        H, D = (NUM_HEADS, HEAD_DIM)
        qkv = hidden_states @ w_attn + b_attn
        q, k, v = jnp.split(qkv, 3, axis=-1)
        q = q.reshape(B, S, H, D)
        k = k.reshape(B, S, H, D)
        v = v.reshape(B, S, H, D)
        scores = jnp.einsum('bqhd,bkhd->bhqk', q, k) * SCALE
        slopes = jnp.asarray(_alibi_slopes(H))
        pos = jnp.arange(S)
        rel = pos[None, :] - pos[:, None]
        bias = slopes[:, None, None] * rel[None, :, :]
        causal = rel <= 0
        scores = jnp.where(causal[None, None], scores + bias[None], -jnp.inf)
        attn = jax.nn.softmax(scores, axis=-1)
        out = jnp.einsum('bhqk,bkhd->bqhd', attn, v).reshape(B, S, HIDDEN)
        return out @ w_proj + b_proj

    def _L0_ffn_ref(x, base_W, base_b, router_W, router_b, A, B, expert_map):
        import jax, jax.numpy as jnp
        import numpy as np
        SCALING = 32.0 / 16.0
        E = A.shape[0]
        base_out = jnp.einsum('btd,od->bto', x, base_W) + base_b
        logits = jnp.einsum('btd,nd->btn', x, router_W) + router_b
        probs = jax.nn.softmax(logits, axis=-1)
        topk_p, topk_i = jax.lax.top_k(probs, E)
        mapped = expert_map[topk_i]
        onehot = (mapped[..., None] == jnp.arange(E)).astype(x.dtype)
        w = jnp.einsum('btk,btke->bte', topk_p, onehot)
        h = jnp.einsum('btd,erd->bter', x, A)
        lora = jnp.einsum('bter,eor->bto', h * w[..., None], B) * SCALING
        return base_out + lora
    h = _L0_tok_ref(x, mask_BS_i1_0, mask_BS_i0_1, mask_BS_i0_1, L0_tok_weight, L0_tok_lora_A_cl, L0_tok_lora_B_cl, L0_tok_lora_A_lm, L0_tok_lora_B_lm, L0_tok_lora_A_cl_prime, L0_tok_lora_B_cl_prime)
    h = h + _L0_attn_ref(_layernorm(h, axis=-1), L0_attn_w_attn, L0_attn_b_attn, L0_attn_w_proj, L0_attn_b_proj)
    h = h + _L0_ffn_ref(_layernorm(h, axis=-1), L0_ffn_base_W, L0_ffn_base_b, L0_ffn_router_W, L0_ffn_router_b, L0_ffn_A, L0_ffn_B, L0_ffn_expert_map)
    return h

_drawn_inputs = setup_inputs


def setup_inputs(seed=0):
    import zlib

    import numpy as np

    out = dict(_drawn_inputs(seed))
    spreads = {'L0_attn_b_attn': (0.0, 0.1), 'L0_attn_b_proj': (0.0, 0.1)}
    factors = {'L0_ffn_base_b': 8.0, 'L0_ffn_router_b': 8.0}
    for name, (base, spread) in spreads.items():
        noise = np.random.default_rng([zlib.crc32(name.encode()), seed]).standard_normal(out[name].shape)
        drawn = base * np.exp(spread * noise) if base else spread * noise
        out[name] = jnp.asarray(drawn.astype(out[name].dtype))
    for name, factor in factors.items():
        out[name] = (out[name] * factor).astype(out[name].dtype)
    return out
```

```python
from contextlib import ExitStack

import numpy as np
import concourse.bass as bass
from concourse import mybir

F32 = mybir.dt.float32
F32R = mybir.dt.float32r
I32 = mybir.dt.int32
ALU = mybir.AluOpType
ACT = mybir.ActivationFunctionType
AX_X = mybir.AxisListType.X

P = 128
T = 2048
NT = T // P
D = 1024
KT = D // P
HALF = 512
V = 8000
R = 128
LORA = 3
TOK_SCALE = 2.0
EPS = 1e-5

H = 32
HD = D // H
QG = 4
NG = NT // QG
ATT_SCALE = 1.0 / HD
CHUNK = 1024
MASKED = -1.0e36

E = 8
ER = 128
NR = 2 * E - 1
ZW = ER + NR + 1
FFN_SCALE = 2.0


def repeat(eng, n, body, peel=1):
    for i in range(peel):
        body(i)
    with eng.Fori(peel, n - 1) as i:
        body(i)
    body(n - 1)


def after(eng, sem, value):
    if isinstance(value, int) and value <= 0:
        return
    eng.wait_ge(sem, value)


def after_plainly(eng, passed, sem, value):
    after(eng, sem, value)
    if not isinstance(value, int):
        eng.sem_inc(passed, 1)


class Chain:

    def __init__(self, eng, sem, passed=None):
        self.eng, self.sem, self.passed, self.base, self.n, self.per = eng, sem, passed, 0, 0, None

    def begin(self, i):
        if self.per is None and not (isinstance(i, int) and i == 0):
            self.per = self.n - self.start
        if isinstance(i, int) and i == 0:
            self.start = self.n
            self.base = 0
        else:
            self.base = i * self.per + self.start
            self.n = 0

    def link(self, ins, plainly=False):
        self.n += 1
        ins.then_inc(self.sem, 1)
        if plainly:
            after_plainly(self.eng, self.passed, self.sem, self.base + self.n)
        else:
            self.eng.wait_ge(self.sem, self.base + self.n)


def product3(pe, out, ah, al, bh, bl, start, stop):
    pe.matmul(out, ah, bh, start=start, stop=False)
    pe.matmul(out, ah, bl, start=False, stop=False)
    return pe.matmul(out, al, bh, start=False, stop=stop)


def wide(t):
    return t.bitcast(F32)


def phase_embed(nc, a, xh, xl, ident, ident_made):
    with ExitStack() as ctx:
        sb = lambda n, s, d=F32: ctx.enter_context(nc.sbuf_tensor(n, s, d))
        ps = lambda n, s: ctx.enter_context(nc.psum_tensor(n, s, F32))
        sem = lambda n: ctx.enter_context(nc.semaphore(n))
        ids = sb("ids", [P, 3 * NT], I32)
        ids_f = sb("ids_f", [P, 3, NT])
        wrap = sb("wrap", [P, 3, NT])
        rows = sb("rows", [P, NT, 3], I32)
        row_now = [sb(f"row_now{b}", [P, 3], I32) for b in range(2)]
        lb_raw = sb("lb_raw", [P, LORA, D])
        lb_h = sb("lb_h", [P, LORA, D], F32R)
        lb_l = sb("lb_l", [P, LORA, D], F32R)
        w_row = [sb(f"w_row{b}", [P, D]) for b in range(2)]
        xn = [sb(f"xn{b}", [P, D]) for b in range(2)]
        a_row = [sb(f"a_row{b}", [P, LORA * R]) for b in range(2)]
        at_h = [sb(f"at_h{b}", [P, LORA, P], F32R) for b in range(2)]
        at_l = [sb(f"at_l{b}", [P, LORA, P], F32R) for b in range(2)]
        stats = sb("stats", [P, 2, 6])
        mv = sb("mv", [P, 2])
        sd = sb("sd", [P, 4])
        p_at = [ps(f"p_at{b}", [P, 4, P])[:, 0:LORA, :] for b in range(2)]
        p_lora = ps("p_lora", [P, D])
        p_xt = [ps(f"p_xt{b}", [P, KT, P]) for b in range(2)]

        ids_in = sem("ids_in")
        lb_in = sem("lb_in")
        lb_high = sem("lb_high")
        lb_split = sem("lb_split")
        rows_ready = sem("rows_ready")
        row_copied = sem("row_copied")
        gathered = [sem(f"gathered{b}") for b in range(2)]
        at_done = sem("at_done")
        at_high = sem("at_high")
        at_split = sem("at_split")
        lora_done = sem("lora_done")
        h_ready = sem("h_ready")
        h_stored = [sem(f"h_stored{b}") for b in range(2)]
        var_ready = sem("var_ready")
        root_ready = sem("root_ready")
        xn_ready = sem("xn_ready")
        xt_done = sem("xt_done")
        xt_high = sem("xt_high")
        xt_split = sem("xt_split")
        idx_step = sem("idx_step")
        ln_step = sem("ln_step")
        block = ctx.enter_context(nc.Block())

        @block.sync
        def _(sp):
            sp.dma_start(ids[:], a["ids"]).then_inc(ids_in, 16)
            sp.dma_start(lb_raw[:], a["lora_b"]).then_inc(lb_in, 16)

            def tile(i):
                for b in range(2):
                    t = 2 * i + b
                    after(sp, h_ready, t + 1)
                    sp.dma_start(a["h_dram"][bass.ds(t, 1)].rearrange("a p d -> (a p) d"), w_row[b][:]).then_inc(h_stored[b], 16)
            repeat(sp, NT // 2, tile)
            for b in range(2):
                sp.wait_ge(h_stored[b], 16 * NT // 2)

        @block.gpsimd
        def _(pool):
            passed = nc.alloc_semaphore("passed1")
            pool.memset(ident[:], 0.0).then_inc(ident_made, 1)
            pool.wait_ge(ident_made, 1)
            pool.affine_select(out=ident[:], in_=ident[:], compare_op=ALU.not_equal, fill=1.0,
                               base=0, pattern=[[-1, P]], channel_multiplier=1).then_inc(ident_made, 1)
            pool.wait_ge(rows_ready, 1)

            def tile(i):
                for b in range(2):
                    t = 2 * i + b
                    after_plainly(pool, passed, gathered[b], 48 * i)
                    pool.tensor_copy(row_now[b][:], rows[:, bass.ds(t, 1), :].rearrange("p a k -> p (a k)")).then_inc(row_copied, 1)
                    after(pool, at_done, t - 1)
                    after(pool, xn_ready, t - 1)
                    after(pool, h_stored[b], 16 * i)
                    after_plainly(pool, passed, row_copied, t + 1)
                    for k, (table, dst) in enumerate(((a["tok_w"], w_row[b][:]), (a["tok_a1"], a_row[b][:, 0:R]),
                                                      (a["tok_a2"], a_row[b][:, R:LORA * R]))):
                        pool.indirect_dma_start(dst, None, table, bass.IndirectOffsetOnAxis(ap=row_now[b][:, k:k + 1], axis=0)
                                                ).then_inc(gathered[b], 16)
            repeat(pool, NT // 2, tile)

        @block.vector
        def _(dve):
            passed = nc.alloc_semaphore("passed2")
            idx = Chain(dve, idx_step)
            dve.wait_ge(ids_in, 16)
            idx.link(dve.tensor_copy(ids_f[:].rearrange("p a t -> p (a t)"), ids[:]))
            for k in (1, 2):
                idx.link(dve.tensor_tensor(ids_f[:, k, :], ids_f[:, 0, :], ids_f[:, k, :], ALU.mult))
            idx.link(dve.tensor_scalar(wrap[:], ids_f[:], 0.0, float(V), ALU.is_lt, ALU.mult))
            idx.link(dve.tensor_tensor(ids_f[:], ids_f[:], wrap[:], ALU.add))
            idx.link(dve.tensor_scalar(ids_f[:], ids_f[:], 0.0, float(V - 1), ALU.max, ALU.min))
            dve.tensor_copy(rows[:].rearrange("p t k -> p k t"), ids_f[:]).then_inc(rows_ready, 1)
            dve.wait_ge(lb_high, 1)
            dve.tensor_tensor(lb_l[:], lb_raw[:], wide(lb_h[:]), ALU.subtract).then_inc(lb_split, 1)
            ln = Chain(dve, ln_step, passed)

            def split_xt(t, b, col):
                after(dve, xt_high, t + 1)
                dve.tensor_tensor(xl[:, :, bass.ds(col, P)], p_xt[b][:], wide(xh[:, :, bass.ds(col, P)]),
                                  ALU.subtract).then_inc(xt_split, 1)

            def tile(i):
                ln.begin(i)
                for b in range(2):
                    t = 2 * i + b
                    after(dve, at_high, t + 1)
                    dve.tensor_tensor(at_l[b][:], p_at[b], wide(at_h[b][:]), ALU.subtract).then_inc(at_split, 1)
                    dve.wait_ge(gathered[b], 48 * i + 48)
                    dve.wait_ge(lora_done, t + 1)
                    ln.link(dve.scalar_tensor_tensor(out=w_row[b][:], in0=p_lora[:], scalar=TOK_SCALE, in1=w_row[b][:],
                                                     op0=ALU.mult, op1=ALU.add))
                    for k in range(2):
                        ins = dve.bn_stats(stats[:, k, :], w_row[b][:, k * HALF:(k + 1) * HALF])
                        if k == 0:
                            ins.then_inc(h_ready, 1)
                    ln.link(ins, plainly=True)
                    ln.link(dve.bn_aggr(mv[:], stats[:]))
                    dve.tensor_scalar(sd[:, 0:1], mv[:, 1:2], EPS, None, ALU.add).then_inc(var_ready, 1)
                    dve.wait_ge(root_ready, t + 1)
                    ln.link(dve.reciprocal(sd[:, 2:3], sd[:, 1:2]))
                    ln.link(dve.scalar_tensor_tensor(out=sd[:, 3:4], in0=sd[:, 2:3], scalar=sd[:, 0:1], in1=sd[:, 1:2],
                                                     op0=ALU.mult, op1=ALU.add))
                    ln.link(dve.tensor_scalar(sd[:, 2:3], sd[:, 3:4], 0.5, None, ALU.mult))
                    ln.link(dve.reciprocal(sd[:, 3:4], sd[:, 2:3]))
                    after(dve, xt_done, t - 1)
                    dve.tensor_scalar(xn[b][:], w_row[b][:], mv[:, 0:1], sd[:, 3:4], ALU.subtract, ALU.mult
                                      ).then_inc(xn_ready, 1)
                    if b == 1:
                        split_xt(t - 1, 0, (t - 1) * P)
                    elif not (isinstance(i, int) and i == 0):
                        split_xt(t - 1, 1, (t - 1) * P)
            repeat(dve, NT // 2, tile, 2)
            split_xt(NT - 1, 1, (NT - 1) * P)

        @block.scalar
        def _(act):
            act.wait_ge(lb_in, 16)
            act.activation(lb_h[:], lb_raw[:], ACT.Copy).then_inc(lb_high, 1)

            def high_xt(t, b, col):
                after(act, xt_done, t + 1)
                act.activation(xh[:, :, bass.ds(col, P)], p_xt[b][:], ACT.Copy).then_inc(xt_high, 1)

            def tile(i):
                for b in range(2):
                    t = 2 * i + b
                    act.wait_ge(at_done, t + 1)
                    after(act, lora_done, t - 1)
                    act.activation(at_h[b][:], p_at[b], ACT.Copy).then_inc(at_high, 1)
                    act.wait_ge(var_ready, t + 1)
                    act.activation(sd[:, 1:2], sd[:, 0:1], ACT.Sqrt).then_inc(root_ready, 1)
                    if b == 1:
                        high_xt(t - 1, 0, (t - 1) * P)
                    elif not (isinstance(i, int) and i == 0):
                        high_xt(t - 1, 1, (t - 1) * P)
            repeat(act, NT // 2, tile, 2)
            high_xt(NT - 1, 1, (NT - 1) * P)

        @block.tensor
        def _(pe):
            pe.wait_ge(ident_made, 2)
            pe.wait_ge(lb_split, 1)
            pe.wait_ge(lb_high, 1)

            def turn_x(t, b):
                pe.wait_ge(xn_ready, t + 1)
                after(pe, xt_split, t - 1)
                for k in range(KT):
                    last = pe.transpose(p_xt[b][:, k, :], xn[b][:, k * P:(k + 1) * P], ident[:])
                last.then_inc(xt_done, 1)

            def tile(i):
                for b in range(2):
                    t = 2 * i + b
                    pe.wait_ge(gathered[b], 48 * i + 48)
                    after(pe, at_split, t - 1)
                    for k in range(LORA):
                        last = pe.transpose(p_at[b][:, k, :], a_row[b][:, k * R:(k + 1) * R], ident[:])
                    last.then_inc(at_done, 1)
                    pe.wait_ge(at_split, t + 1)
                    after(pe, h_ready, t)
                    for c in range(2):
                        n = slice(c * HALF, (c + 1) * HALF)
                        for k in range(LORA):
                            last = product3(pe, p_lora[:, n], at_h[b][:, k, :], at_l[b][:, k, :],
                                            lb_h[:, k, n], lb_l[:, k, n], k == 0, k == LORA - 1)
                    last.then_inc(lora_done, 1)
                    if b == 1:
                        turn_x(t - 1, 0)
                    elif not (isinstance(i, int) and i == 0):
                        turn_x(t - 1, 1)
            repeat(pe, NT // 2, tile, 2)
            turn_x(NT - 1, 1)


def phase_qkv(nc, a, xh, xl, ident):
    with ExitStack() as ctx:
        sb = lambda n, s, d=F32: ctx.enter_context(nc.sbuf_tensor(n, s, d))
        ps = lambda n, s: ctx.enter_context(nc.psum_tensor(n, s, F32))
        sem = lambda n: ctx.enter_context(nc.semaphore(n))
        NB = T // HALF
        TB = HALF // P
        w_raw = [sb(f"wq_raw{b}", [P, KT, P]) for b in range(3)]
        w_h = [sb(f"wq_h{b}", [P, KT, P], F32R) for b in range(3)]
        w_l = [sb(f"wq_l{b}", [P, KT, P], F32R) for b in range(3)]
        bias = sb("qkv_bias", [P, 3, KT])
        y = [sb(f"y{k}", [P, HALF]) for k in range(2)]
        y_h = [sb(f"y_h{k}", [P, HALF], F32R) for k in range(NB)]
        y_l = [sb(f"y_l{k}", [P, HALF], F32R) for k in range(NB)]
        v_out = [sb(f"v_out{k}", [P, 2, TB, 2 * HD]) for k in range(2)]
        p_y = [ps(f"p_y{k}", [P, HALF]) for k in range(NB)]
        p_vt = [ps(f"p_vt{k}", [P, TB, P]) for k in range(2)]

        bias_in = sem("bias_in")
        w_in = [sem(f"wq_in{b}") for b in range(3)]
        w_high = sem("wq_high")
        w_split = sem("wq_split")
        y_done = sem("y_done")
        y_biased = sem("y_biased")
        y_high = sem("y_high")
        y_split = sem("y_split")
        vt_done = sem("vt_done")
        v_ready = sem("v_ready")
        qk_stored = [sem(f"qk_stored{k}") for k in range(NB)]
        v_stored = [sem(f"v_stored{k}") for k in range(2)]
        block = ctx.enter_context(nc.Block())

        def staggered(eng, n, first, then):
            def body(i):
                for b in range(3):
                    first(i, b)
                    if b:
                        then(i, b - 1)
                    elif not (isinstance(i, int) and i == 0):
                        then(i - 1, 2)
            repeat(eng, n, body, 2)
            then(n - 1, 2)

        @block.sync
        def _(sp):
            sp.dma_start(bias[:], a["b_qkv"]).then_inc(bias_in, 16)

            def load(i, b):
                after(sp, w_split, 3 * (i - 1) + b + 1)
                sp.dma_start(w_raw[b][:].rearrange("p k c -> p (k c)"),
                             a["w_qkv"][bass.ds(3 * i + b, 1)].rearrange("a p n -> (a p) n")).then_inc(w_in[b], 16)

            def store(i, b):
                for k in range(NB):
                    if b < 2:
                        sp.wait_ge(y_split, 2 * NB * i + NB * b + k + 1)
                        to = (bass.ds(i * P, P), slice(k * HALF, (k + 1) * HALF))
                        sp.dma_start(a[("qh", "kh")[b]][to], wide(y_h[k][:])).then_inc(qk_stored[k], 16)
                        sp.dma_start(a[("ql", "kl")[b]][to], wide(y_l[k][:])).then_inc(qk_stored[k], 16)
                    else:
                        sp.wait_ge(v_ready, NB * i + k + 1)
                        sp.dma_start(a["v_dram"][bass.ds(2 * i, 2), :, TB * k:TB * k + TB, :].rearrange("a p t d -> p a (t d)"),
                                     v_out[k % 2][:].rearrange("p a t d -> p a (t d)")).then_inc(v_stored[k % 2], 16)
            staggered(sp, KT, load, store)
            for k in range(NB):
                sp.wait_ge(qk_stored[k], 4 * 16 * KT)
            for k in range(2):
                sp.wait_ge(v_stored[k], 2 * 16 * KT)

        @block.scalar
        def _(act):
            def weights(i, b):
                act.wait_ge(w_in[b], 16 * i + 16)
                after(act, y_done, NB * (3 * (i - 1) + b + 1))
                act.activation(w_h[b][:], w_raw[b][:], ACT.Copy).then_inc(w_high, 1)

            def results(i, b):
                for k in range(NB):
                    if b < 2:
                        act.wait_ge(y_biased, NB * (3 * i + b) + k + 1)
                        after(act, qk_stored[k], 32 * (2 * i + b))
                        act.activation(y_h[k][:], y[k % 2][:], ACT.Copy).then_inc(y_high, 1)
                    else:
                        act.wait_ge(vt_done, NB * i + k + 1)
                        after(act, v_stored[k % 2], 16 * (2 * i + k // 2))
                        act.activation(v_out[k % 2][:].rearrange("p a t d -> p t a d"), p_vt[k % 2][:].rearrange(
                            "p t (a d) -> p t a d", a=2), ACT.Copy).then_inc(v_ready, 1)
            staggered(act, KT, weights, results)

        @block.vector
        def _(dve):
            dve.wait_ge(bias_in, 16)

            def weights(i, b):
                dve.wait_ge(w_high, 3 * i + b + 1)
                dve.tensor_tensor(w_l[b][:], w_raw[b][:], wide(w_h[b][:]), ALU.subtract).then_inc(w_split, 1)

            def results(i, b):
                for k in range(NB):
                    at = NB * (3 * i + b) + k
                    dve.wait_ge(y_done, at + 1)
                    if b == 2 and k >= 2:
                        dve.wait_ge(vt_done, NB * i + k - 1)
                    elif b == 0 and k < 2:
                        after(dve, vt_done, NB * (i - 1) + k + 3)
                    else:
                        dve.wait_ge(y_split, 2 * NB * i + NB * b + k - 1)
                    dve.tensor_scalar(y[k % 2][:], p_y[k][:], bias[:, b, bass.ds(i, 1)], ATT_SCALE if b == 0 else 1.0,
                                      ALU.add, ALU.mult).then_inc(y_biased, 1)
                    if b < 2:
                        dve.wait_ge(y_high, 2 * NB * i + NB * b + k + 1)
                        dve.tensor_tensor(y_l[k][:], y[k % 2][:], wide(y_h[k][:]), ALU.subtract).then_inc(y_split, 1)
            staggered(dve, KT, weights, results)

        @block.tensor
        def _(pe):
            def turn_v(i, k):
                pe.wait_ge(y_biased, NB * (3 * i + 2) + k + 1)
                after(pe, v_ready, NB * i + k - 1)
                for t in range(TB):
                    last = pe.transpose(p_vt[k % 2][:, t, :], y[k % 2][:, t * P:(t + 1) * P], ident[:])
                last.then_inc(vt_done, 1)

            def cols(i):
                for b in range(3):
                    g = 3 * i + b
                    pe.wait_ge(w_split, g + 1)
                    for k in range(NB):
                        after(pe, y_biased, NB * (g - 1) + k + 1)
                        n = slice(k * HALF, (k + 1) * HALF)
                        for c in range(KT):
                            last = product3(pe, p_y[k][:], w_h[b][:, c, :], w_l[b][:, c, :], xh[:, c, n], xl[:, c, n],
                                            c == 0, c == KT - 1)
                        last.then_inc(y_done, 1)
                        if b == 0 and not (isinstance(i, int) and i == 0):
                            turn_v(i - 1, k)
            repeat(pe, KT, cols, 2)
            for k in range(NB):
                turn_v(KT - 1, k)


def phase_attention(nc, a, o, ident):
    with ExitStack() as ctx:
        sb = lambda n, s, d=F32: ctx.enter_context(nc.sbuf_tensor(n, s, d))
        ps = lambda n, s: ctx.enter_context(nc.psum_tensor(n, s, F32))
        sem = lambda n: ctx.enter_context(nc.semaphore(n))
        PAIRS = H // 2
        UNITS = 2 * NG
        DIAG = (NT - 1) * P
        tiles = [QG * (u % NG) + QG for u in range(UNITS)]
        pieces = [[(q, c) for q in range(QG) for c in range(0, P * (QG * (u % NG) + q + 1), CHUNK)] for u in range(UNITS)]
        TILES, PIECES = sum(tiles), sum(len(x) for x in pieces)
        tile0 = [sum(tiles[:u]) for u in range(UNITS)]
        piece0 = [sum(len(x) for x in pieces[:u]) for u in range(UNITS)]

        slopes = sb("slopes", [P, H])
        rel = sb("rel", [P, T])
        bias = [sb(f"bias{b}", [P, T]) for b in range(2)]
        slope_now = sb("slope_now", [P, 2])
        qs = [sb(f"qs{b}", [P, T], F32R) for b in range(2)]
        ks = [sb(f"ks{b}", [P, T], F32R) for b in range(2)]
        v_pair = sb("v_pair", [P, NT, 2, HD])
        vs = [sb(f"vs{b}", [P, NT, HD]) for b in range(2)]
        s = [[sb(f"s{u}{q}", [P, T]) for q in range(QG)] for u in range(2)]
        top = sb("top", [P, 2, QG, 2])
        shift = sb("shift", [P, 2, QG])
        total = sb("total", [P, 2, QG])
        share = sb("share", [P, 2, QG])
        pt = [sb(f"pt{k}", [P, HALF]) for k in range(4)]
        ot = sb("ot", [HD, HALF])
        p_s = [ps(f"p_s{k}", [P, CHUNK]) for k in range(2)]
        p_t = [ps(f"p_t{k}", [P, HALF]) for k in range(2)]
        p_o = ps("p_o", [P, HALF])
        p_on = ps("p_on", [P, HALF // HD, HD])[:, 0:QG, :]

        slopes_in = sem("slopes_in")
        rel_made = sem("rel_made")
        slope_got = sem("slope_got")
        bias_made = sem("bias_made")
        stack_in = [sem(f"stack_in{b}") for b in range(2)]
        v_in = sem("v_in")
        vs_made = sem("vs_made")
        s_done = sem("s_done")
        s_biased = sem("s_biased")
        top_made = sem("top_made")
        shift_made = sem("shift_made")
        exp_done = sem("exp_done")
        pt_done = sem("pt_done")
        pt_even = sem("pt_even")
        pt_odd = sem("pt_odd")
        pv_done = sem("pv_done")
        ot_copied = sem("ot_copied")
        on_done = sem("on_done")
        share_made = sem("share_made")
        o_made = sem("o_made")
        block = ctx.enter_context(nc.Block())

        def slots(i, u):
            u1, i1 = (u + 1, i) if u + 1 < UNITS else (0, i + 1)
            nxt = None if isinstance(i1, int) and i1 == PAIRS else (i1, u1)
            at = [q * tiles[u] // QG for q in range(QG)]
            for k in range(tiles[u] + 1):
                yield (k, nxt, [q for q in range(QG) if nxt and at[q] == k], [q for q in range(QG) if nxt and at[q] + 1 == k])

        @block.sync
        def _(sp):
            sp.dma_start(slopes[:], a["slopes"]).then_inc(slopes_in, 16)

            def pair(i):
                for b in range(2):
                    after(sp, s_done, PIECES * (i - 1) + piece0[NG * b + NG - 1] + len(pieces[NG - 1]))
                    row = bass.ds((2 * i + b) * HD, HD)
                    for n, (q, k) in enumerate((("qh", "kh"), ("ql", "kh"), ("qh", "kl"), ("ql", "kl"))):
                        sp.dma_start(wide(qs[b][n * HD:(n + 1) * HD, :]), a[q][row, :]).then_inc(stack_in[b], 16)
                        sp.dma_start(wide(ks[b][n * HD:(n + 1) * HD, :]), a[k][row, :]).then_inc(stack_in[b], 16)
                    if b == 0:
                        after(sp, vs_made, 2 * i)
                        sp.dma_start(v_pair[:].rearrange("p t a d -> p (t a d)"),
                                     a["v_dram"][bass.ds(i, 1)].rearrange("a p t d -> (a p) (t d)")).then_inc(v_in, 16)
            repeat(sp, PAIRS, pair)

        @block.gpsimd
        def _(pool):
            passed = nc.alloc_semaphore("passed3")
            pool.iota(rel[:], pattern=[[1, T]], base=-DIAG, channel_multiplier=-1,
                      allow_small_or_imprecise_dtypes=True).then_inc(rel_made, 1)
            pool.wait_ge(rel_made, 1)
            pool.affine_select(out=rel[:], in_=rel[:], compare_op=ALU.is_ge, fill=MASKED, base=DIAG,
                               pattern=[[-1, T]], channel_multiplier=1).then_inc(rel_made, 1)
            pool.wait_ge(rel_made, 2)
            pool.wait_ge(slopes_in, 16)

            def pair(i):
                for b in range(2):
                    h = 2 * i + b
                    pool.tensor_copy(slope_now[:, b:b + 1], slopes[:, bass.ds(h, 1)]).then_inc(slope_got, 1)
                    pool.wait_ge(slope_got, h + 1)
                    after_plainly(pool, passed, s_biased, PIECES * (i - 1) + piece0[NG * b + NG - 1] + len(pieces[NG - 1]))
                    pool.tensor_scalar(bias[b][:], rel[:], slope_now[:, b:b + 1], None, ALU.mult).then_inc(bias_made, 1)
                    pool.wait_ge(v_in, 16 * i + 16)
                    after_plainly(pool, passed, pv_done, TILES * (i - 1) + tile0[NG * b + NG - 1] + tiles[NG - 1])
                    pool.tensor_copy(vs[b][:], v_pair[:, :, b, :]).then_inc(vs_made, 1)
            repeat(pool, PAIRS, pair)

        @block.vector
        def _(dve):
            passed = nc.alloc_semaphore("passed4")
            def score(i, u, q):
                b, g = u // NG, u % NG
                U = UNITS * i + u
                if q == 0:
                    dve.wait_ge(bias_made, 2 * i + b + 1)
                    after(dve, pt_done, TILES * i + tile0[u - 1] if u else TILES * (i - 1) + tile0[UNITS - 1])
                base = P * (QG * g + q)
                mine = [n for n, x in enumerate(pieces[u]) if x[0] == q]
                for n in mine:
                    at = PIECES * i + piece0[u] + n
                    c = pieces[u][n][1]
                    w = min(CHUNK, base + P - c)
                    after_plainly(dve, passed, s_done, at + 1)
                    dve.tensor_tensor_reduce(s[u % 2][q][:, c:c + w], p_s[n % 2][:, 0:w],
                                             bias[b][:, DIAG - base + c:DIAG - base + c + w], 1.0, MASKED,
                                             ALU.add, ALU.max, top[:, u % 2, q, c // CHUNK:c // CHUNK + 1]).then_inc(s_biased, 1)
                dve.wait_ge(s_biased, at + 1)
                n = UNITS * QG * i + QG * u + q
                dve.tensor_reduce(top[:, u % 2, q, 0:1], top[:, u % 2, q, 0:len(mine)], AX_X, ALU.max).then_inc(top_made, 1)
                dve.wait_ge(top_made, n + 1)
                dve.tensor_scalar(shift[:, u % 2, q:q + 1], top[:, u % 2, q, 0:1], -1.0, None, ALU.mult).then_inc(shift_made, 1)

            def divide(i, u):
                b, g = u // NG, u % NG
                dve.wait_ge(on_done, UNITS * i + u + 1)
                to = o[:, QG * g:QG * g + QG, bass.ds((2 * i + b) * HD, HD)]
                dve.tensor_tensor(to, p_on, share[:, u % 2, :].unsqueeze(2).to_broadcast([P, QG, HD]), ALU.mult
                                  ).then_inc(o_made, 1)

            def pair(i):
                for u in range(UNITS):
                    U = UNITS * i + u
                    dve.wait_ge(exp_done, QG * (U + 1))
                    dve.reciprocal(share[:, u % 2, :], total[:, u % 2, :]).then_inc(share_made, 1)
                    for k, nxt, now, _ in slots(i, u):
                        for q in now:
                            score(*nxt, q)
                        if k % 2 == 1:
                            w = P * max(0, k - QG * (u % NG))
                            at = TILES * i + tile0[u] + k
                            dve.wait_ge(pt_done, at + 1)
                            after(dve, pv_done, at - 3)
                            dve.tensor_copy(pt[k % 4][:, w:], p_t[1][:, w:]).then_inc(pt_odd, 1)
                        if k == 1 and not (isinstance(i, int) and i == 0 and u == 0):
                            divide(*((i, u - 1) if u else (i - 1, UNITS - 1)))
            for q in range(QG):
                score(0, 0, q)
            repeat(dve, PAIRS, pair)
            divide(PAIRS - 1, UNITS - 1)

        @block.scalar
        def _(act):
            def exponentials(i, u, q):
                U = UNITS * i + u
                n = P * (QG * (u % NG) + q + 1)
                act.wait_ge(shift_made, QG * U + q + 1)
                if q == 0:
                    after(act, share_made, U - 1)
                act.activation(s[u % 2][q][:, 0:n], s[u % 2][q][:, 0:n], ACT.Exp, bias=shift[:, u % 2, q:q + 1],
                               accum_out=total[:, u % 2, q:q + 1]).then_inc(exp_done, 1)

            def copy_out(i, u):
                act.wait_ge(pv_done, TILES * i + tile0[u] + tiles[u])
                after(act, on_done, UNITS * i + u)
                act.activation(ot[:], p_o[0:HD, :], ACT.Copy).then_inc(ot_copied, 1)

            def pair(i):
                for u in range(UNITS):
                    if not (isinstance(i, int) and i == 0 and u == 0):
                        copy_out(*((i, u - 1) if u else (i - 1, UNITS - 1)))
                    for k, nxt, _, late in slots(i, u):
                        if k < tiles[u] and k % 2 == 0:
                            w = P * max(0, k - QG * (u % NG))
                            at = TILES * i + tile0[u] + k
                            act.wait_ge(pt_done, at + 1)
                            after(act, pv_done, at - 3)
                            act.activation(pt[k % 4][:, w:], p_t[0][:, w:], ACT.Copy).then_inc(pt_even, 1)
                        for q in late:
                            exponentials(*nxt, q)
            for q in range(QG):
                exponentials(0, 0, q)
            repeat(act, PAIRS, pair)
            copy_out(PAIRS - 1, UNITS - 1)

        @block.tensor
        def _(pe):
            passed = nc.alloc_semaphore("passed5")
            def score(i, u, q):
                b, g = u // NG, u % NG
                if g == 0 and q == 0:
                    pe.wait_ge(stack_in[b], 8 * 16 * (i + 1))
                base = P * (QG * g + q)
                for n, (mine, c0) in enumerate(pieces[u]):
                    if mine != q:
                        continue
                    at = PIECES * i + piece0[u] + n
                    after(pe, s_biased, at - 1)
                    end = min(c0 + CHUNK, base + P)
                    for c in range(c0, end, HALF):
                        w = min(HALF, end - c)
                        last = pe.matmul(p_s[n % 2][:, c - c0:c - c0 + w], qs[b][:, base:base + P], ks[b][:, c:c + w],
                                         start=True, stop=True)
                    last.then_inc(s_done, 1)

            def turn(i, u, k):
                at = TILES * i + tile0[u] + k
                if k == 0:
                    pe.wait_ge(exp_done, QG * (UNITS * i + u + 1))
                after(pe, (pt_even, pt_odd)[k % 2], TILES // 2 * i + (tile0[u] + k) // 2)
                for q in range(max(0, k - QG * (u % NG)), QG):
                    last = pe.transpose(p_t[k % 2][:, q * P:(q + 1) * P], s[u % 2][q][:, k * P:(k + 1) * P], ident[:])
                last.then_inc(pt_done, 1)

            def weigh(i, u, k):
                b = u // NG
                if k == 0:
                    after(pe, ot_copied, UNITS * i + u)
                    if u % NG == 0:
                        pe.wait_ge(vs_made, 2 * i + b + 1)
                pe.wait_ge((pt_even, pt_odd)[k % 2], TILES // 2 * i + (tile0[u] + k) // 2 + 1)
                w = P * max(0, k - QG * (u % NG))
                pe.matmul(p_o[0:HD, w:], vs[b][:, k, :], pt[k % 4][:, w:], start=(k == 0), stop=(k == tiles[u] - 1)
                          ).then_inc(pv_done, 1)

            def turn_out(i, u):
                U = UNITS * i + u
                pe.wait_ge(ot_copied, U + 1)
                after_plainly(pe, passed, o_made, U)
                for q in range(QG):
                    last = pe.transpose(p_on[:, q, :], ot[:, q * P:(q + 1) * P], ident[0:HD, 0:HD])
                last.then_inc(on_done, 1)

            def pair(i):
                for u in range(UNITS):
                    turn(i, u, 0)
                    for k, nxt, now, _ in slots(i, u):
                        for q in now:
                            score(*nxt, q)
                        if k + 1 < tiles[u]:
                            turn(i, u, k + 1)
                        if k < tiles[u]:
                            weigh(i, u, k)
                        if k == 0 and not (isinstance(i, int) and i == 0 and u == 0):
                            turn_out(*((i, u - 1) if u else (i - 1, UNITS - 1)))
            for q in range(QG):
                score(0, 0, q)
            repeat(pe, PAIRS, pair)
            turn_out(PAIRS - 1, UNITS - 1)


def root_of_variance(dve, ln, act_root_ready, count, sd, rstd):
    dve.wait_ge(act_root_ready, count)
    ln.link(dve.reciprocal(sd[:, 2:3], sd[:, 1:2]))
    ln.link(dve.scalar_tensor_tensor(out=sd[:, 3:4], in0=sd[:, 2:3], scalar=sd[:, 0:1], in1=sd[:, 1:2],
                                     op0=ALU.mult, op1=ALU.add))
    ln.link(dve.tensor_scalar(sd[:, 2:3], sd[:, 3:4], 0.5, None, ALU.mult))
    return dve.reciprocal(rstd, sd[:, 2:3])


def phase_project(nc, a, o, norm, ident):
    with ExitStack() as ctx:
        sb = lambda n, s, d=F32: ctx.enter_context(nc.sbuf_tensor(n, s, d))
        ps = lambda n, s: ctx.enter_context(nc.psum_tensor(n, s, F32))
        sem = lambda n: ctx.enter_context(nc.semaphore(n))
        w_raw = [sb(f"wp_raw{k}", [P, D]) for k in range(2)]
        w_h = sb("wp_h", [P, KT, D], F32R)
        w_l = sb("wp_l", [P, KT, D], F32R)
        bias = sb("p_bias", [P, D])
        h_in = [sb(f"h_in{b}", [P, D]) for b in range(2)]
        o_now = [sb(f"o_now{b}", [P, D]) for b in range(2)]
        a_h = [sb(f"a_h{b}", [P, KT, P], F32R) for b in range(2)]
        a_l = [sb(f"a_l{b}", [P, KT, P], F32R) for b in range(2)]
        stats = sb("stats2", [P, 2, 6])
        mv = sb("mv2", [P, 2])
        sd = sb("sd2", [P, 4])
        p_x = ps("p_x2", [P, KT, P])
        p_e = [ps(f"p_e{b}", [P, D]) for b in range(2)]

        bias_in = sem("p_bias_in")
        w_in = [sem(f"wp_in{k}") for k in range(2)]
        w_high = sem("wp_high")
        w_split = sem("wp_split")
        h_loaded = [sem(f"h_loaded{b}") for b in range(2)]
        h_biased = sem("h_biased")
        o_copied = sem("o_copied")
        at_done = sem("at2_done")
        at_high = sem("at2_high")
        at_split = sem("at2_split")
        e_done = sem("e_done")
        h2_ready = sem("h2_ready")
        var_ready = sem("var2_ready")
        root_ready = sem("root2_ready")
        norm_ready = sem("norm_ready")
        ln_step = sem("ln2_step")
        block = ctx.enter_context(nc.Block())

        @block.sync
        def _(sp):
            sp.dma_start(bias[:], a["b_proj"].to_broadcast([P, D])).then_inc(bias_in, 16)
            for k in range(KT):
                after(sp, w_split, k - 1)
                sp.dma_start(w_raw[k % 2][:], a["w_proj"][k * P:(k + 1) * P, :]).then_inc(w_in[k % 2], 16)

            def tile(i):
                for b in range(2):
                    t = 2 * i + b
                    after(sp, h2_ready, t - 1)
                    sp.dma_start(h_in[b][:], a["h_dram"][bass.ds(t, 1)].rearrange("a p d -> (a p) d")).then_inc(h_loaded[b], 16)
            repeat(sp, NT // 2, tile)

        @block.gpsimd
        def _(pool):
            def copy(t, b):
                after(pool, at_done, t - 1)
                pool.tensor_copy(o_now[b][:], o[:, bass.ds(t, 1), :].rearrange("p a d -> p (a d)")).then_inc(o_copied, 1)
            copy(0, 0)
            pool.wait_ge(bias_in, 16)

            def tile(i):
                for b in range(2):
                    t = 2 * i + b
                    if not (isinstance(i, int) and t == NT - 1):
                        copy(t + 1, 1 - b)
                    pool.wait_ge(h_loaded[b], 16 * i + 16)
                    pool.tensor_tensor(h_in[b][:], h_in[b][:], bias[:], ALU.add).then_inc(h_biased, 1)
            repeat(pool, NT // 2, tile)

        @block.scalar
        def _(act):
            def high(t, b):
                act.wait_ge(at_done, t + 1)
                after(act, e_done, t - 1)
                act.activation(a_h[b][:], p_x[:], ACT.Copy).then_inc(at_high, 1)
            for k in range(KT):
                act.wait_ge(w_in[k % 2], 16 * (k // 2 + 1))
                act.activation(w_h[:, k, :], w_raw[k % 2][:], ACT.Copy).then_inc(w_high, 1)
            high(0, 0)

            def tile(i):
                for b in range(2):
                    t = 2 * i + b
                    if not (isinstance(i, int) and t == NT - 1):
                        high(t + 1, 1 - b)
                    act.wait_ge(var_ready, t + 1)
                    act.activation(sd[:, 1:2], sd[:, 0:1], ACT.Sqrt).then_inc(root_ready, 1)
            repeat(act, NT // 2, tile)

        @block.vector
        def _(dve):
            passed = nc.alloc_semaphore("passed6")
            ln = Chain(dve, ln_step, passed)

            def low(t, b):
                dve.wait_ge(at_high, t + 1)
                dve.tensor_tensor(a_l[b][:], p_x[:], wide(a_h[b][:]), ALU.subtract).then_inc(at_split, 1)
            for k in range(KT):
                dve.wait_ge(w_high, k + 1)
                dve.tensor_tensor(w_l[:, k, :], w_raw[k % 2][:], wide(w_h[:, k, :]), ALU.subtract).then_inc(w_split, 1)
            low(0, 0)

            def tile(i):
                ln.begin(i)
                for b in range(2):
                    t = 2 * i + b
                    if not (isinstance(i, int) and t == NT - 1):
                        low(t + 1, 1 - b)
                    dve.wait_ge(h_biased, t + 1)
                    dve.wait_ge(e_done, t + 1)
                    dve.wait_ge(o_copied, t + 1)
                    dve.tensor_tensor(o[:, bass.ds(t, 1), :].rearrange("p a d -> p (a d)"), p_e[b][:], h_in[b][:], ALU.add
                                      ).then_inc(h2_ready, 1)
                    after_plainly(dve, passed, h2_ready, t + 1)
                    for k in range(2):
                        ins = dve.bn_stats(stats[:, k, :], o[:, bass.ds(t, 1), k * HALF:(k + 1) * HALF].rearrange("p a d -> p (a d)"))
                    ln.link(ins, plainly=True)
                    ln.link(dve.bn_aggr(mv[:], stats[:]))
                    dve.tensor_copy(norm[:, bass.ds(t, 1), 0:1].rearrange("p a k -> p (a k)"), mv[:, 0:1])
                    dve.tensor_scalar(sd[:, 0:1], mv[:, 1:2], EPS, None, ALU.add).then_inc(var_ready, 1)
                    root_of_variance(dve, ln, root_ready, t + 1, sd, norm[:, bass.ds(t, 1), 1:2].rearrange("p a k -> p (a k)")
                                     ).then_inc(norm_ready, 1)
            repeat(dve, NT // 2, tile)

        @block.tensor
        def _(pe):
            def turn(t, b):
                pe.wait_ge(o_copied, t + 1)
                after(pe, at_split, t)
                for k in range(KT):
                    last = pe.transpose(p_x[:, k, :], o_now[b][:, k * P:(k + 1) * P], ident[:])
                last.then_inc(at_done, 1)
            turn(0, 0)
            pe.wait_ge(w_split, KT)

            def tile(i):
                for b in range(2):
                    t = 2 * i + b
                    pe.wait_ge(at_split, t + 1)
                    after(pe, h2_ready, t - 1)
                    for c in range(2):
                        n = slice(c * HALF, (c + 1) * HALF)
                        for k in range(KT):
                            last = product3(pe, p_e[b][:, n], a_h[b][:, k, :], a_l[b][:, k, :], w_h[:, k, n], w_l[:, k, n],
                                            k == 0, k == KT - 1)
                        if c == 0 and not (isinstance(i, int) and t == NT - 1):
                            turn(t + 1, 1 - b)
                    last.then_inc(e_done, 1)
            repeat(pe, NT // 2, tile)


def phase_ffn(nc, a, o, norm, ident):
    with ExitStack() as ctx:
        sb = lambda n, s, d=F32: ctx.enter_context(nc.sbuf_tensor(n, s, d))
        ps = lambda n, s: ctx.enter_context(nc.psum_tensor(n, s, F32))
        sem = lambda n: ctx.enter_context(nc.semaphore(n))
        RAW = KT * ZW
        w_raw = [sb(f"wf_raw{k}", [P, RAW]) for k in range(2)]
        w_h = sb("wf_h", [P, KT, D], F32R)
        w_l = sb("wf_l", [P, KT, D], F32R)
        z_h = sb("wz_h", [P, KT, ZW], F32R)
        z_l = sb("wz_l", [P, KT, ZW], F32R)
        l_h = sb("wl_h", [P, D], F32R)
        l_l = sb("wl_l", [P, D], F32R)
        weights = ([(a["w_z"], RAW, z_h[:].rearrange("p k n -> p (k n)"), z_l[:].rearrange("p k n -> p (k n)"))]
                   + [(a["w_base"][k * P:(k + 1) * P, :], D, w_h[:, k, :], w_l[:, k, :]) for k in range(KT)]
                   + [(a["w_lora"], D, l_h[:], l_l[:])])
        bias = sb("f_bias", [P, D])
        r_bias = sb("r_bias", [P, NR])
        emap = sb("emap", [P, NR], I32)
        emap_f = sb("emap_f", [P, NR])
        onehot = sb("onehot", [P, E, NR])
        norm_now = [sb(f"norm_now{b}", [P, 2]) for b in range(2)]
        xn = sb("xn2", [P, D])
        x_h = [sb(f"x2_h{b}", [P, KT, P], F32R) for b in range(2)]
        x_l = [sb(f"x2_l{b}", [P, KT, P], F32R) for b in range(2)]
        rest = [sb(f"rest{b}", [P, D]) for b in range(2)]
        out = [sb(f"out{b}", [P, D]) for b in range(2)]
        logit = sb("logit", [P, NR])
        peak = sb("peak", [P, 2])
        ex = sb("ex", [P, NR])
        ex_sum = sb("ex_sum", [P, 2])
        prob = sb("prob", [P, NR])
        top8 = sb("top8", [P, 8])
        unchosen = sb("unchosen", [P, NR])
        spread = sb("spread", [P, E, NR])
        gate = sb("gate", [P, E])
        hw = sb("hw", [P, ER])
        hwt_h = sb("hwt_h", [P, P], F32R)
        hwt_l = sb("hwt_l", [P, P], F32R)
        p_x = ps("p_x3", [P, KT, P])
        p_e = [ps(f"p_f{b}", [P, D]) for b in range(2)]
        p_z = ps("p_z", [P, HALF])
        p_hw = ps("p_hw", [P, HALF])

        small_in = sem("small_in")
        bias_in = sem("f_bias_in")
        w_in = [sem(f"wf_in{k}") for k in range(2)]
        w_high = sem("wf_high")
        w_split = sem("wf_split")
        map_step = sem("map_step")
        norm_got = sem("norm_got")
        rest_ready = sem("rest_ready")
        xn_ready = sem("xn3_ready")
        xt_done = sem("xt3_done")
        xt_high = sem("xt3_high")
        xt_split = sem("xt3_split")
        z_done = sem("z_done")
        route = sem("route")
        logit_ready = sem("logit_ready")
        exp_ready = sem("exp_ready")
        hw_ready = sem("hw_ready")
        hwt_done = sem("hwt_done")
        hwt_high = sem("hwt_high")
        hwt_split = sem("hwt_split")
        e_done = sem("f_done")
        out_ready = sem("out_ready")
        stored = [sem(f"stored{b}") for b in range(2)]
        block = ctx.enter_context(nc.Block())

        def last_tile(i, t):
            return isinstance(i, int) and t == NT - 1

        @block.sync
        def _(sp):
            sp.dma_start(r_bias[:], a["b_router"].to_broadcast([P, NR])).then_inc(small_in, 16)
            sp.dma_start(emap[:], a["expert_map"].to_broadcast([P, NR])).then_inc(small_in, 16)
            sp.dma_start(bias[:], a["b_base"].to_broadcast([P, D])).then_inc(bias_in, 16)
            for n, (src, w, _, _) in enumerate(weights):
                after(sp, w_split, n - 1)
                sp.dma_start(w_raw[n % 2][:, 0:w], src).then_inc(w_in[n % 2], 16)

            def tile(i):
                for b in range(2):
                    t = 2 * i + b
                    sp.wait_ge(out_ready, t + 1)
                    sp.dma_start(a["out"][bass.ds(t, 1)].rearrange("a p d -> (a p) d"), out[b][:]).then_inc(stored[b], 16)
            repeat(sp, NT // 2, tile)
            for b in range(2):
                sp.wait_ge(stored[b], 16 * NT // 2)

        @block.gpsimd
        def _(pool):
            pool.wait_ge(bias_in, 16)

            def tile(i):
                for b in range(2):
                    t = 2 * i + b
                    after(pool, xn_ready, t - 1)
                    pool.tensor_copy(norm_now[b][:], norm[:, bass.ds(t, 1), :].rearrange("p a k -> p (a k)")).then_inc(norm_got, 1)
                    after(pool, out_ready, t - 1)
                    pool.tensor_tensor(rest[b][:], o[:, bass.ds(t, 1), :].rearrange("p a d -> p (a d)"), bias[:], ALU.add
                                       ).then_inc(rest_ready, 1)
            repeat(pool, NT // 2, tile)

        @block.scalar
        def _(act):
            def high(t, b):
                act.wait_ge(xt_done, t + 1)
                after(act, e_done, t - 1)
                act.activation(x_h[b][:], p_x[:], ACT.Copy).then_inc(xt_high, 1)
            for n, (_, w, wh, _) in enumerate(weights):
                act.wait_ge(w_in[n % 2], 16 * (n // 2 + 1))
                act.activation(wh, w_raw[n % 2][:, 0:w], ACT.Copy).then_inc(w_high, 1)
            high(0, 0)

            def tile(i):
                for b in range(2):
                    t = 2 * i + b
                    act.wait_ge(logit_ready, t + 1)
                    act.activation(ex[:], logit[:], ACT.Exp, bias=peak[:, 1:2], accum_out=ex_sum[:, 0:1]).then_inc(exp_ready, 1)
                    if not last_tile(i, t):
                        high(t + 1, 1 - b)
                    act.wait_ge(hwt_done, t + 1)
                    after(act, e_done, t)
                    act.activation(hwt_h[:], p_hw[:, 0:P], ACT.Copy).then_inc(hwt_high, 1)
            repeat(act, NT // 2, tile)

        @block.vector
        def _(dve):
            passed = nc.alloc_semaphore("passed7")
            step = Chain(dve, map_step)
            dve.wait_ge(small_in, 32)
            step.link(dve.tensor_copy(emap_f[:], emap[:]))
            for e in range(E):
                ins = dve.tensor_scalar(onehot[:, e, :], emap_f[:], float(e), FFN_SCALE, ALU.is_equal, ALU.mult)
            step.link(ins)

            def normalise(t, b):
                dve.wait_ge(norm_got, t + 1)
                after(dve, xt_done, t)
                dve.tensor_scalar(xn[:], o[:, bass.ds(t, 1), :].rearrange("p a d -> p (a d)"), norm_now[b][:, 0:1],
                                  norm_now[b][:, 1:2], ALU.subtract, ALU.mult).then_inc(xn_ready, 1)

            def low(t, b):
                dve.wait_ge(xt_high, t + 1)
                dve.tensor_tensor(x_l[b][:], p_x[:], wide(x_h[b][:]), ALU.subtract).then_inc(xt_split, 1)
            normalise(0, 0)
            for n, (_, w, wh, wl) in enumerate(weights):
                dve.wait_ge(w_high, n + 1)
                dve.tensor_tensor(wl, w_raw[n % 2][:, 0:w], wide(wh), ALU.subtract).then_inc(w_split, 1)
            low(0, 0)
            r = Chain(dve, route, passed)

            def tile(i):
                r.begin(i)
                for b in range(2):
                    t = 2 * i + b
                    if not last_tile(i, t):
                        normalise(t + 1, 1 - b)
                    dve.wait_ge(z_done, t + 1)
                    r.link(dve.tensor_tensor(logit[:], p_z[:, ER:ER + NR], r_bias[:], ALU.add))
                    r.link(dve.tensor_reduce(peak[:, 0:1], logit[:], AX_X, ALU.max))
                    dve.tensor_scalar(peak[:, 1:2], peak[:, 0:1], -1.0, None, ALU.mult).then_inc(logit_ready, 1)
                    dve.wait_ge(exp_ready, t + 1)
                    r.link(dve.reciprocal(ex_sum[:, 1:2], ex_sum[:, 0:1]))
                    r.link(dve.tensor_scalar(prob[:], ex[:], ex_sum[:, 1:2], None, ALU.mult), plainly=True)
                    r.link(dve.max(top8[:], prob[:]), plainly=True)
                    r.link(dve.match_replace(unchosen[:], top8[:], prob[:], 0.0))
                    r.link(dve.tensor_tensor(prob[:], prob[:], unchosen[:], ALU.subtract))
                    r.link(dve.tensor_tensor(spread[:], onehot[:], prob[:].unsqueeze(1).to_broadcast([P, E, NR]), ALU.mult))
                    r.link(dve.tensor_reduce(gate[:], spread[:], AX_X, ALU.add))
                    after(dve, hwt_done, t)
                    dve.tensor_tensor(hw[:].rearrange("p (e r) -> p e r", e=E), p_z[:, 0:ER].rearrange("p (e r) -> p e r", e=E),
                                      gate[:].unsqueeze(2).to_broadcast([P, E, ER // E]), ALU.mult).then_inc(hw_ready, 1)
                    if not last_tile(i, t):
                        low(t + 1, 1 - b)
                    dve.wait_ge(hwt_high, t + 1)
                    dve.tensor_tensor(hwt_l[:], p_hw[:, 0:P], wide(hwt_h[:]), ALU.subtract).then_inc(hwt_split, 1)
                    dve.wait_ge(e_done, t + 1)
                    dve.wait_ge(rest_ready, t + 1)
                    after(dve, stored[b], 16 * i)
                    dve.tensor_tensor(out[b][:], p_e[b][:], rest[b][:], ALU.add).then_inc(out_ready, 1)
            repeat(dve, NT // 2, tile)

        @block.tensor
        def _(pe):
            def turn(t):
                pe.wait_ge(xn_ready, t + 1)
                after(pe, xt_split, t)
                for k in range(KT):
                    last = pe.transpose(p_x[:, k, :], xn[:, k * P:(k + 1) * P], ident[:])
                last.then_inc(xt_done, 1)
            turn(0)
            pe.wait_ge(w_split, len(weights))

            def base(b, c):
                n = slice(c * HALF, (c + 1) * HALF)
                for k in range(KT):
                    product3(pe, p_e[b][:, n], x_h[b][:, k, :], x_l[b][:, k, :], w_h[:, k, n], w_l[:, k, n], k == 0, False)

            def tile(i):
                for b in range(2):
                    t = 2 * i + b
                    pe.wait_ge(xt_split, t + 1)
                    after(pe, hw_ready, t)
                    for k in range(KT):
                        last = product3(pe, p_z[:, 0:ZW], x_h[b][:, k, :], x_l[b][:, k, :], z_h[:, k, :], z_l[:, k, :],
                                        k == 0, k == KT - 1)
                    last.then_inc(z_done, 1)
                    after(pe, out_ready, t - 1)
                    base(b, 0)
                    if not last_tile(i, t):
                        turn(t + 1)
                    pe.wait_ge(hw_ready, t + 1)
                    after(pe, hwt_split, t)
                    pe.transpose(p_hw[:, 0:P], hw[:], ident[:]).then_inc(hwt_done, 1)
                    base(b, 1)
                    pe.wait_ge(hwt_split, t + 1)
                    for c in range(2):
                        n = slice(c * HALF, (c + 1) * HALF)
                        last = product3(pe, p_e[b][:, n], hwt_h[:], hwt_l[:], l_h[:, n], l_l[:, n], False, True)
                    last.then_inc(e_done, 1)
            repeat(pe, NT // 2, tile)


def build(nc, a):
    with ExitStack() as ctx:
        ident = ctx.enter_context(nc.sbuf_tensor("ident", [P, P], F32))
        norm = ctx.enter_context(nc.sbuf_tensor("norm", [P, NT, 2], F32))
        ident_made = ctx.enter_context(nc.semaphore("ident_made"))
        with ExitStack() as front:
            xh = front.enter_context(nc.sbuf_tensor("xh", [P, KT, T], F32R))
            xl = front.enter_context(nc.sbuf_tensor("xl", [P, KT, T], F32R))
            phase_embed(nc, a, xh, xl, ident, ident_made)
            phase_qkv(nc, a, xh, xl, ident)
        o = ctx.enter_context(nc.sbuf_tensor("o", [P, NT, D], F32))
        phase_attention(nc, a, o, ident)
        phase_project(nc, a, o, norm, ident)
        phase_ffn(nc, a, o, norm, ident)


def kernel(x, mask_BS_i1_0, mask_BS_i0_1, L0_tok_weight, L0_tok_lora_A_cl, L0_tok_lora_B_cl, L0_tok_lora_A_lm,
           L0_tok_lora_B_lm, L0_tok_lora_A_cl_prime, L0_tok_lora_B_cl_prime, L0_attn_w_attn, L0_attn_b_attn,
           L0_attn_w_proj, L0_attn_b_proj, L0_ffn_base_W, L0_ffn_base_b, L0_ffn_router_W, L0_ffn_router_b,
           L0_ffn_A, L0_ffn_B, L0_ffn_expert_map):
    import concourse.bacc as bacc
    from concourse.bass_utils import run_bass_kernel_spmd

    arr = lambda v: np.asarray(v)
    slopes = (2.0 ** (-2.0 ** -(np.log2(H) - 3))) ** np.arange(1, H + 1, dtype=np.float32)
    w_attn = arr(L0_attn_w_attn).reshape(KT, P, 3, KT, P)
    z = np.concatenate([arr(L0_ffn_A).reshape(ER, D), arr(L0_ffn_router_W), np.zeros((1, D), np.float32)])
    ins = {
        "ids": np.stack([arr(m).reshape(NT, P) for m in (x, mask_BS_i1_0, mask_BS_i0_1)]).transpose(2, 0, 1).reshape(P, 3 * NT),
        "tok_w": arr(L0_tok_weight),
        "tok_a1": arr(L0_tok_lora_A_cl),
        "tok_a2": np.concatenate([arr(L0_tok_lora_A_lm), arr(L0_tok_lora_A_cl_prime)], 1),
        "lora_b": np.stack([arr(m) for m in (L0_tok_lora_B_cl, L0_tok_lora_B_lm, L0_tok_lora_B_cl_prime)], 1),
        "w_qkv": w_attn.transpose(3, 2, 1, 0, 4).reshape(3 * KT, P, KT * P),
        "b_qkv": arr(L0_attn_b_attn).reshape(3, KT, P).transpose(2, 0, 1),
        "slopes": np.broadcast_to(slopes.astype(np.float32), (P, H)),
        "w_proj": arr(L0_attn_w_proj),
        "b_proj": arr(L0_attn_b_proj).reshape(1, D),
        "w_base": arr(L0_ffn_base_W).T,
        "b_base": arr(L0_ffn_base_b).reshape(1, D),
        "w_z": z.T.reshape(KT, P, ZW).transpose(1, 0, 2).reshape(P, KT * ZW),
        "b_router": arr(L0_ffn_router_b).reshape(1, NR),
        "w_lora": arr(L0_ffn_B).transpose(0, 2, 1).reshape(ER, D),
        "expert_map": arr(L0_ffn_expert_map).reshape(1, NR),
    }
    nc = bacc.Bacc("TRN2", target_bir_lowering=False, num_devices=1)
    arrays, a = {}, {}
    for name, v in ins.items():
        v = np.ascontiguousarray(v)
        arrays["in_" + name] = v
        a[name] = nc.dram_tensor("in_" + name, v.shape, mybir.dt.from_np(v.dtype), kind="ExternalInput").ap()
    for name in ("qh", "ql", "kh", "kl"):
        a[name] = nc.dram_tensor(name + "_scratch", (D, T), F32, kind="Internal").ap()
    a["v_dram"] = nc.dram_tensor("v_scratch", (H // 2, P, NT, 2 * HD), F32, kind="Internal").ap()
    a["h_dram"] = nc.dram_tensor("h_scratch", (NT, P, D), F32, kind="Internal").ap()
    a["out"] = nc.dram_tensor("out_dram", (NT, P, D), F32, kind="ExternalOutput").ap()
    build(nc, a)
    r = run_bass_kernel_spmd(nc, [arrays], core_ids=[0])
    return r.results[0]["out_dram"].reshape(1, T, D)
```

```python
from contextlib import ExitStack

import numpy as np
import concourse.bass as bass
from concourse import mybir

F32 = mybir.dt.float32
F32R = mybir.dt.float32r
I32 = mybir.dt.int32
ALU = mybir.AluOpType
ACT = mybir.ActivationFunctionType
AX_X = mybir.AxisListType.X

P = 128
T = 2048
NT = T // P
D = 1024
KT = D // P
HALF = 512
V = 8000
R = 128
LORA = 3
TOK_SCALE = 2.0
EPS = 1e-5

H = 32
HD = D // H
QG = 4
NG = NT // QG
ATT_SCALE = 1.0 / HD
CHUNK = 1024
MASKED = -1.0e36

E = 8
ER = 128
NR = 2 * E - 1
ZW = ER + NR + 1
FFN_SCALE = 2.0


def repeat(eng, n, body, peel=1):
    for i in range(peel):
        body(i)
    with eng.Fori(peel, n - 1) as i:
        body(i)
    body(n - 1)


def after(eng, sem, value):
    if isinstance(value, int) and value <= 0:
        return
    eng.wait_ge(sem, value)


def after_plainly(eng, passed, sem, value):
    after(eng, sem, value)
    if not isinstance(value, int):
        eng.sem_inc(passed, 1)


class Chain:

    def __init__(self, eng, sem, passed=None):
        self.eng, self.sem, self.passed, self.base, self.n, self.per = eng, sem, passed, 0, 0, None

    def begin(self, i):
        if self.per is None and not (isinstance(i, int) and i == 0):
            self.per = self.n - self.start
        if isinstance(i, int) and i == 0:
            self.start = self.n
            self.base = 0
        else:
            self.base = i * self.per + self.start
            self.n = 0

    def link(self, ins, plainly=False):
        self.n += 1
        ins.then_inc(self.sem, 1)
        if plainly:
            after_plainly(self.eng, self.passed, self.sem, self.base + self.n)
        else:
            self.eng.wait_ge(self.sem, self.base + self.n)


def product3(pe, out, ah, al, bh, bl, start, stop):
    pe.matmul(out, ah, bh, start=start, stop=False)
    pe.matmul(out, ah, bl, start=False, stop=False)
    return pe.matmul(out, al, bh, start=False, stop=stop)


def wide(t):
    return t.bitcast(F32)


def phase_embed(nc, a, xh, xl, ident, ident_made):
    with ExitStack() as ctx:
        sb = lambda n, s, d=F32: ctx.enter_context(nc.sbuf_tensor(n, s, d))
        ps = lambda n, s: ctx.enter_context(nc.psum_tensor(n, s, F32))
        sem = lambda n: ctx.enter_context(nc.semaphore(n))
        ids = sb("ids", [P, 3 * NT], I32)
        ids_f = sb("ids_f", [P, 3, NT])
        wrap = sb("wrap", [P, 3, NT])
        rows = sb("rows", [P, NT, 3], I32)
        row_now = [sb(f"row_now{b}", [P, 3], I32) for b in range(2)]
        lb_raw = sb("lb_raw", [P, LORA, D])
        lb_h = sb("lb_h", [P, LORA, D], F32R)
        lb_l = sb("lb_l", [P, LORA, D], F32R)
        w_row = [sb(f"w_row{b}", [P, D]) for b in range(2)]
        xn = [sb(f"xn{b}", [P, D]) for b in range(2)]
        a_row = [sb(f"a_row{b}", [P, LORA * R]) for b in range(2)]
        at_h = [sb(f"at_h{b}", [P, LORA, P], F32R) for b in range(2)]
        at_l = [sb(f"at_l{b}", [P, LORA, P], F32R) for b in range(2)]
        stats = sb("stats", [P, 2, 6])
        mv = sb("mv", [P, 2])
        sd = sb("sd", [P, 4])
        p_at = [ps(f"p_at{b}", [P, 4, P])[:, 0:LORA, :] for b in range(2)]
        p_lora = ps("p_lora", [P, D])
        p_xt = [ps(f"p_xt{b}", [P, KT, P]) for b in range(2)]

        ids_in = sem("ids_in")
        lb_in = sem("lb_in")
        lb_high = sem("lb_high")
        lb_split = sem("lb_split")
        rows_ready = sem("rows_ready")
        row_copied = sem("row_copied")
        gathered = [sem(f"gathered{b}") for b in range(2)]
        at_done = sem("at_done")
        at_high = sem("at_high")
        at_split = sem("at_split")
        lora_done = sem("lora_done")
        h_ready = sem("h_ready")
        h_stored = [sem(f"h_stored{b}") for b in range(2)]
        var_ready = sem("var_ready")
        root_ready = sem("root_ready")
        xn_ready = sem("xn_ready")
        xt_done = sem("xt_done")
        xt_high = sem("xt_high")
        xt_split = sem("xt_split")
        idx_step = sem("idx_step")
        ln_step = sem("ln_step")
        block = ctx.enter_context(nc.Block())

        @block.sync
        def _(sp):
            sp.dma_start(ids[:], a["ids"]).then_inc(ids_in, 16)
            sp.dma_start(lb_raw[:], a["lora_b"]).then_inc(lb_in, 16)

            def tile(i):
                for b in range(2):
                    t = 2 * i + b
                    after(sp, h_ready, t + 1)
                    sp.dma_start(a["h_dram"][bass.ds(t, 1)].rearrange("a p d -> (a p) d"), w_row[b][:]).then_inc(h_stored[b], 16)
            repeat(sp, NT // 2, tile)
            for b in range(2):
                sp.wait_ge(h_stored[b], 16 * NT // 2)

        @block.gpsimd
        def _(pool):
            passed = nc.alloc_semaphore("passed1")
            pool.memset(ident[:], 0.0).then_inc(ident_made, 1)
            pool.wait_ge(ident_made, 1)
            pool.affine_select(out=ident[:], in_=ident[:], compare_op=ALU.not_equal, fill=1.0,
                               base=0, pattern=[[-1, P]], channel_multiplier=1).then_inc(ident_made, 1)
            pool.wait_ge(rows_ready, 1)

            def tile(i):
                for b in range(2):
                    t = 2 * i + b
                    after_plainly(pool, passed, gathered[b], 48 * i)
                    pool.tensor_copy(row_now[b][:], rows[:, bass.ds(t, 1), :].rearrange("p a k -> p (a k)")).then_inc(row_copied, 1)
                    after(pool, at_done, t - 1)
                    after(pool, xn_ready, t - 1)
                    after(pool, h_stored[b], 16 * i)
                    after_plainly(pool, passed, row_copied, t + 1)
                    for k, (table, dst) in enumerate(((a["tok_w"], w_row[b][:]), (a["tok_a1"], a_row[b][:, 0:R]),
                                                      (a["tok_a2"], a_row[b][:, R:LORA * R]))):
                        pool.indirect_dma_start(dst, None, table, bass.IndirectOffsetOnAxis(ap=row_now[b][:, k:k + 1], axis=0)
                                                ).then_inc(gathered[b], 16)
            repeat(pool, NT // 2, tile)

        @block.vector
        def _(dve):
            passed = nc.alloc_semaphore("passed2")
            idx = Chain(dve, idx_step)
            dve.wait_ge(ids_in, 16)
            idx.link(dve.tensor_copy(ids_f[:].rearrange("p a t -> p (a t)"), ids[:]))
            for k in (1, 2):
                idx.link(dve.tensor_tensor(ids_f[:, k, :], ids_f[:, 0, :], ids_f[:, k, :], ALU.mult))
            idx.link(dve.tensor_scalar(wrap[:], ids_f[:], 0.0, float(V), ALU.is_lt, ALU.mult))
            idx.link(dve.tensor_tensor(ids_f[:], ids_f[:], wrap[:], ALU.add))
            idx.link(dve.tensor_scalar(ids_f[:], ids_f[:], 0.0, float(V - 1), ALU.max, ALU.min))
            dve.tensor_copy(rows[:].rearrange("p t k -> p k t"), ids_f[:]).then_inc(rows_ready, 1)
            dve.wait_ge(lb_high, 1)
            dve.tensor_tensor(lb_l[:], lb_raw[:], wide(lb_h[:]), ALU.subtract).then_inc(lb_split, 1)
            ln = Chain(dve, ln_step, passed)

            def split_xt(t, b, col):
                after(dve, xt_high, t + 1)
                dve.tensor_tensor(xl[:, :, bass.ds(col, P)], p_xt[b][:], wide(xh[:, :, bass.ds(col, P)]),
                                  ALU.subtract).then_inc(xt_split, 1)

            def tile(i):
                ln.begin(i)
                for b in range(2):
                    t = 2 * i + b
                    after(dve, at_high, t + 1)
                    dve.tensor_tensor(at_l[b][:], p_at[b], wide(at_h[b][:]), ALU.subtract).then_inc(at_split, 1)
                    dve.wait_ge(gathered[b], 48 * i + 48)
                    dve.wait_ge(lora_done, t + 1)
                    ln.link(dve.scalar_tensor_tensor(out=w_row[b][:], in0=p_lora[:], scalar=TOK_SCALE, in1=w_row[b][:],
                                                     op0=ALU.mult, op1=ALU.add))
                    for k in range(2):
                        ins = dve.bn_stats(stats[:, k, :], w_row[b][:, k * HALF:(k + 1) * HALF])
                        if k == 0:
                            ins.then_inc(h_ready, 1)
                    ln.link(ins, plainly=True)
                    ln.link(dve.bn_aggr(mv[:], stats[:]))
                    dve.tensor_scalar(sd[:, 0:1], mv[:, 1:2], EPS, None, ALU.add).then_inc(var_ready, 1)
                    dve.wait_ge(root_ready, t + 1)
                    ln.link(dve.reciprocal(sd[:, 2:3], sd[:, 1:2]))
                    ln.link(dve.scalar_tensor_tensor(out=sd[:, 3:4], in0=sd[:, 2:3], scalar=sd[:, 0:1], in1=sd[:, 1:2],
                                                     op0=ALU.mult, op1=ALU.add))
                    ln.link(dve.tensor_scalar(sd[:, 2:3], sd[:, 3:4], 0.5, None, ALU.mult))
                    ln.link(dve.reciprocal(sd[:, 3:4], sd[:, 2:3]))
                    after(dve, xt_done, t - 1)
                    dve.tensor_scalar(xn[b][:], w_row[b][:], mv[:, 0:1], sd[:, 3:4], ALU.subtract, ALU.mult
                                      ).then_inc(xn_ready, 1)
                    if b == 1:
                        split_xt(t - 1, 0, (t - 1) * P)
                    elif not (isinstance(i, int) and i == 0):
                        split_xt(t - 1, 1, (t - 1) * P)
            repeat(dve, NT // 2, tile, 2)
            split_xt(NT - 1, 1, (NT - 1) * P)

        @block.scalar
        def _(act):
            act.wait_ge(lb_in, 16)
            act.activation(lb_h[:], lb_raw[:], ACT.Copy).then_inc(lb_high, 1)

            def high_xt(t, b, col):
                after(act, xt_done, t + 1)
                act.activation(xh[:, :, bass.ds(col, P)], p_xt[b][:], ACT.Copy).then_inc(xt_high, 1)

            def tile(i):
                for b in range(2):
                    t = 2 * i + b
                    act.wait_ge(at_done, t + 1)
                    after(act, lora_done, t - 1)
                    act.activation(at_h[b][:], p_at[b], ACT.Copy).then_inc(at_high, 1)
                    act.wait_ge(var_ready, t + 1)
                    act.activation(sd[:, 1:2], sd[:, 0:1], ACT.Sqrt).then_inc(root_ready, 1)
                    if b == 1:
                        high_xt(t - 1, 0, (t - 1) * P)
                    elif not (isinstance(i, int) and i == 0):
                        high_xt(t - 1, 1, (t - 1) * P)
            repeat(act, NT // 2, tile, 2)
            high_xt(NT - 1, 1, (NT - 1) * P)

        @block.tensor
        def _(pe):
            pe.wait_ge(ident_made, 2)
            pe.wait_ge(lb_split, 1)
            pe.wait_ge(lb_high, 1)

            def turn_x(t, b):
                pe.wait_ge(xn_ready, t + 1)
                after(pe, xt_split, t - 1)
                for k in range(KT):
                    last = pe.transpose(p_xt[b][:, k, :], xn[b][:, k * P:(k + 1) * P], ident[:])
                last.then_inc(xt_done, 1)

            def tile(i):
                for b in range(2):
                    t = 2 * i + b
                    pe.wait_ge(gathered[b], 48 * i + 48)
                    after(pe, at_split, t - 1)
                    for k in range(LORA):
                        last = pe.transpose(p_at[b][:, k, :], a_row[b][:, k * R:(k + 1) * R], ident[:])
                    last.then_inc(at_done, 1)
                    pe.wait_ge(at_split, t + 1)
                    after(pe, h_ready, t)
                    for c in range(2):
                        n = slice(c * HALF, (c + 1) * HALF)
                        for k in range(LORA):
                            last = product3(pe, p_lora[:, n], at_h[b][:, k, :], at_l[b][:, k, :],
                                            lb_h[:, k, n], lb_l[:, k, n], k == 0, k == LORA - 1)
                    last.then_inc(lora_done, 1)
                    if b == 1:
                        turn_x(t - 1, 0)
                    elif not (isinstance(i, int) and i == 0):
                        turn_x(t - 1, 1)
            repeat(pe, NT // 2, tile, 2)
            turn_x(NT - 1, 1)


def phase_qkv(nc, a, xh, xl, ident):
    with ExitStack() as ctx:
        sb = lambda n, s, d=F32: ctx.enter_context(nc.sbuf_tensor(n, s, d))
        ps = lambda n, s: ctx.enter_context(nc.psum_tensor(n, s, F32))
        sem = lambda n: ctx.enter_context(nc.semaphore(n))
        NB = T // HALF
        TB = HALF // P
        w_raw = [sb(f"wq_raw{b}", [P, KT, P]) for b in range(3)]
        w_h = [sb(f"wq_h{b}", [P, KT, P], F32R) for b in range(3)]
        w_l = [sb(f"wq_l{b}", [P, KT, P], F32R) for b in range(3)]
        bias = sb("qkv_bias", [P, 3, KT])
        y = [sb(f"y{k}", [P, HALF]) for k in range(2)]
        y_h = [sb(f"y_h{k}", [P, HALF], F32R) for k in range(NB)]
        y_l = [sb(f"y_l{k}", [P, HALF], F32R) for k in range(NB)]
        v_out = [sb(f"v_out{k}", [P, P // HD, TB, HD]) for k in range(2)]
        p_y = [ps(f"p_y{k}", [P, HALF]) for k in range(NB)]
        p_vt = [ps(f"p_vt{k}", [P, TB, P]) for k in range(2)]

        bias_in = sem("bias_in")
        w_in = [sem(f"wq_in{b}") for b in range(3)]
        w_high = sem("wq_high")
        w_split = sem("wq_split")
        y_done = sem("y_done")
        y_biased = sem("y_biased")
        y_high = sem("y_high")
        y_split = sem("y_split")
        vt_done = sem("vt_done")
        v_ready = sem("v_ready")
        qk_stored = [sem(f"qk_stored{k}") for k in range(NB)]
        v_stored = [sem(f"v_stored{k}") for k in range(2)]
        block = ctx.enter_context(nc.Block())

        def staggered(eng, n, first, then):
            def body(i):
                for b in range(3):
                    first(i, b)
                    if b:
                        then(i, b - 1)
                    elif not (isinstance(i, int) and i == 0):
                        then(i - 1, 2)
            repeat(eng, n, body, 2)
            then(n - 1, 2)

        @block.sync
        def _(sp):
            sp.dma_start(bias[:], a["b_qkv"]).then_inc(bias_in, 16)

            def load(i, b):
                after(sp, w_split, 3 * (i - 1) + b + 1)
                sp.dma_start(w_raw[b][:].rearrange("p k c -> p (k c)"),
                             a["w_qkv"][bass.ds(3 * i + b, 1)].rearrange("a p n -> (a p) n")).then_inc(w_in[b], 16)

            def store(i, b):
                for k in range(NB):
                    if b < 2:
                        sp.wait_ge(y_split, 2 * NB * i + NB * b + k + 1)
                        to = (bass.ds(i * P, P), slice(k * HALF, (k + 1) * HALF))
                        sp.dma_start(a[("qh", "kh")[b]][to], wide(y_h[k][:])).then_inc(qk_stored[k], 16)
                        sp.dma_start(a[("ql", "kl")[b]][to], wide(y_l[k][:])).then_inc(qk_stored[k], 16)
                    else:
                        sp.wait_ge(v_ready, NB * i + k + 1)
                        sp.dma_start(a["v_dram"][bass.ds(P // HD * i, P // HD), :, TB * k:TB * k + TB, :].rearrange("a p t d -> p a (t d)"),
                                     v_out[k % 2][:].rearrange("p a t d -> p a (t d)")).then_inc(v_stored[k % 2], 16)
            staggered(sp, KT, load, store)
            for k in range(NB):
                sp.wait_ge(qk_stored[k], 4 * 16 * KT)
            for k in range(2):
                sp.wait_ge(v_stored[k], 2 * 16 * KT)

        @block.scalar
        def _(act):
            def weights(i, b):
                act.wait_ge(w_in[b], 16 * i + 16)
                after(act, y_done, NB * (3 * (i - 1) + b + 1))
                act.activation(w_h[b][:], w_raw[b][:], ACT.Copy).then_inc(w_high, 1)

            def results(i, b):
                for k in range(NB):
                    if b < 2:
                        act.wait_ge(y_biased, NB * (3 * i + b) + k + 1)
                        after(act, qk_stored[k], 32 * (2 * i + b))
                        act.activation(y_h[k][:], y[k % 2][:], ACT.Copy).then_inc(y_high, 1)
                    else:
                        act.wait_ge(vt_done, NB * i + k + 1)
                        after(act, v_stored[k % 2], 16 * (2 * i + k // 2))
                        act.activation(v_out[k % 2][:].rearrange("p a t d -> p t a d"), p_vt[k % 2][:].rearrange(
                            "p t (a d) -> p t a d", a=P // HD), ACT.Copy).then_inc(v_ready, 1)
            staggered(act, KT, weights, results)

        @block.vector
        def _(dve):
            dve.wait_ge(bias_in, 16)

            def weights(i, b):
                dve.wait_ge(w_high, 3 * i + b + 1)
                dve.tensor_tensor(w_l[b][:], w_raw[b][:], wide(w_h[b][:]), ALU.subtract).then_inc(w_split, 1)

            def results(i, b):
                for k in range(NB):
                    at = NB * (3 * i + b) + k
                    dve.wait_ge(y_done, at + 1)
                    if b == 2 and k >= 2:
                        dve.wait_ge(vt_done, NB * i + k - 1)
                    elif b == 0 and k < 2:
                        after(dve, vt_done, NB * (i - 1) + k + 3)
                    else:
                        dve.wait_ge(y_split, 2 * NB * i + NB * b + k - 1)
                    dve.tensor_scalar(y[k % 2][:], p_y[k][:], bias[:, b, bass.ds(i, 1)], ATT_SCALE if b == 0 else 1.0,
                                      ALU.add, ALU.mult).then_inc(y_biased, 1)
                    if b < 2:
                        dve.wait_ge(y_high, 2 * NB * i + NB * b + k + 1)
                        dve.tensor_tensor(y_l[k][:], y[k % 2][:], wide(y_h[k][:]), ALU.subtract).then_inc(y_split, 1)
            staggered(dve, KT, weights, results)

        @block.tensor
        def _(pe):
            def turn_v(i, k):
                pe.wait_ge(y_biased, NB * (3 * i + 2) + k + 1)
                after(pe, v_ready, NB * i + k - 1)
                for t in range(TB):
                    last = pe.transpose(p_vt[k % 2][:, t, :], y[k % 2][:, t * P:(t + 1) * P], ident[:])
                last.then_inc(vt_done, 1)

            def cols(i):
                for b in range(3):
                    g = 3 * i + b
                    pe.wait_ge(w_split, g + 1)
                    for k in range(NB):
                        after(pe, y_biased, NB * (g - 1) + k + 1)
                        n = slice(k * HALF, (k + 1) * HALF)
                        for c in range(KT):
                            last = product3(pe, p_y[k][:], w_h[b][:, c, :], w_l[b][:, c, :], xh[:, c, n], xl[:, c, n],
                                            c == 0, c == KT - 1)
                        last.then_inc(y_done, 1)
                        if b == 0 and not (isinstance(i, int) and i == 0):
                            turn_v(i - 1, k)
            repeat(pe, KT, cols, 2)
            for k in range(NB):
                turn_v(KT - 1, k)


class HeadPlan:

    LAG = 4
    RING = 5

    def __init__(self):
        self.groups = list(range(NG - 1, -1, -1))
        self.slots = [(u, g, k) for u, g in enumerate(self.groups) for k in range(QG * g + QG)]
        n = len(self.slots)
        self.ends = [max(i for i, x in enumerate(self.slots) if x[0] == u) for u in range(NG)]
        ahead = []
        for u, g in enumerate(self.groups):
            own = [("score", u, q, c) for q in range(QG - 1, -1, -1) for c in range(0, P * (QG * g + q + 1), CHUNK)]
            if u:
                own.insert(2, ("shift", u - 1))
            ahead += own
        ahead.append(("shift", NG - 1))
        cost = [min(CHUNK, self.width(x) - x[3]) // P if x[0] == "score" else 1 for x in ahead]
        self.ahead = ahead
        timed = [(sum(cost[:i]) * (n - 2) / sum(cost), x) for i, x in enumerate(ahead)]
        for u in range(NG):
            at = self.ends[u] + self.LAG + 2
            timed.append((at % n + 0.5, ("output", u, at // n)))
        self.items = [(int(t), x) for t, x in sorted(timed, key=lambda y: y[0])]
        self.high = ["A" if i % 2 else "D" for i in range(n)]
        self.low = ["D" if i % 8 == 3 else "P" for i in range(n)]

    def width(self, x):
        return P * (QG * self.groups[x[1]] + x[2] + 1)

    def present(self, h):
        first, last = isinstance(h, int) and h == 0, isinstance(h, int) and h == H - 1
        return [(t, x) for t, x in self.items
                if not (first and x[0] == "output" and x[2]) and not (last and x[0] != "output")]

    def period(self, h):
        if isinstance(h, int) and h == -1:
            return [(0, x, i) for i, x in enumerate(self.ahead)]
        late = sum(1 for _, x in self.items if x[0] == "output" and x[2])
        base = len(self.ahead) + (len(self.items) * h - late if not isinstance(h, int) or h else 0)
        return [(t, x, base + i) for i, (t, x) in enumerate(self.present(h))]

    def buffer(self, h, i):
        late = sum(1 for _, x in self.items if x[0] == "output" and x[2])
        if isinstance(h, int) and h <= 0:
            return (i + (len(self.ahead) if h == 0 else 0)) % 2
        return (len(self.ahead) - late + i) % 2


def back(h, s, by, n):
    return (h, s - by) if s >= by else (h - 1, s - by + n)


def phase_attention(nc, a, o, ident):
    plan = HeadPlan()
    N = len(plan.slots)
    NI = len(plan.items)
    assert NI % 2 == 0 and N % plan.RING == 0 and N % 2 == 0 and NG % 2 == 0 and len(plan.ahead) % 2 == 0
    BF16 = mybir.dt.bfloat16
    ROWS = 3 * HD
    VC = 2 * HD + 1
    OC = 80
    DIAG = (NT - 1) * P
    MID = HALF // 2
    DELTAS = NT
    with ExitStack() as ctx:
        sb = lambda n, s, d=F32: ctx.enter_context(nc.sbuf_tensor(n, s, d))
        ps = lambda n, s: ctx.enter_context(nc.psum_tensor(n, s, F32))
        sem = lambda n: ctx.enter_context(nc.semaphore(n))
        slopes = sb("slopes", [P, H])
        rel = sb("rel", [P, T])
        bias = sb("bias", [P, T])
        pos = sb("pos", [P, DELTAS + QG])
        spos = [sb(f"spos{b}", [P, DELTAS + QG]) for b in range(3)]
        ident_b = sb("ident_b", [P, P], BF16)
        mask_b = sb("mask_b", [P, P], BF16)
        qs = [sb(f"qs{b}", [P, T], F32R) for b in range(3)]
        ks = [sb(f"ks{b}", [P, T], F32R) for b in range(3)]
        v_raw = [sb(f"v_raw{b}", [P, NT, HD]) for b in range(3)]
        vs = [sb(f"vs{b}", [P, NT, VC], F32R) for b in range(3)]
        unread = [sb(f"unread{k}", [P, CHUNK]) for k in range(2)]
        top = sb("top", [P, NG, QG, 2])
        peak = sb("peak1", [P, NG, QG])
        w = sb("w", [P, NG, QG])
        w_hl = sb("w_hl", [P, NG, QG, 2], F32R)
        pt = [sb(f"pt{k}", [P, HALF]) for k in range(plan.RING)]
        pt_h = [sb(f"pt_h{k}", [P, HALF], F32R) for k in range(plan.RING)]
        pt_l = [sb(f"pt_l{k}", [P, HALF], F32R) for k in range(plan.RING)]
        ot = [sb(f"ot{k}", [VC, HALF]) for k in range(2)]
        share = sb("share", [P, QG])
        osum = sb("osum", [P, QG, HD])
        p_s = [ps(f"p_s{k}", [P, CHUNK]) for k in range(2)]
        p_t = [ps(f"p_t{k}", [P, HALF]) for k in range(2)]
        p_o = [ps(f"p_o{k}", [P, HALF]) for k in range(2)]

        slopes_in = sem("slopes_in")
        tables_made = sem("tables_made")
        table_step = sem("table_step")
        stack_in = [sem(f"stack_in{b}") for b in range(3)]
        v_in = [sem(f"v_in{b}") for b in range(3)]
        bias_made = sem("bias_made")
        spos_made = sem("spos_made")
        vs_step = sem("vs_step")
        item_done = sem("item_done")
        item_used = sem("item_used")
        w_step = sem("w_step")
        w_made = sem("w_made")
        st_done = sem("st_done")
        exp_done = sem("exp_done")
        high_a = sem("high_a")
        high_d = sem("high_d")
        low_p = sem("low_p")
        low_d = sem("low_d")
        pv_done = sem("pv_done")
        ot_copied = sem("ot_copied")
        o_made = sem("o_made")
        block = ctx.enter_context(nc.Block())

        def heads(eng, body):
            for h in range(2):
                body(h, h % 3)
            with eng.Fori(0, (H - 5) // 3) as i:
                for b in range(3):
                    body(i * 3 + (2 + b), (2 + b) % 3)
            for h in range(H - 3, H):
                body(h, h % 3)

        def count(kinds, kind, h, s):
            return kinds.count(kind) * h + kinds[:s + 1].count(kind)

        def high_ready(eng, h, s):
            eng_high = {"A": high_a, "D": high_d}[plan.high[s]]
            after(eng, eng_high, count(plan.high, plan.high[s], h, s))

        def low_ready(eng, h, s):
            eng_low = {"P": low_p, "D": low_d}[plan.low[s]]
            after(eng, eng_low, count(plan.low, plan.low[s], h, s))

        def exists(h):
            return not isinstance(h, int) or h >= 0

        def masked_columns(g, k):
            return P * max(0, k - QG * g)

        @block.sync
        def _(sp):
            sp.dma_start(slopes[:], a["slopes"]).then_inc(slopes_in, 16)

            passed = nc.alloc_semaphore("passed_sp")

            def load(h, b):
                row = bass.ds(h * HD, HD)
                for n, (q, k) in enumerate((("qh", "kh"), ("ql", "kh"), ("qh", "kl"))):
                    sp.dma_start(wide(qs[b][n * HD:(n + 1) * HD, :]), a[q][row, :]).then_inc(stack_in[b], 16)
                    sp.dma_start(wide(ks[b][n * HD:(n + 1) * HD, :]), a[k][row, :]).then_inc(stack_in[b], 16)
                sp.dma_start(v_raw[b][:].rearrange("p t d -> p (t d)"),
                             a["v_dram"][bass.ds(h, 1)].rearrange("a p t d -> (a p) (t d)")).then_inc(v_in[b], 48)
            load(0, 0)
            load(1, 1)

            def period(h, b):
                if isinstance(h, int) and h + 2 >= H:
                    return
                after_plainly(sp, passed, st_done, N * h)
                after_plainly(sp, passed, vs_step, 2 * h)
                load(h + 2, (b + 2) % 3)
            heads(sp, period)

        @block.gpsimd
        def _(pool):
            step = Chain(pool, table_step)
            step.link(pool.iota(rel[:], pattern=[[1, T]], base=-DIAG, channel_multiplier=-1,
                                allow_small_or_imprecise_dtypes=True))
            step.link(pool.affine_select(out=rel[:], in_=rel[:], compare_op=ALU.is_ge, fill=MASKED, base=DIAG,
                                         pattern=[[-1, T]], channel_multiplier=1))
            step.link(pool.iota(pos[:, 0:DELTAS], pattern=[[P, DELTAS]], base=-(DELTAS - QG) * P - MID, channel_multiplier=1,
                                allow_small_or_imprecise_dtypes=True))
            step.link(pool.iota(pos[:, DELTAS:], pattern=[[P, QG]], base=-MID, channel_multiplier=1,
                                allow_small_or_imprecise_dtypes=True))
            step.link(pool.tensor_copy(ident_b[:], ident[:]))
            step.link(pool.memset(mask_b[:], 0.0))
            step.link(pool.affine_select(out=mask_b[:], in_=mask_b[:], compare_op=ALU.is_ge, fill=MASKED, base=0,
                                         pattern=[[1, P]], channel_multiplier=-1))
            for b in range(3):
                step.link(pool.memset(wide(ks[b][ROWS:ROWS + 2, :]), 1.0))
                step.link(pool.memset(wide(vs[b][:, :, 2 * HD:VC]), 1.0))
            pool.sem_inc(tables_made, 1)

            def period(h, _):
                for s in range(N):
                    if plan.low[s] != "P":
                        continue
                    u, g, k = plan.slots[s]
                    c = masked_columns(g, k)
                    r = s % plan.RING
                    after(pool, exp_done, N * h + s + 1)
                    high_ready(pool, h, s)
                    before = back(h, s, plan.RING, N)
                    after(pool, pv_done, N * before[0] + before[1] + 1)
                    pool.tensor_tensor(pt_l[r][:, c:], pt[r][:, c:], wide(pt_h[r][:, c:]), ALU.subtract).then_inc(low_p, 1)
            heads(pool, period)

        @block.vector
        def _(dve):
            passed = nc.alloc_semaphore("passed_dve")
            dve.wait_ge(slopes_in, 16)
            dve.wait_ge(tables_made, 1)

            def tables(h, b):
                slope = slopes[:, bass.ds(h, 1)]
                if not isinstance(h, int) or h:
                    dve.wait_ge(item_used, plan.period(h - 1)[0][2])
                dve.tensor_scalar(bias[:], rel[:], slope, None, ALU.mult).then_inc(bias_made, 1)
                dve.tensor_scalar(spos[b][:], pos[:], slope, None, ALU.mult).then_inc(spos_made, 1)
                dve.wait_ge(v_in[b], (h - b) * 16 + 48)
                after(dve, pv_done, N * (h - 2))
                dve.tensor_copy(vs[b][:, :, 0:HD], v_raw[b][:]).then_inc(vs_step, 1)
                dve.wait_ge(vs_step, 2 * h + 1)
                dve.tensor_tensor(vs[b][:, :, HD:2 * HD], v_raw[b][:], wide(vs[b][:, :, 0:HD]), ALU.subtract).then_inc(vs_step, 1)

            def score(h, b, x, n, buf):
                _, u, q, c = x
                g = plan.groups[u]
                width = min(CHUNK, plan.width(x) - c)
                off = DIAG - (plan.width(x) - P) + c
                pieces = [y for y in plan.ahead if y[0] == "score"]
                if x == pieces[0]:
                    dve.wait_ge(bias_made, h + 1)
                after_plainly(dve, passed, item_done, n + 1)
                dve.tensor_tensor_reduce(unread[buf][:, 0:width], p_s[buf][:, 0:width], bias[:, off:off + width], 1.0, MASKED,
                                         ALU.add, ALU.max, top[:, u, q, c // CHUNK:c // CHUNK + 1]).then_inc(item_used, 1)
                if x != [y for y in pieces if y[1] == u][-1]:
                    return
                dve.wait_ge(item_used, n + 1)
                m = top[:, u, :, 0]
                if g >= NG // 2:
                    dve.tensor_reduce(peak[:, u, :], top[:, u, :, :], AX_X, ALU.max).then_inc(w_step, 1)
                    dve.wait_ge(w_step, (3 * NG - NG // 2) * h + 3 * u + 1)
                    m = peak[:, u, :]
                done = (3 * NG - NG // 2) * h + sum(3 if y >= NG // 2 else 2 for y in plan.groups[:u + 1])
                after(dve, w_made, NG * (h - 1) + u + 1)
                dve.scalar_tensor_tensor(out=w[:, u, :], in0=m, scalar=-1.0, in1=spos[b][:, DELTAS:], op0=ALU.mult,
                                         op1=ALU.subtract).then_inc(w_step, 1)
                dve.wait_ge(w_step, done - 1)
                dve.tensor_copy(w_hl[:, u, :, 0], w[:, u, :]).then_inc(w_step, 1)
                dve.wait_ge(w_step, done)
                dve.tensor_tensor(w_hl[:, u, :, 1], w[:, u, :], wide(w_hl[:, u, :, 0]), ALU.subtract).then_inc(w_made, 1)

            def shift(h, b, x, n, buf):
                g = plan.groups[x[1]]
                dve.wait_ge(item_done, n + 1)
                dve.tensor_copy(qs[b][ROWS:ROWS + 2, g * HALF:(g + 1) * HALF], p_s[buf][0:2, 0:HALF]).then_inc(item_used, 1)

            def output(h, x, n, buf):
                g = plan.groups[x[1]]
                got = p_s[buf][:, 0:QG * OC].rearrange("p (q c) -> p q c", q=QG)
                U = NG * h + x[1]
                dve.wait_ge(item_done, n + 1)
                after(dve, o_made, U)
                dve.reciprocal(share[:], got[:, :, 2 * HD])
                dve.tensor_reduce(osum[:], got[:, :, 0:2 * HD].rearrange("p q (a d) -> p q d a", a=2), AX_X, ALU.add).then_inc(item_used, 1)
                dve.wait_ge(item_used, n + 1)
                dve.tensor_tensor(o[:, QG * g:QG * g + QG, bass.ds(h * HD, HD)], osum[:],
                                  share[:].unsqueeze(2).to_broadcast([P, QG, HD]), ALU.mult).then_inc(o_made, 1)

            def item(h, b, x, n, buf):
                if x[0] == "score":
                    score(h + 1, (b + 1) % 3, x, n, buf)
                elif x[0] == "shift":
                    shift(h + 1, (b + 1) % 3, x, n, buf)
                else:
                    output(h - x[2], x, n, buf)

            def part(h, s):
                if not exists(h):
                    return
                u, g, k = plan.slots[s]
                c = masked_columns(g, k)
                r = s % plan.RING
                before = back(h, s, plan.RING, N)
                if plan.high[s] == "D" or plan.low[s] == "D":
                    dve.wait_ge(exp_done, N * h + s + 1)
                    after(dve, pv_done, N * before[0] + before[1] + 1)
                if plan.high[s] == "D":
                    dve.tensor_copy(pt_h[r][:, c:], pt[r][:, c:]).then_inc(high_d, 1)
                if plan.low[s] == "D":
                    high_ready(dve, h, s)
                    dve.tensor_tensor(pt_l[r][:, c:], pt[r][:, c:], wide(pt_h[r][:, c:]), ALU.subtract).then_inc(low_d, 1)

            tables(0, 0)
            for _, x, n in plan.period(-1):
                item(-1, 2, x, n, n % 2)

            def period(h, b):
                if not (isinstance(h, int) and h == H - 1):
                    tables(h + 1, (b + 1) % 3)
                items = plan.period(h)
                for s in range(N):
                    for i, (t, x, n) in enumerate(items):
                        if t == s:
                            item(h, b, x, n, plan.buffer(h, i))
                    part(*back(h, s, 1, N))
            heads(dve, period)
            part(H - 1, N - 1)
            for i, (x, n) in enumerate(tail(plan)):
                output(H - 1, x, n, plan.buffer(H - 1, len(plan.present(H - 1)) + i))

        @block.scalar
        def _(act):
            def exponentials(h, b, s):
                u, g, k = plan.slots[s]
                c = masked_columns(g, k)
                r = s % plan.RING
                if s == 0:
                    act.wait_ge(spos_made, h + 1)
                before = back(h, s, plan.RING, N)
                if exists(before[0]):
                    low_ready(act, *before)
                at = k - QG * g + DELTAS - QG
                act.wait_ge(st_done, N * h + s + 1)
                act.activation(pt[r][:, c:], p_t[s % 2][:, c:], ACT.Exp, bias=spos[b][:, at:at + 1]).then_inc(exp_done, 1)
                if plan.high[s] == "A":
                    after(act, pv_done, N * before[0] + before[1] + 1)
                    act.activation(pt_h[r][:, c:], p_t[s % 2][:, c:], ACT.Exp, bias=spos[b][:, at:at + 1]).then_inc(high_a, 1)

            def copy_out(h, u):
                if not exists(h):
                    return
                act.wait_ge(pv_done, N * h + plan.ends[u] + 1)
                after(act, o_made, NG * h + u - 1)
                act.activation(ot[u % 2][:], p_o[u % 2][0:VC, :], ACT.Copy).then_inc(ot_copied, 1)

            def period(h, b):
                for s in range(N):
                    exponentials(h, b, s)
                    for u in range(NG):
                        at = plan.ends[u] + plan.LAG
                        if at % N == s:
                            copy_out(h - at // N, u)
            heads(act, period)
            for u in range(NG):
                if plan.ends[u] + plan.LAG >= N:
                    copy_out(H - 1, u)

        @block.tensor
        def _(pe):
            passed = nc.alloc_semaphore("passed_pe")
            pe.wait_ge(tables_made, 1)

            def score(h, b, x, buf):
                _, u, q, c0 = x
                end = min(c0 + CHUNK, plan.width(x))
                base = plan.width(x) - P
                if x == plan.ahead[0]:
                    pe.wait_ge(stack_in[b], (h - b) * 32 + 96)
                for c in range(c0, end, HALF):
                    n = min(HALF, end - c)
                    last = pe.matmul(p_s[buf][:, c - c0:c - c0 + n], qs[b][0:ROWS, base:base + P], ks[b][0:ROWS, c:c + n],
                                     start=True, stop=True)
                return last

            def turn_shift(h, x, buf):
                u = x[1]
                pe.wait_ge(w_made, NG * h + u + 1)
                for q in range(QG):
                    last = pe.transpose(p_s[buf][0:2, q * P:(q + 1) * P], wide(w_hl[:, u, q, :]), ident[:])
                return last

            def turn_out(h, x, buf):
                u = x[1]
                after_plainly(pe, passed, ot_copied, NG * h + u + 1)
                for q in range(QG):
                    last = pe.transpose(p_s[buf][:, q * OC:q * OC + VC], ot[u % 2][:, q * P:(q + 1) * P], ident[0:VC, 0:VC])
                return last

            def item(h, b, x, n, buf):
                after(pe, item_used, n - 1)
                if x[0] == "score":
                    last = score(h + 1, (b + 1) % 3, x, buf)
                elif x[0] == "shift":
                    last = turn_shift(h + 1, x, buf)
                else:
                    last = turn_out(h - x[2], x, buf)
                last.then_inc(item_done, 1)

            def key_scores(h, b, s):
                u, g, k = plan.slots[s]
                c = masked_columns(g, k)
                if k == 0:
                    pe.wait_ge(item_used, [n for _, x, n in plan.period(h - 1) if x == ("shift", u)][0] + 1)
                before = back(h, s, 2, N)
                if exists(before[0]):
                    if plan.high[before[1]] == "A":
                        high_ready(pe, *before)
                    else:
                        after(pe, exp_done, N * before[0] + before[1] + 1)
                last = pe.matmul(p_t[s % 2][:, c:], ks[b][0:ROWS + 2, k * P:(k + 1) * P],
                                 qs[b][0:ROWS + 2, g * HALF + c:(g + 1) * HALF], start=True, stop=(k < QG * g))
                if k >= QG * g:
                    last = pe.matmul(p_t[s % 2][:, c:c + P], ident_b[:], mask_b[:], start=False, stop=True)
                last.then_inc(st_done, 1)

            def weigh(h, b, s):
                if not exists(h):
                    return
                u, g, k = plan.slots[s]
                c = masked_columns(g, k)
                r = s % plan.RING
                if s == 0:
                    pe.wait_ge(vs_step, 2 * h + 2)
                if k == 0:
                    after(pe, ot_copied, NG * h + u - 1)
                high_ready(pe, h, s)
                pe.matmul(p_o[u % 2][0:VC, c:], vs[b][:, k, :], pt_h[r][:, c:], start=(k == 0), stop=False)
                low_ready(pe, h, s)
                pe.matmul(p_o[u % 2][0:VC, c:], vs[b][:, k, :], pt_l[r][:, c:], start=False, stop=(k == QG * g + QG - 1)
                          ).then_inc(pv_done, 1)

            for _, x, n in plan.period(-1):
                item(-1, 2, x, n, n % 2)

            def period(h, b):
                items = plan.period(h)
                for s in range(N):
                    key_scores(h, b, s)
                    for i, (t, x, n) in enumerate(items):
                        if t == s:
                            item(h, b, x, n, plan.buffer(h, i))
                    weigh(back(h, s, plan.LAG, N)[0], b if s >= plan.LAG else (b + 2) % 3, back(h, s, plan.LAG, N)[1])
            heads(pe, period)
            for s in range(N - plan.LAG, N):
                weigh(H - 1, (H - 1) % 3, s)
            for i, (x, n) in enumerate(tail(plan)):
                item(H - 1, (H - 1) % 3, x, n, plan.buffer(H - 1, len(plan.present(H - 1)) + i))


def tail(plan):
    number = plan.period(H - 1)[-1][2] + 1
    late = [x for _, x in plan.items if x[0] == "output" and x[2]]
    return [(("output", x[1], 0), number + i) for i, x in enumerate(late)]


def root_of_variance(dve, ln, act_root_ready, count, sd, rstd):
    dve.wait_ge(act_root_ready, count)
    ln.link(dve.reciprocal(sd[:, 2:3], sd[:, 1:2]))
    ln.link(dve.scalar_tensor_tensor(out=sd[:, 3:4], in0=sd[:, 2:3], scalar=sd[:, 0:1], in1=sd[:, 1:2],
                                     op0=ALU.mult, op1=ALU.add))
    ln.link(dve.tensor_scalar(sd[:, 2:3], sd[:, 3:4], 0.5, None, ALU.mult))
    return dve.reciprocal(rstd, sd[:, 2:3])


def phase_project(nc, a, o, norm, ident):
    with ExitStack() as ctx:
        sb = lambda n, s, d=F32: ctx.enter_context(nc.sbuf_tensor(n, s, d))
        ps = lambda n, s: ctx.enter_context(nc.psum_tensor(n, s, F32))
        sem = lambda n: ctx.enter_context(nc.semaphore(n))
        w_raw = [sb(f"wp_raw{k}", [P, D]) for k in range(2)]
        w_h = sb("wp_h", [P, KT, D], F32R)
        w_l = sb("wp_l", [P, KT, D], F32R)
        bias = sb("p_bias", [P, D])
        h_in = [sb(f"h_in{b}", [P, D]) for b in range(2)]
        o_now = [sb(f"o_now{b}", [P, D]) for b in range(2)]
        a_h = [sb(f"a_h{b}", [P, KT, P], F32R) for b in range(2)]
        a_l = [sb(f"a_l{b}", [P, KT, P], F32R) for b in range(2)]
        stats = sb("stats2", [P, 2, 6])
        mv = sb("mv2", [P, 2])
        sd = sb("sd2", [P, 4])
        p_x = ps("p_x2", [P, KT, P])
        p_e = [ps(f"p_e{b}", [P, D]) for b in range(2)]

        bias_in = sem("p_bias_in")
        w_in = [sem(f"wp_in{k}") for k in range(2)]
        w_high = sem("wp_high")
        w_split = sem("wp_split")
        h_loaded = [sem(f"h_loaded{b}") for b in range(2)]
        h_biased = sem("h_biased")
        o_copied = sem("o_copied")
        at_done = sem("at2_done")
        at_high = sem("at2_high")
        at_split = sem("at2_split")
        e_done = sem("e_done")
        h2_ready = sem("h2_ready")
        var_ready = sem("var2_ready")
        root_ready = sem("root2_ready")
        norm_ready = sem("norm_ready")
        ln_step = sem("ln2_step")
        block = ctx.enter_context(nc.Block())

        @block.sync
        def _(sp):
            sp.dma_start(bias[:], a["b_proj"].to_broadcast([P, D])).then_inc(bias_in, 16)
            for k in range(KT):
                after(sp, w_split, k - 1)
                sp.dma_start(w_raw[k % 2][:], a["w_proj"][k * P:(k + 1) * P, :]).then_inc(w_in[k % 2], 16)

            def tile(i):
                for b in range(2):
                    t = 2 * i + b
                    after(sp, h2_ready, t - 1)
                    sp.dma_start(h_in[b][:], a["h_dram"][bass.ds(t, 1)].rearrange("a p d -> (a p) d")).then_inc(h_loaded[b], 16)
            repeat(sp, NT // 2, tile)

        @block.gpsimd
        def _(pool):
            def copy(t, b):
                after(pool, at_done, t - 1)
                pool.tensor_copy(o_now[b][:], o[:, bass.ds(t, 1), :].rearrange("p a d -> p (a d)")).then_inc(o_copied, 1)
            copy(0, 0)
            pool.wait_ge(bias_in, 16)

            def tile(i):
                for b in range(2):
                    t = 2 * i + b
                    if not (isinstance(i, int) and t == NT - 1):
                        copy(t + 1, 1 - b)
                    pool.wait_ge(h_loaded[b], 16 * i + 16)
                    pool.tensor_tensor(h_in[b][:], h_in[b][:], bias[:], ALU.add).then_inc(h_biased, 1)
            repeat(pool, NT // 2, tile)

        @block.scalar
        def _(act):
            def high(t, b):
                act.wait_ge(at_done, t + 1)
                after(act, e_done, t - 1)
                act.activation(a_h[b][:], p_x[:], ACT.Copy).then_inc(at_high, 1)
            for k in range(KT):
                act.wait_ge(w_in[k % 2], 16 * (k // 2 + 1))
                act.activation(w_h[:, k, :], w_raw[k % 2][:], ACT.Copy).then_inc(w_high, 1)
            high(0, 0)

            def tile(i):
                for b in range(2):
                    t = 2 * i + b
                    if not (isinstance(i, int) and t == NT - 1):
                        high(t + 1, 1 - b)
                    act.wait_ge(var_ready, t + 1)
                    act.activation(sd[:, 1:2], sd[:, 0:1], ACT.Sqrt).then_inc(root_ready, 1)
            repeat(act, NT // 2, tile)

        @block.vector
        def _(dve):
            passed = nc.alloc_semaphore("passed6")
            ln = Chain(dve, ln_step, passed)

            def low(t, b):
                dve.wait_ge(at_high, t + 1)
                dve.tensor_tensor(a_l[b][:], p_x[:], wide(a_h[b][:]), ALU.subtract).then_inc(at_split, 1)
            for k in range(KT):
                dve.wait_ge(w_high, k + 1)
                dve.tensor_tensor(w_l[:, k, :], w_raw[k % 2][:], wide(w_h[:, k, :]), ALU.subtract).then_inc(w_split, 1)
            low(0, 0)

            def tile(i):
                ln.begin(i)
                for b in range(2):
                    t = 2 * i + b
                    if not (isinstance(i, int) and t == NT - 1):
                        low(t + 1, 1 - b)
                    dve.wait_ge(h_biased, t + 1)
                    dve.wait_ge(e_done, t + 1)
                    dve.wait_ge(o_copied, t + 1)
                    dve.tensor_tensor(o[:, bass.ds(t, 1), :].rearrange("p a d -> p (a d)"), p_e[b][:], h_in[b][:], ALU.add
                                      ).then_inc(h2_ready, 1)
                    after_plainly(dve, passed, h2_ready, t + 1)
                    for k in range(2):
                        ins = dve.bn_stats(stats[:, k, :], o[:, bass.ds(t, 1), k * HALF:(k + 1) * HALF].rearrange("p a d -> p (a d)"))
                    ln.link(ins, plainly=True)
                    ln.link(dve.bn_aggr(mv[:], stats[:]))
                    dve.tensor_copy(norm[:, bass.ds(t, 1), 0:1].rearrange("p a k -> p (a k)"), mv[:, 0:1])
                    dve.tensor_scalar(sd[:, 0:1], mv[:, 1:2], EPS, None, ALU.add).then_inc(var_ready, 1)
                    root_of_variance(dve, ln, root_ready, t + 1, sd, norm[:, bass.ds(t, 1), 1:2].rearrange("p a k -> p (a k)")
                                     ).then_inc(norm_ready, 1)
            repeat(dve, NT // 2, tile)

        @block.tensor
        def _(pe):
            def turn(t, b):
                pe.wait_ge(o_copied, t + 1)
                after(pe, at_split, t)
                for k in range(KT):
                    last = pe.transpose(p_x[:, k, :], o_now[b][:, k * P:(k + 1) * P], ident[:])
                last.then_inc(at_done, 1)
            turn(0, 0)
            pe.wait_ge(w_split, KT)

            def tile(i):
                for b in range(2):
                    t = 2 * i + b
                    pe.wait_ge(at_split, t + 1)
                    after(pe, h2_ready, t - 1)
                    for c in range(2):
                        n = slice(c * HALF, (c + 1) * HALF)
                        for k in range(KT):
                            last = product3(pe, p_e[b][:, n], a_h[b][:, k, :], a_l[b][:, k, :], w_h[:, k, n], w_l[:, k, n],
                                            k == 0, k == KT - 1)
                        if c == 0 and not (isinstance(i, int) and t == NT - 1):
                            turn(t + 1, 1 - b)
                    last.then_inc(e_done, 1)
            repeat(pe, NT // 2, tile)


def phase_ffn(nc, a, o, norm, ident):
    with ExitStack() as ctx:
        sb = lambda n, s, d=F32: ctx.enter_context(nc.sbuf_tensor(n, s, d))
        ps = lambda n, s: ctx.enter_context(nc.psum_tensor(n, s, F32))
        sem = lambda n: ctx.enter_context(nc.semaphore(n))
        RAW = KT * ZW
        w_raw = [sb(f"wf_raw{k}", [P, RAW]) for k in range(2)]
        w_h = sb("wf_h", [P, KT, D], F32R)
        w_l = sb("wf_l", [P, KT, D], F32R)
        z_h = sb("wz_h", [P, KT, ZW], F32R)
        z_l = sb("wz_l", [P, KT, ZW], F32R)
        l_h = sb("wl_h", [P, D], F32R)
        l_l = sb("wl_l", [P, D], F32R)
        weights = ([(a["w_z"], RAW, z_h[:].rearrange("p k n -> p (k n)"), z_l[:].rearrange("p k n -> p (k n)"))]
                   + [(a["w_base"][k * P:(k + 1) * P, :], D, w_h[:, k, :], w_l[:, k, :]) for k in range(KT)]
                   + [(a["w_lora"], D, l_h[:], l_l[:])])
        bias = sb("f_bias", [P, D])
        r_bias = sb("r_bias", [P, NR])
        emap = sb("emap", [P, NR], I32)
        emap_f = sb("emap_f", [P, NR])
        onehot = sb("onehot", [P, E, NR])
        norm_now = [sb(f"norm_now{b}", [P, 2]) for b in range(2)]
        xn = sb("xn2", [P, D])
        x_h = [sb(f"x2_h{b}", [P, KT, P], F32R) for b in range(2)]
        x_l = [sb(f"x2_l{b}", [P, KT, P], F32R) for b in range(2)]
        rest = [sb(f"rest{b}", [P, D]) for b in range(2)]
        out = [sb(f"out{b}", [P, D]) for b in range(2)]
        logit = sb("logit", [P, NR])
        peak = sb("peak", [P, 2])
        ex = sb("ex", [P, NR])
        ex_sum = sb("ex_sum", [P, 2])
        prob = sb("prob", [P, NR])
        top8 = sb("top8", [P, 8])
        unchosen = sb("unchosen", [P, NR])
        spread = sb("spread", [P, E, NR])
        gate = sb("gate", [P, E])
        hw = sb("hw", [P, ER])
        hwt_h = sb("hwt_h", [P, P], F32R)
        hwt_l = sb("hwt_l", [P, P], F32R)
        p_x = ps("p_x3", [P, KT, P])
        p_e = [ps(f"p_f{b}", [P, D]) for b in range(2)]
        p_z = ps("p_z", [P, HALF])
        p_hw = ps("p_hw", [P, HALF])

        small_in = sem("small_in")
        bias_in = sem("f_bias_in")
        w_in = [sem(f"wf_in{k}") for k in range(2)]
        w_high = sem("wf_high")
        w_split = sem("wf_split")
        map_step = sem("map_step")
        norm_got = sem("norm_got")
        rest_ready = sem("rest_ready")
        xn_ready = sem("xn3_ready")
        xt_done = sem("xt3_done")
        xt_high = sem("xt3_high")
        xt_split = sem("xt3_split")
        z_done = sem("z_done")
        route = sem("route")
        logit_ready = sem("logit_ready")
        exp_ready = sem("exp_ready")
        hw_ready = sem("hw_ready")
        hwt_done = sem("hwt_done")
        hwt_high = sem("hwt_high")
        hwt_split = sem("hwt_split")
        e_done = sem("f_done")
        out_ready = sem("out_ready")
        stored = [sem(f"stored{b}") for b in range(2)]
        block = ctx.enter_context(nc.Block())

        def last_tile(i, t):
            return isinstance(i, int) and t == NT - 1

        @block.sync
        def _(sp):
            sp.dma_start(r_bias[:], a["b_router"].to_broadcast([P, NR])).then_inc(small_in, 16)
            sp.dma_start(emap[:], a["expert_map"].to_broadcast([P, NR])).then_inc(small_in, 16)
            sp.dma_start(bias[:], a["b_base"].to_broadcast([P, D])).then_inc(bias_in, 16)
            for n, (src, w, _, _) in enumerate(weights):
                after(sp, w_split, n - 1)
                sp.dma_start(w_raw[n % 2][:, 0:w], src).then_inc(w_in[n % 2], 16)

            def tile(i):
                for b in range(2):
                    t = 2 * i + b
                    sp.wait_ge(out_ready, t + 1)
                    sp.dma_start(a["out"][bass.ds(t, 1)].rearrange("a p d -> (a p) d"), out[b][:]).then_inc(stored[b], 16)
            repeat(sp, NT // 2, tile)
            for b in range(2):
                sp.wait_ge(stored[b], 16 * NT // 2)

        @block.gpsimd
        def _(pool):
            pool.wait_ge(bias_in, 16)

            def tile(i):
                for b in range(2):
                    t = 2 * i + b
                    after(pool, xn_ready, t - 1)
                    pool.tensor_copy(norm_now[b][:], norm[:, bass.ds(t, 1), :].rearrange("p a k -> p (a k)")).then_inc(norm_got, 1)
                    after(pool, out_ready, t - 1)
                    pool.tensor_tensor(rest[b][:], o[:, bass.ds(t, 1), :].rearrange("p a d -> p (a d)"), bias[:], ALU.add
                                       ).then_inc(rest_ready, 1)
            repeat(pool, NT // 2, tile)

        @block.scalar
        def _(act):
            def high(t, b):
                act.wait_ge(xt_done, t + 1)
                after(act, e_done, t - 1)
                act.activation(x_h[b][:], p_x[:], ACT.Copy).then_inc(xt_high, 1)
            for n, (_, w, wh, _) in enumerate(weights):
                act.wait_ge(w_in[n % 2], 16 * (n // 2 + 1))
                act.activation(wh, w_raw[n % 2][:, 0:w], ACT.Copy).then_inc(w_high, 1)
            high(0, 0)

            def tile(i):
                for b in range(2):
                    t = 2 * i + b
                    act.wait_ge(logit_ready, t + 1)
                    act.activation(ex[:], logit[:], ACT.Exp, bias=peak[:, 1:2], accum_out=ex_sum[:, 0:1]).then_inc(exp_ready, 1)
                    if not last_tile(i, t):
                        high(t + 1, 1 - b)
                    act.wait_ge(hwt_done, t + 1)
                    after(act, e_done, t)
                    act.activation(hwt_h[:], p_hw[:, 0:P], ACT.Copy).then_inc(hwt_high, 1)
            repeat(act, NT // 2, tile)

        @block.vector
        def _(dve):
            passed = nc.alloc_semaphore("passed7")
            step = Chain(dve, map_step)
            dve.wait_ge(small_in, 32)
            step.link(dve.tensor_copy(emap_f[:], emap[:]))
            for e in range(E):
                ins = dve.tensor_scalar(onehot[:, e, :], emap_f[:], float(e), FFN_SCALE, ALU.is_equal, ALU.mult)
            step.link(ins)

            def normalise(t, b):
                dve.wait_ge(norm_got, t + 1)
                after(dve, xt_done, t)
                dve.tensor_scalar(xn[:], o[:, bass.ds(t, 1), :].rearrange("p a d -> p (a d)"), norm_now[b][:, 0:1],
                                  norm_now[b][:, 1:2], ALU.subtract, ALU.mult).then_inc(xn_ready, 1)

            def low(t, b):
                dve.wait_ge(xt_high, t + 1)
                dve.tensor_tensor(x_l[b][:], p_x[:], wide(x_h[b][:]), ALU.subtract).then_inc(xt_split, 1)
            normalise(0, 0)
            for n, (_, w, wh, wl) in enumerate(weights):
                dve.wait_ge(w_high, n + 1)
                dve.tensor_tensor(wl, w_raw[n % 2][:, 0:w], wide(wh), ALU.subtract).then_inc(w_split, 1)
            low(0, 0)
            r = Chain(dve, route, passed)

            def tile(i):
                r.begin(i)
                for b in range(2):
                    t = 2 * i + b
                    if not last_tile(i, t):
                        normalise(t + 1, 1 - b)
                    dve.wait_ge(z_done, t + 1)
                    r.link(dve.tensor_tensor(logit[:], p_z[:, ER:ER + NR], r_bias[:], ALU.add))
                    r.link(dve.tensor_reduce(peak[:, 0:1], logit[:], AX_X, ALU.max))
                    dve.tensor_scalar(peak[:, 1:2], peak[:, 0:1], -1.0, None, ALU.mult).then_inc(logit_ready, 1)
                    dve.wait_ge(exp_ready, t + 1)
                    r.link(dve.reciprocal(ex_sum[:, 1:2], ex_sum[:, 0:1]))
                    r.link(dve.tensor_scalar(prob[:], ex[:], ex_sum[:, 1:2], None, ALU.mult), plainly=True)
                    r.link(dve.max(top8[:], prob[:]), plainly=True)
                    r.link(dve.match_replace(unchosen[:], top8[:], prob[:], 0.0))
                    r.link(dve.tensor_tensor(prob[:], prob[:], unchosen[:], ALU.subtract))
                    r.link(dve.tensor_tensor(spread[:], onehot[:], prob[:].unsqueeze(1).to_broadcast([P, E, NR]), ALU.mult))
                    r.link(dve.tensor_reduce(gate[:], spread[:], AX_X, ALU.add))
                    after(dve, hwt_done, t)
                    dve.tensor_tensor(hw[:].rearrange("p (e r) -> p e r", e=E), p_z[:, 0:ER].rearrange("p (e r) -> p e r", e=E),
                                      gate[:].unsqueeze(2).to_broadcast([P, E, ER // E]), ALU.mult).then_inc(hw_ready, 1)
                    if not last_tile(i, t):
                        low(t + 1, 1 - b)
                    dve.wait_ge(hwt_high, t + 1)
                    dve.tensor_tensor(hwt_l[:], p_hw[:, 0:P], wide(hwt_h[:]), ALU.subtract).then_inc(hwt_split, 1)
                    dve.wait_ge(e_done, t + 1)
                    dve.wait_ge(rest_ready, t + 1)
                    after(dve, stored[b], 16 * i)
                    dve.tensor_tensor(out[b][:], p_e[b][:], rest[b][:], ALU.add).then_inc(out_ready, 1)
            repeat(dve, NT // 2, tile)

        @block.tensor
        def _(pe):
            def turn(t):
                pe.wait_ge(xn_ready, t + 1)
                after(pe, xt_split, t)
                for k in range(KT):
                    last = pe.transpose(p_x[:, k, :], xn[:, k * P:(k + 1) * P], ident[:])
                last.then_inc(xt_done, 1)
            turn(0)
            pe.wait_ge(w_split, len(weights))

            def base(b, c):
                n = slice(c * HALF, (c + 1) * HALF)
                for k in range(KT):
                    product3(pe, p_e[b][:, n], x_h[b][:, k, :], x_l[b][:, k, :], w_h[:, k, n], w_l[:, k, n], k == 0, False)

            def tile(i):
                for b in range(2):
                    t = 2 * i + b
                    pe.wait_ge(xt_split, t + 1)
                    after(pe, hw_ready, t)
                    for k in range(KT):
                        last = product3(pe, p_z[:, 0:ZW], x_h[b][:, k, :], x_l[b][:, k, :], z_h[:, k, :], z_l[:, k, :],
                                        k == 0, k == KT - 1)
                    last.then_inc(z_done, 1)
                    after(pe, out_ready, t - 1)
                    base(b, 0)
                    if not last_tile(i, t):
                        turn(t + 1)
                    pe.wait_ge(hw_ready, t + 1)
                    after(pe, hwt_split, t)
                    pe.transpose(p_hw[:, 0:P], hw[:], ident[:]).then_inc(hwt_done, 1)
                    base(b, 1)
                    pe.wait_ge(hwt_split, t + 1)
                    for c in range(2):
                        n = slice(c * HALF, (c + 1) * HALF)
                        last = product3(pe, p_e[b][:, n], hwt_h[:], hwt_l[:], l_h[:, n], l_l[:, n], False, True)
                    last.then_inc(e_done, 1)
            repeat(pe, NT // 2, tile)


def build(nc, a):
    with ExitStack() as ctx:
        ident = ctx.enter_context(nc.sbuf_tensor("ident", [P, P], F32))
        norm = ctx.enter_context(nc.sbuf_tensor("norm", [P, NT, 2], F32))
        ident_made = ctx.enter_context(nc.semaphore("ident_made"))
        with ExitStack() as front:
            xh = front.enter_context(nc.sbuf_tensor("xh", [P, KT, T], F32R))
            xl = front.enter_context(nc.sbuf_tensor("xl", [P, KT, T], F32R))
            phase_embed(nc, a, xh, xl, ident, ident_made)
            phase_qkv(nc, a, xh, xl, ident)
        o = ctx.enter_context(nc.sbuf_tensor("o", [P, NT, D], F32))
        phase_attention(nc, a, o, ident)
        phase_project(nc, a, o, norm, ident)
        phase_ffn(nc, a, o, norm, ident)


def kernel(x, mask_BS_i1_0, mask_BS_i0_1, L0_tok_weight, L0_tok_lora_A_cl, L0_tok_lora_B_cl, L0_tok_lora_A_lm,
           L0_tok_lora_B_lm, L0_tok_lora_A_cl_prime, L0_tok_lora_B_cl_prime, L0_attn_w_attn, L0_attn_b_attn,
           L0_attn_w_proj, L0_attn_b_proj, L0_ffn_base_W, L0_ffn_base_b, L0_ffn_router_W, L0_ffn_router_b,
           L0_ffn_A, L0_ffn_B, L0_ffn_expert_map):
    import concourse.bacc as bacc
    from concourse.bass_utils import run_bass_kernel_spmd

    arr = lambda v: np.asarray(v)
    slopes = (2.0 ** (-2.0 ** -(np.log2(H) - 3))) ** np.arange(1, H + 1, dtype=np.float32)
    w_attn = arr(L0_attn_w_attn).reshape(KT, P, 3, KT, P)
    z = np.concatenate([arr(L0_ffn_A).reshape(ER, D), arr(L0_ffn_router_W), np.zeros((1, D), np.float32)])
    ins = {
        "ids": np.stack([arr(m).reshape(NT, P) for m in (x, mask_BS_i1_0, mask_BS_i0_1)]).transpose(2, 0, 1).reshape(P, 3 * NT),
        "tok_w": arr(L0_tok_weight),
        "tok_a1": arr(L0_tok_lora_A_cl),
        "tok_a2": np.concatenate([arr(L0_tok_lora_A_lm), arr(L0_tok_lora_A_cl_prime)], 1),
        "lora_b": np.stack([arr(m) for m in (L0_tok_lora_B_cl, L0_tok_lora_B_lm, L0_tok_lora_B_cl_prime)], 1),
        "w_qkv": w_attn.transpose(3, 2, 1, 0, 4).reshape(3 * KT, P, KT * P),
        "b_qkv": arr(L0_attn_b_attn).reshape(3, KT, P).transpose(2, 0, 1),
        "slopes": np.broadcast_to(slopes.astype(np.float32), (P, H)),
        "w_proj": arr(L0_attn_w_proj),
        "b_proj": arr(L0_attn_b_proj).reshape(1, D),
        "w_base": arr(L0_ffn_base_W).T,
        "b_base": arr(L0_ffn_base_b).reshape(1, D),
        "w_z": z.T.reshape(KT, P, ZW).transpose(1, 0, 2).reshape(P, KT * ZW),
        "b_router": arr(L0_ffn_router_b).reshape(1, NR),
        "w_lora": arr(L0_ffn_B).transpose(0, 2, 1).reshape(ER, D),
        "expert_map": arr(L0_ffn_expert_map).reshape(1, NR),
    }
    nc = bacc.Bacc("TRN2", target_bir_lowering=False, num_devices=1)
    arrays, a = {}, {}
    for name, v in ins.items():
        v = np.ascontiguousarray(v)
        arrays["in_" + name] = v
        a[name] = nc.dram_tensor("in_" + name, v.shape, mybir.dt.from_np(v.dtype), kind="ExternalInput").ap()
    for name in ("qh", "ql", "kh", "kl"):
        a[name] = nc.dram_tensor(name + "_scratch", (D, T), F32, kind="Internal").ap()
    a["v_dram"] = nc.dram_tensor("v_scratch", (H, P, NT, HD), F32, kind="Internal").ap()
    a["h_dram"] = nc.dram_tensor("h_scratch", (NT, P, D), F32, kind="Internal").ap()
    a["out"] = nc.dram_tensor("out_dram", (NT, P, D), F32, kind="ExternalOutput").ap()
    build(nc, a)
    r = run_bass_kernel_spmd(nc, [arrays], core_ids=[0])
    return r.results[0]["out_dram"].reshape(1, T, D)
```

```python
from contextlib import ExitStack

import numpy as np
import concourse.bass as bass
from concourse import mybir

F32 = mybir.dt.float32
F32R = mybir.dt.float32r
I32 = mybir.dt.int32
ALU = mybir.AluOpType
ACT = mybir.ActivationFunctionType
AX_X = mybir.AxisListType.X

P = 128
T = 2048
NT = T // P
D = 1024
KT = D // P
HALF = 512
V = 8000
R = 128
LORA = 3
TOK_SCALE = 2.0
EPS = 1e-5

H = 32
HD = D // H
VC = 2 * HD + 1
QG = 4
NG = NT // QG
ATT_SCALE = 1.0 / HD
CHUNK = 1024
MASKED = -1.0e36

E = 8
ER = 128
NR = 2 * E - 1
ZW = ER + NR + 1
FFN_SCALE = 2.0
WB = 4


def repeat(eng, n, body, peel=1):
    for i in range(peel):
        body(i)
    with eng.Fori(peel, n - 1) as i:
        body(i)
    body(n - 1)


def after(eng, sem, value):
    if isinstance(value, int) and value <= 0:
        return
    eng.wait_ge(sem, value)


def after_plainly(eng, passed, sem, value):
    after(eng, sem, value)
    if not isinstance(value, int):
        eng.sem_inc(passed, 1)


class Chain:

    def __init__(self, eng, sem, passed=None):
        self.eng, self.sem, self.passed, self.base, self.n, self.per = eng, sem, passed, 0, 0, None

    def begin(self, i):
        if self.per is None and not (isinstance(i, int) and i == 0):
            self.per = self.n - self.start
        if isinstance(i, int) and i == 0:
            self.start = self.n
            self.base = 0
        else:
            self.base = i * self.per + self.start
            self.n = 0

    def link(self, ins, plainly=False):
        self.n += 1
        ins.then_inc(self.sem, 1)
        if plainly:
            after_plainly(self.eng, self.passed, self.sem, self.base + self.n)
        else:
            self.eng.wait_ge(self.sem, self.base + self.n)


def product3(pe, out, ah, al, bh, bl, start, stop):
    pe.matmul(out, ah, bh, start=start, stop=False)
    pe.matmul(out, ah, bl, start=False, stop=False)
    return pe.matmul(out, al, bh, start=False, stop=stop)


def wide(t):
    return t.bitcast(F32)


def phase_embed(nc, a, xh, xl, ident, ident_made):
    with ExitStack() as ctx:
        sb = lambda n, s, d=F32: ctx.enter_context(nc.sbuf_tensor(n, s, d))
        ps = lambda n, s: ctx.enter_context(nc.psum_tensor(n, s, F32))
        sem = lambda n: ctx.enter_context(nc.semaphore(n))
        ids = sb("ids", [P, 3 * NT], I32)
        ids_f = sb("ids_f", [P, 3, NT])
        wrap = sb("wrap", [P, 3, NT])
        rows = sb("rows", [P, NT, 3], I32)
        row_w = [sb(f"row_w{b}", [P, 1], I32) for b in range(2)]
        row_a = [sb(f"row_a{b}", [P, 2], I32) for b in range(2)]
        lb_raw = sb("lb_raw", [P, LORA, D])
        lb_h = sb("lb_h", [P, LORA, D], F32R)
        lb_l = sb("lb_l", [P, LORA, D], F32R)
        w_row = [sb(f"w_row{b}", [P, D]) for b in range(2)]
        xn = [sb(f"xn{b}", [P, D]) for b in range(2)]
        a_row = [sb(f"a_row{b}", [P, LORA * R]) for b in range(2)]
        at_h = [sb(f"at_h{b}", [P, LORA, P], F32R) for b in range(2)]
        at_l = [sb(f"at_l{b}", [P, LORA, P], F32R) for b in range(2)]
        stats = sb("stats", [P, 2, 6])
        mv = sb("mv", [P, 2])
        sd = sb("sd", [P, 4])
        p_at = [ps(f"p_at{b}", [P, 4, P])[:, 0:LORA, :] for b in range(2)]
        p_lora = ps("p_lora", [P, D])
        p_xt = [ps(f"p_xt{b}", [P, KT, P]) for b in range(2)]

        ids_in = sem("ids_in")
        lb_in = sem("lb_in")
        lb_high = sem("lb_high")
        lb_split = sem("lb_split")
        rows_ready = sem("rows_ready")
        row_w_copied = sem("row_w_copied")
        row_a_copied = sem("row_a_copied")
        w_in = [sem(f"w_row_in{b}") for b in range(2)]
        a_in = [sem(f"a_row_in{b}") for b in range(2)]
        at_done = sem("at_done")
        at_high = sem("at_high")
        at_split = sem("at_split")
        lora_done = sem("lora_done")
        half_ready = sem("half_ready")
        h_ready = sem("h_ready")
        h_stored = [sem(f"h_stored{b}") for b in range(2)]
        var_ready = sem("var_ready")
        root_ready = sem("root_ready")
        xn_ready = sem("xn_ready")
        xt_done = sem("xt_done")
        xt_high = sem("xt_high")
        xt_split = sem("xt_split")
        idx_step = sem("idx_step")
        ln_step = sem("ln_step")
        block = ctx.enter_context(nc.Block())

        def last_tile(t):
            return isinstance(t, int) and t == NT - 1

        @block.sync
        def _(sp):
            sp.dma_start(ids[:], a["ids"]).then_inc(ids_in, 16)
            sp.dma_start(lb_raw[:], a["lora_b"]).then_inc(lb_in, 16)

            def tile(i):
                for b in range(2):
                    t = 2 * i + b
                    after(sp, h_ready, t + 1)
                    sp.dma_start(a["h_dram"][bass.ds(t, 1)].rearrange("a p d -> (a p) d"), w_row[b][:]).then_inc(h_stored[b], 16)
            repeat(sp, NT // 2, tile)
            for b in range(2):
                sp.wait_ge(h_stored[b], 16 * NT // 2)

        @block.gpsimd
        def _(pool):
            passed = nc.alloc_semaphore("passed1")
            pool.memset(ident[:], 0.0).then_inc(ident_made, 1)
            pool.wait_ge(ident_made, 1)
            pool.affine_select(out=ident[:], in_=ident[:], compare_op=ALU.not_equal, fill=1.0,
                               base=0, pattern=[[-1, P]], channel_multiplier=1).then_inc(ident_made, 1)
            pool.wait_ge(rows_ready, 1)

            def gather_a(t, b, before):
                after_plainly(pool, passed, a_in[b], 32 * before)
                pool.tensor_copy(row_a[b][:], rows[:, bass.ds(t, 1), 1:3].rearrange("p a k -> p (a k)")).then_inc(row_a_copied, 1)
                after(pool, at_done, t - 1)
                after_plainly(pool, passed, row_a_copied, t + 1)
                for k, (table, dst) in enumerate(((a["tok_a1"], a_row[b][:, 0:R]), (a["tok_a2"], a_row[b][:, R:LORA * R]))):
                    pool.indirect_dma_start(dst, None, table, bass.IndirectOffsetOnAxis(ap=row_a[b][:, k:k + 1], axis=0)
                                            ).then_inc(a_in[b], 16)

            def gather_w(t, b, before):
                after_plainly(pool, passed, w_in[b], 16 * before)
                pool.tensor_copy(row_w[b][:], rows[:, bass.ds(t, 1), 0:1].rearrange("p a k -> p (a k)")).then_inc(row_w_copied, 1)
                after(pool, xn_ready, t - 1)
                after(pool, h_stored[b], 16 * before)
                after_plainly(pool, passed, row_w_copied, t + 1)
                pool.indirect_dma_start(w_row[b][:], None, a["tok_w"], bass.IndirectOffsetOnAxis(ap=row_w[b][:, 0:1], axis=0)
                                        ).then_inc(w_in[b], 16)
            gather_a(0, 0, 0)

            def tile(i):
                for b in range(2):
                    t = 2 * i + b
                    if not last_tile(t):
                        gather_a(t + 1, 1 - b, i + b)
                    gather_w(t, b, i)
            repeat(pool, NT // 2, tile, 2)

        @block.vector
        def _(dve):
            passed = nc.alloc_semaphore("passed2")
            idx = Chain(dve, idx_step)
            dve.wait_ge(ids_in, 16)
            idx.link(dve.tensor_copy(ids_f[:].rearrange("p a t -> p (a t)"), ids[:]))
            for k in (1, 2):
                idx.link(dve.tensor_tensor(ids_f[:, k, :], ids_f[:, 0, :], ids_f[:, k, :], ALU.mult))
            idx.link(dve.tensor_scalar(wrap[:], ids_f[:], 0.0, float(V), ALU.is_lt, ALU.mult))
            idx.link(dve.tensor_tensor(ids_f[:], ids_f[:], wrap[:], ALU.add))
            idx.link(dve.tensor_scalar(ids_f[:], ids_f[:], 0.0, float(V - 1), ALU.max, ALU.min))
            dve.tensor_copy(rows[:].rearrange("p t k -> p k t"), ids_f[:]).then_inc(rows_ready, 1)
            dve.wait_ge(lb_high, 1)
            dve.tensor_tensor(lb_l[:], lb_raw[:], wide(lb_h[:]), ALU.subtract).then_inc(lb_split, 1)
            ln = Chain(dve, ln_step, passed)

            def split_xt(t, b, col):
                after(dve, xt_high, t + 1)
                dve.tensor_tensor(xl[:, :, bass.ds(col, P)], p_xt[b][:], wide(xh[:, :, bass.ds(col, P)]),
                                  ALU.subtract).then_inc(xt_split, 1)

            def low_at(t, b):
                after(dve, at_high, t + 1)
                dve.tensor_tensor(at_l[b][:], p_at[b], wide(at_h[b][:]), ALU.subtract).then_inc(at_split, 1)
            low_at(0, 0)

            def tile(i):
                ln.begin(i)
                for b in range(2):
                    t = 2 * i + b
                    if not last_tile(t):
                        low_at(t + 1, 1 - b)
                    dve.wait_ge(w_in[b], 16 * i + 16)
                    for k in range(2):
                        n = slice(k * HALF, (k + 1) * HALF)
                        dve.wait_ge(lora_done, 2 * t + k + 1)
                        ins = dve.scalar_tensor_tensor(out=w_row[b][:, n], in0=p_lora[:, n], scalar=TOK_SCALE, in1=w_row[b][:, n],
                                                       op0=ALU.mult, op1=ALU.add)
                        if k == 0:
                            ins.then_inc(half_ready, 1)
                    ln.link(ins)
                    after_plainly(dve, passed, half_ready, t + 1)
                    for k in range(2):
                        ins = dve.bn_stats(stats[:, k, :], w_row[b][:, k * HALF:(k + 1) * HALF])
                        if k == 0:
                            ins.then_inc(h_ready, 1)
                    ln.link(ins, plainly=True)
                    ln.link(dve.bn_aggr(mv[:], stats[:]))
                    dve.tensor_scalar(sd[:, 0:1], mv[:, 1:2], EPS, 0.25, ALU.add, ALU.mult).then_inc(var_ready, 1)
                    dve.wait_ge(root_ready, t + 1)
                    ln.link(dve.reciprocal(sd[:, 2:3], sd[:, 1:2]))
                    ln.link(dve.scalar_tensor_tensor(out=sd[:, 3:4], in0=sd[:, 2:3], scalar=sd[:, 0:1], in1=sd[:, 1:2],
                                                     op0=ALU.mult, op1=ALU.add))
                    ln.link(dve.reciprocal(sd[:, 2:3], sd[:, 3:4]))
                    after(dve, xt_done, t - 1)
                    dve.tensor_scalar(xn[b][:], w_row[b][:], mv[:, 0:1], sd[:, 2:3], ALU.subtract, ALU.mult
                                      ).then_inc(xn_ready, 1)
                    if b == 1:
                        split_xt(t - 1, 0, (t - 1) * P)
                    elif not (isinstance(i, int) and i == 0):
                        split_xt(t - 1, 1, (t - 1) * P)
            repeat(dve, NT // 2, tile, 2)
            split_xt(NT - 1, 1, (NT - 1) * P)

        @block.scalar
        def _(act):
            act.wait_ge(lb_in, 16)
            act.activation(lb_h[:], lb_raw[:], ACT.Copy).then_inc(lb_high, 1)

            def high_xt(t, b, col):
                after(act, xt_done, t + 1)
                act.activation(xh[:, :, bass.ds(col, P)], p_xt[b][:], ACT.Copy).then_inc(xt_high, 1)

            def high_at(t, b):
                act.wait_ge(at_done, t + 1)
                after(act, lora_done, 2 * (t - 1))
                act.activation(at_h[b][:], p_at[b], ACT.Copy).then_inc(at_high, 1)
            high_at(0, 0)

            def tile(i):
                for b in range(2):
                    t = 2 * i + b
                    if not last_tile(t):
                        high_at(t + 1, 1 - b)
                    act.wait_ge(var_ready, t + 1)
                    act.activation(sd[:, 1:2], sd[:, 0:1], ACT.Sqrt).then_inc(root_ready, 1)
                    if b == 1:
                        high_xt(t - 1, 0, (t - 1) * P)
                    elif not (isinstance(i, int) and i == 0):
                        high_xt(t - 1, 1, (t - 1) * P)
            repeat(act, NT // 2, tile, 2)
            high_xt(NT - 1, 1, (NT - 1) * P)

        @block.tensor
        def _(pe):
            pe.wait_ge(ident_made, 2)

            def turn_x(t, b):
                pe.wait_ge(xn_ready, t + 1)
                after(pe, xt_split, t - 1)
                for k in range(KT):
                    last = pe.transpose(p_xt[b][:, k, :], xn[b][:, k * P:(k + 1) * P], ident[:])
                last.then_inc(xt_done, 1)

            def turn_a(t, b, before):
                pe.wait_ge(a_in[b], 32 * before + 32)
                after(pe, at_split, t - 1)
                for k in range(LORA):
                    last = pe.transpose(p_at[b][:, k, :], a_row[b][:, k * R:(k + 1) * R], ident[:])
                last.then_inc(at_done, 1)
            turn_a(0, 0, 0)
            pe.wait_ge(lb_split, 1)
            pe.wait_ge(lb_high, 1)

            def tile(i):
                for b in range(2):
                    t = 2 * i + b
                    if not last_tile(t):
                        turn_a(t + 1, 1 - b, i + b)
                    pe.wait_ge(at_split, t + 1)
                    for c in range(2):
                        after(pe, h_ready if c else half_ready, t)
                        n = slice(c * HALF, (c + 1) * HALF)
                        for k in range(LORA):
                            last = product3(pe, p_lora[:, n], at_h[b][:, k, :], at_l[b][:, k, :],
                                            lb_h[:, k, n], lb_l[:, k, n], k == 0, k == LORA - 1)
                        last.then_inc(lora_done, 1)
                    if b == 1:
                        turn_x(t - 1, 0)
                    elif not (isinstance(i, int) and i == 0):
                        turn_x(t - 1, 1)
            repeat(pe, NT // 2, tile, 2)
            turn_x(NT - 1, 1)


def phase_qkv(nc, a, xh, xl, ident):
    with ExitStack() as ctx:
        sb = lambda n, s, d=F32: ctx.enter_context(nc.sbuf_tensor(n, s, d))
        ps = lambda n, s: ctx.enter_context(nc.psum_tensor(n, s, F32))
        sem = lambda n: ctx.enter_context(nc.semaphore(n))
        NB = T // HALF
        TB = HALF // P
        w_raw = [sb(f"wq_raw{b}", [P, KT, P]) for b in range(3)]
        w_h = [sb(f"wq_h{b}", [P, KT, P], F32R) for b in range(3)]
        w_l = [sb(f"wq_l{b}", [P, KT, P], F32R) for b in range(3)]
        bias = sb("qkv_bias", [P, 3, KT])
        y = [sb(f"y{k}", [P, HALF]) for k in range(2)]
        y_h = [sb(f"y_h{k}", [P, HALF], F32R) for k in range(NB)]
        y_l = [sb(f"y_l{k}", [P, HALF], F32R) for k in range(NB)]
        v_out = [sb(f"v_out{k}", [P, P // HD, TB, VC], F32R) for k in range(2)]
        rows_raw = sb("rows_raw", [P, HALF])
        rows = sb("rows_r", [P, HALF], F32R)
        p_y = [ps(f"p_y{k}", [P, HALF]) for k in range(NB)]
        p_vt = [ps(f"p_vt{k}", [P, TB, P]) for k in range(2)]

        bias_in = sem("bias_in")
        w_in = [sem(f"wq_in{b}") for b in range(3)]
        w_high = sem("wq_high")
        w_split = sem("wq_split")
        y_done = sem("y_done")
        y_biased = sem("y_biased")
        y_high = sem("y_high")
        y_split = sem("y_split")
        vt_done = sem("vt_done")
        rows_in = sem("rows_in")
        rows_rounded = sem("rows_rounded")
        rows_stored = sem("rows_stored")
        v_ones = sem("v_ones")
        v_high = sem("v_high")
        v_ready = sem("v_ready")
        qk_stored = [sem(f"qk_stored{k}") for k in range(NB)]
        v_stored = [sem(f"v_stored{k}") for k in range(2)]
        block = ctx.enter_context(nc.Block())

        def staggered(eng, n, weights, results):
            weights(0, 0)

            def body(i):
                weights(i, 1)
                if not (isinstance(i, int) and i == 0):
                    results(i - 1, 2)
                results(i, 0)
                weights(i, 2)
                results(i, 1)
                if not (isinstance(i, int) and i == n - 1):
                    weights(i + 1, 0)
            repeat(eng, n, body, 2)
            results(n - 1, 2)

        @block.sync
        def _(sp):
            sp.dma_start(bias[:], a["b_qkv"]).then_inc(bias_in, 16)
            sp.dma_start(rows_raw[:], a["query_rows"]).then_inc(rows_in, 16)

            def store(i, b):
                for k in range(NB):
                    if b < 2:
                        sp.wait_ge(y_split, 2 * NB * i + NB * b + k + 1)
                        to = (bass.ds(i * P, P), slice(k * HALF, (k + 1) * HALF))
                        sp.dma_start(a[("qh", "kh")[b]][to], wide(y_h[k][:])).then_inc(qk_stored[k], 16)
                        sp.dma_start(a[("ql", "kl")[b]][to], wide(y_l[k][:])).then_inc(qk_stored[k], 16)
                    else:
                        sp.wait_ge(v_ready, NB * i + k + 1)
                        sp.dma_start(a["v_dram"][bass.ds(P // HD * i, P // HD), :, TB * k:TB * k + TB, :].rearrange("a p t d -> p a (t d)"),
                                     wide(v_out[k % 2][:]).rearrange("p a t d -> p a (t d)")).then_inc(v_stored[k % 2], 16)
            staggered(sp, KT, lambda i, b: None, store)
            sp.wait_ge(rows_rounded, 1)
            sp.dma_start(a["rows_dram"], wide(rows[:])).then_inc(rows_stored, 16)
            sp.wait_ge(rows_stored, 16)
            for k in range(NB):
                sp.wait_ge(qk_stored[k], 4 * 16 * KT)
            for k in range(2):
                sp.wait_ge(v_stored[k], 2 * 16 * KT)

        @block.gpsimd
        def _(pool):
            passed = nc.alloc_semaphore("passed_wq")

            def load(i, b):
                after_plainly(pool, passed, w_split, 3 * (i - 1) + b + 1)
                pool.dma_start(w_raw[b][:].rearrange("p k c -> p (k c)"),
                               a["w_qkv"][bass.ds(3 * i + b, 1)].rearrange("a p n -> (a p) n")).then_inc(w_in[b], 16)
            staggered(pool, KT, load, lambda i, b: None)

        @block.scalar
        def _(act):
            def weights(i, b):
                act.wait_ge(w_in[b], 16 * i + 16)
                after(act, y_done, NB * (3 * (i - 1) + b + 1))
                act.activation(w_h[b][:], w_raw[b][:], ACT.Copy).then_inc(w_high, 1)

            def results(i, b):
                for k in range(NB):
                    if b < 2:
                        act.wait_ge(y_biased, NB * (3 * i + b) + k + 1)
                        after(act, qk_stored[k], 32 * (2 * i + b))
                        act.activation(y_h[k][:], y[k % 2][:], ACT.Copy).then_inc(y_high, 1)
                    else:
                        act.wait_ge(vt_done, NB * i + k + 1)
                        after(act, v_stored[k % 2], 16 * (2 * i + k // 2))
                        act.activation(v_out[k % 2][:, :, :, 0:HD].rearrange("p a t d -> p t a d"), p_vt[k % 2][:].rearrange(
                            "p t (a d) -> p t a d", a=P // HD), ACT.Copy).then_inc(v_high, 1)
            staggered(act, KT, weights, results)

        @block.vector
        def _(dve):
            for k in range(2):
                dve.memset(wide(v_out[k][:, :, :, 2 * HD:VC]), 1.0).then_inc(v_ones, 1)
            dve.wait_ge(v_ones, 2)
            dve.wait_ge(rows_in, 16)
            dve.tensor_copy(rows[:], rows_raw[:]).then_inc(rows_rounded, 1)
            dve.wait_ge(bias_in, 16)

            def low_v(i, k):
                dve.wait_ge(v_high, NB * i + k + 1)
                dve.tensor_tensor(v_out[k % 2][:, :, :, HD:2 * HD].rearrange("p a t d -> p t a d"),
                                  p_vt[k % 2][:].rearrange("p t (a d) -> p t a d", a=P // HD),
                                  wide(v_out[k % 2][:, :, :, 0:HD].rearrange("p a t d -> p t a d")), ALU.subtract).then_inc(v_ready, 1)

            def weights(i, b):
                dve.wait_ge(w_high, 3 * i + b + 1)
                dve.tensor_tensor(w_l[b][:], w_raw[b][:], wide(w_h[b][:]), ALU.subtract).then_inc(w_split, 1)

            def results(i, b):
                for k in range(NB):
                    at = NB * (3 * i + b) + k
                    dve.wait_ge(y_done, at + 1)
                    if b == 2 and k >= 2:
                        dve.wait_ge(vt_done, NB * i + k - 1)
                    elif b == 0 and k < 2:
                        after(dve, vt_done, NB * (i - 1) + k + 3)
                    else:
                        dve.wait_ge(y_split, 2 * NB * i + NB * b + k - 1)
                    dve.tensor_scalar(y[k % 2][:], p_y[k][:], bias[:, b, bass.ds(i, 1)], ATT_SCALE if b == 0 else 1.0,
                                      ALU.add, ALU.mult).then_inc(y_biased, 1)
                    if b < 2:
                        dve.wait_ge(y_high, 2 * NB * i + NB * b + k + 1)
                        dve.tensor_tensor(y_l[k][:], y[k % 2][:], wide(y_h[k][:]), ALU.subtract).then_inc(y_split, 1)
                    elif k:
                        low_v(i, k - 1)
                if b == 2:
                    low_v(i, NB - 1)
            staggered(dve, KT, weights, results)

        @block.tensor
        def _(pe):
            def turn_v(i, k):
                pe.wait_ge(y_biased, NB * (3 * i + 2) + k + 1)
                after(pe, v_ready, NB * i + k - 1)
                for t in range(TB):
                    last = pe.transpose(p_vt[k % 2][:, t, :], y[k % 2][:, t * P:(t + 1) * P], ident[:])
                last.then_inc(vt_done, 1)

            def cols(i):
                for b in range(3):
                    g = 3 * i + b
                    pe.wait_ge(w_split, g + 1)
                    for k in range(NB):
                        after(pe, y_biased, NB * (g - 1) + k + 1)
                        n = slice(k * HALF, (k + 1) * HALF)
                        for c in range(KT):
                            last = product3(pe, p_y[k][:], w_h[b][:, c, :], w_l[b][:, c, :], xh[:, c, n], xl[:, c, n],
                                            c == 0, c == KT - 1)
                        last.then_inc(y_done, 1)
                        if b == 0 and not (isinstance(i, int) and i == 0):
                            turn_v(i - 1, k)
            repeat(pe, KT, cols, 2)
            for k in range(NB):
                turn_v(KT - 1, k)


class HeadPlan:

    LAG = 6
    RAW = 8
    RING = 10

    def __init__(self):
        self.groups = list(range(NG - 1, -1, -1))
        self.slots = [(u, g, k) for u, g in enumerate(self.groups) for k in range(QG * g + QG)]
        n = len(self.slots)
        self.ends = [max(i for i, x in enumerate(self.slots) if x[0] == u) for u in range(NG)]
        ahead = []
        for u, g in enumerate(self.groups):
            own = [("score", u, q, c) for q in range(QG - 1, -1, -1) for c in range(0, P * (QG * g + q + 1), CHUNK)]
            if u:
                own.insert(2, ("shift", u - 1))
            ahead += own
        ahead.append(("shift", NG - 1))
        self.ahead = ahead
        scores = [x for x in ahead if x[0] == "score"]
        cost = [min(CHUNK, self.width(x) - x[3]) // P for x in scores]
        timed = [(sum(cost[:i]) * (n - 2) // sum(cost), x) for i, x in enumerate(scores)]
        self.last_piece = [max(t for t, x in timed if x[1] == u) for u in range(NG)]
        for u in range(NG):
            timed.append((min(self.last_piece[u] + 3, n - 1) + 0.1, ("shift", u)))
            at = self.ends[u] + self.LAG + 2
            timed.append((at % n + 0.5, ("output", u, at // n)))
        assert max(self.last_piece) <= n - 3
        self.items = [(int(t), x) for t, x in sorted(timed, key=lambda y: y[0])]
        self.high = ["A" if i % 2 else "D" for i in range(n)]
        self.low = ["D" if i in (4, 9, 17, 21, 30) else "P" for i in range(n)]

    def width(self, x):
        return P * (QG * self.groups[x[1]] + x[2] + 1)

    def present(self, h):
        first, last = isinstance(h, int) and h == 0, isinstance(h, int) and h == H - 1
        return [(t, x) for t, x in self.items
                if not (first and x[0] == "output" and x[2]) and not (last and x[0] != "output")]

    def period(self, h):
        late = sum(1 for _, x in self.items if x[0] == "output" and x[2])
        own = [(0, x) for x in self.ahead] if isinstance(h, int) and h == -1 else self.present(h)
        n = d = 0
        if not isinstance(h, int) or h >= 0:
            n, d = len(self.ahead), len(self.ahead) - NG
        if not isinstance(h, int) or h > 0:
            n, d = n + len(self.items) * h - late, d + (len(self.items) - NG) * h - late
        out, taken = [], 0
        for i, (t, x) in enumerate(own):
            out.append((t, x, n + i, d + taken))
            taken += x[0] != "shift"
        return out

    def buffer(self, h, i):
        late = sum(1 for _, x in self.items if x[0] == "output" and x[2])
        if isinstance(h, int) and h <= 0:
            return (i + (len(self.ahead) if h == 0 else 0)) % 2
        return (len(self.ahead) - late + i) % 2


def back(h, s, by, n):
    return (h, s - by) if s >= by else (h - 1, s - by + n)


def phase_attention(nc, a, o, ident):
    plan = HeadPlan()
    N = len(plan.slots)
    NI = len(plan.items)
    assert NI % 2 == 0 and N % plan.RING == 0 and N % plan.RAW == 0 and N % 2 == 0 and NG % 2 == 0 and len(plan.ahead) % 2 == 0
    BF16 = mybir.dt.bfloat16
    ROWS = 3 * HD
    OC = 80
    MID = HALF // 2
    DELTAS = NT
    with ExitStack() as ctx:
        sb = lambda n, s, d=F32: ctx.enter_context(nc.sbuf_tensor(n, s, d))
        ps = lambda n, s: ctx.enter_context(nc.psum_tensor(n, s, F32))
        sem = lambda n: ctx.enter_context(nc.semaphore(n))
        slopes = sb("slopes", [P, H])
        key_rows = sb("key_rows", [P, T])
        pos = sb("pos", [P, DELTAS + NG])
        spos = [sb(f"spos{b}", [P, DELTAS + NG]) for b in range(3)]
        ident_b = sb("ident_b", [P, P], BF16)
        mask_b = sb("mask_b", [P, P], BF16)
        qs = [sb(f"qs{b}", [P, T], F32R) for b in range(3)]
        ks = [sb(f"ks{b}", [P, T], F32R) for b in range(3)]
        vs = [sb(f"vs{b}", [P, NT, VC], F32R) for b in range(3)]
        top = sb("top", [P, NG, QG, 2])
        peak = sb("peak1", [P, NG, QG])
        w = sb("w", [P, NG, QG])
        w_hl = sb("w_hl", [P, NG, QG, 2], F32R)
        pt = [sb(f"pt{k}", [P, HALF]) for k in range(plan.RAW)]
        pt_h = [sb(f"pt_h{k}", [P, HALF], F32R) for k in range(plan.RING)]
        pt_l = [sb(f"pt_l{k}", [P, HALF], F32R) for k in range(plan.RING)]
        ot = [sb(f"ot{k}", [VC, HALF]) for k in range(2)]
        share = sb("share", [P, QG])
        osum = sb("osum", [P, QG, HD])
        p_s = [ps(f"p_s{k}", [P, CHUNK]) for k in range(2)]
        p_t = [ps(f"p_t{k}", [P, HALF]) for k in range(2)]
        p_o = [ps(f"p_o{k}", [P, HALF]) for k in range(2)]

        slopes_in = sem("slopes_in")
        tables_made = sem("tables_made")
        table_step = sem("table_step")
        stack_in = [sem(f"stack_in{b}") for b in range(3)]
        v_in = [sem(f"v_in{b}") for b in range(3)]
        spos_made = sem("spos_made")
        key_rows_in = sem("key_rows_in")
        key_rows_made = sem("key_rows_made")
        item_done = sem("item_done")
        item_used = sem("item_used")
        shift_used = sem("shift_used")
        osum_made = sem("osum_made")
        w_step = sem("w_step")
        w_made = sem("w_made")
        st_done = sem("st_done")
        exp_done = sem("exp_done")
        high_a = sem("high_a")
        high_d = sem("high_d")
        low_p = sem("low_p")
        low_d = sem("low_d")
        pv_done = sem("pv_done")
        ot_copied = sem("ot_copied")
        o_made = sem("o_made")
        block = ctx.enter_context(nc.Block())

        def heads(eng, body):
            for h in range(2):
                body(h, h % 3)
            with eng.Fori(0, (H - 5) // 3) as i:
                for b in range(3):
                    body(i * 3 + (2 + b), (2 + b) % 3)
            for h in range(H - 3, H):
                body(h, h % 3)

        def count(kinds, kind, h, s):
            return kinds.count(kind) * h + kinds[:s + 1].count(kind)

        def high_ready(eng, h, s):
            eng_high = {"A": high_a, "D": high_d}[plan.high[s]]
            after(eng, eng_high, count(plan.high, plan.high[s], h, s))

        def low_ready(eng, h, s):
            eng_low = {"P": low_p, "D": low_d}[plan.low[s]]
            after(eng, eng_low, count(plan.low, plan.low[s], h, s))

        def exists(h):
            return not isinstance(h, int) or h >= 0

        def masked_columns(g, k):
            return P * max(0, k - QG * g)

        @block.sync
        def _(sp):
            sp.dma_start(slopes[:], a["slopes"]).then_inc(slopes_in, 16)
            sp.dma_start(key_rows[ROWS:ROWS + 4, :], a["key_rows"]).then_inc(key_rows_in, 16)

            passed = nc.alloc_semaphore("passed_sp")

            def load(h, b):
                row = bass.ds(h * HD, HD)
                for n, (q, k) in enumerate((("qh", "kh"), ("ql", "kh"), ("qh", "kl"))):
                    sp.dma_start(wide(qs[b][n * HD:(n + 1) * HD, :]), a[q][row, :]).then_inc(stack_in[b], 16)
                    sp.dma_start(wide(ks[b][n * HD:(n + 1) * HD, :]), a[k][row, :]).then_inc(stack_in[b], 16)
                sp.dma_start(wide(qs[b][ROWS:ROWS + 4, :]).rearrange("r (g t) -> r g t", g=NG),
                             a["rows_dram"][bass.ds(h * 4, 4), :].unsqueeze(1).to_broadcast([4, NG, HALF])).then_inc(stack_in[b], 48)
                sp.dma_start(wide(vs[b][:]).rearrange("p t d -> p (t d)"),
                             a["v_dram"][bass.ds(h, 1)].rearrange("a p t d -> (a p) (t d)")).then_inc(v_in[b], 48)
            load(0, 0)
            load(1, 1)

            def period(h, b):
                if isinstance(h, int) and h + 2 >= H:
                    return
                after_plainly(sp, passed, st_done, N * h)
                after_plainly(sp, passed, pv_done, N * h)
                load(h + 2, (b + 2) % 3)
            heads(sp, period)

        @block.gpsimd
        def _(pool):
            step = Chain(pool, table_step)
            step.link(pool.iota(pos[:, 0:DELTAS], pattern=[[P, DELTAS]], base=-(DELTAS - QG) * P - MID, channel_multiplier=1,
                                allow_small_or_imprecise_dtypes=True))
            step.link(pool.iota(pos[:, DELTAS:], pattern=[[HALF, NG]], base=MID, channel_multiplier=0,
                                allow_small_or_imprecise_dtypes=True))
            step.link(pool.tensor_copy(ident_b[:], ident[:]))
            step.link(pool.memset(mask_b[:], 0.0))
            step.link(pool.affine_select(out=mask_b[:], in_=mask_b[:], compare_op=ALU.is_ge, fill=MASKED, base=0,
                                         pattern=[[1, P]], channel_multiplier=-1))
            pool.sem_inc(tables_made, 1)

            def period(h, _):
                for s in range(N):
                    if plan.low[s] != "P":
                        continue
                    u, g, k = plan.slots[s]
                    c = masked_columns(g, k)
                    r = s % plan.RING
                    after(pool, exp_done, N * h + s + 1)
                    high_ready(pool, h, s)
                    before = back(h, s, plan.RING, N)
                    after(pool, pv_done, N * before[0] + before[1] + 1)
                    pool.tensor_tensor(pt_l[r][:, c:], pt[s % plan.RAW][:, c:], wide(pt_h[r][:, c:]), ALU.subtract).then_inc(low_p, 1)
            heads(pool, period)

        @block.vector
        def _(dve):
            dve.wait_ge(slopes_in, 16)
            dve.wait_ge(tables_made, 1)

            def tables(h, b):
                after(dve, exp_done, N * (h - 2))
                after(dve, w_made, NG * (h - 2))
                dve.tensor_scalar(spos[b][:], pos[:], slopes[:, bass.ds(h, 1)], None, ALU.mult).then_inc(spos_made, 1)

            def score(x, n, d, buf):
                _, u, q, c = x
                width = min(CHUNK, plan.width(x) - c)
                dve.wait_ge(item_done, n + 1)
                dve.tensor_reduce(top[:, u, q, c // CHUNK:c // CHUNK + 1], p_s[buf][:, 0:width], AX_X, ALU.max).then_inc(item_used, 1)

            def output(x, n, d, buf):
                got = p_s[buf][:, 0:QG * OC].rearrange("p (q c) -> p q c", q=QG)
                dve.wait_ge(item_done, n + 1)
                dve.reciprocal(share[:], got[:, :, 2 * HD]).then_inc(osum_made, 1)
                dve.tensor_reduce(osum[:], got[:, :, 0:2 * HD].rearrange("p q (a d) -> p q d a", a=2), AX_X, ALU.add).then_inc(item_used, 1)

            def share_out(h, x, d):
                g = plan.groups[x[1]]
                dve.wait_ge(item_used, d + 1)
                dve.wait_ge(osum_made, NG * h + x[1] + 1)
                dve.tensor_tensor(o[:, QG * g:QG * g + QG, bass.ds(h * HD, HD)], osum[:],
                                  share[:].unsqueeze(2).to_broadcast([P, QG, HD]), ALU.mult).then_inc(o_made, 1)

            def item(h, x, n, d, buf):
                if x[0] == "score":
                    score(x, n, d, buf)
                elif x[0] == "output":
                    after(dve, o_made, NG * (h - x[2]) + x[1])
                    output(x, n, d, buf)

            WIDE = sum(1 for g in plan.groups if g >= NG // 2)
            assert plan.groups[:WIDE] == [g for g in plan.groups if g >= NG // 2]

            def steps(h, u):
                return (2 * NG + WIDE) * h + 2 * u + min(u, WIDE)

            def peak_of(h, u, d):
                if u < WIDE:
                    dve.wait_ge(item_used, d + 1)
                    dve.tensor_reduce(peak[:, u, :], top[:, u, :, :], AX_X, ALU.max).then_inc(w_step, 1)

            def w_of(h, b, u, d):
                mid = spos[b][:, DELTAS + plan.groups[u]:DELTAS + plan.groups[u] + 1]
                m = peak[:, u, :] if u < WIDE else top[:, u, :, 0]
                if u == 0:
                    dve.wait_ge(spos_made, h + 1)
                if u < WIDE:
                    dve.wait_ge(w_step, steps(h, u) + 1)
                else:
                    dve.wait_ge(item_used, d + 1)
                dve.tensor_scalar(w[:, u, :], m, -1.0, mid, ALU.mult, ALU.add).then_inc(w_step, 1)
                dve.tensor_scalar(w_hl[:, u, :, 0], m, -1.0, mid, ALU.mult, ALU.add).then_inc(w_step, 1)
                dve.wait_ge(w_step, steps(h, u + 1))
                dve.tensor_tensor(w_hl[:, u, :, 1], w[:, u, :], wide(w_hl[:, u, :, 0]), ALU.subtract).then_inc(w_made, 1)

            def last_piece(items, u):
                return [d for _, x, _, d in items if x[0] == "score" and x[1] == u][-1]

            def part(h, s):
                if not exists(h):
                    return
                u, g, k = plan.slots[s]
                c = masked_columns(g, k)
                r = s % plan.RING
                before = back(h, s, plan.RING, N)
                if plan.high[s] == "D" or plan.low[s] == "D":
                    dve.wait_ge(exp_done, N * h + s + 1)
                    after(dve, pv_done, N * before[0] + before[1] + 1)
                if plan.high[s] == "D":
                    dve.tensor_copy(pt_h[r][:, c:], pt[s % plan.RAW][:, c:]).then_inc(high_d, 1)
                if plan.low[s] == "D":
                    high_ready(dve, h, s)
                    dve.tensor_tensor(pt_l[r][:, c:], pt[s % plan.RAW][:, c:], wide(pt_h[r][:, c:]), ALU.subtract).then_inc(low_d, 1)

            dve.wait_ge(key_rows_in, 16)
            for b in range(3):
                dve.tensor_copy(ks[b][ROWS:ROWS + 4, :], key_rows[ROWS:ROWS + 4, :]).then_inc(key_rows_made, 1)
            tables(0, 0)
            first = plan.period(-1)
            for _, x, n, d in first:
                item(-1, x, n, d, n % 2)
                if x[0] == "score" and d == last_piece(first, x[1]):
                    peak_of(0, x[1], d)
                    w_of(0, 0, x[1], d)

            def period(h, b):
                more = not (isinstance(h, int) and h == H - 1)
                if more:
                    tables(h + 1, (b + 1) % 3)
                items = plan.period(h)
                for s in range(N):
                    for i, (t, x, n, d) in enumerate(items):
                        if t == s:
                            item(h, x, n, d, plan.buffer(h, i))
                    part(*back(h, s, 1, N))
                    for t, x, n, d in items:
                        if t == s and x[0] == "output":
                            share_out(h - x[2], x, d)
                    for u in range(NG):
                        if more and plan.last_piece[u] == s:
                            peak_of(h + 1, u, last_piece(items, u))
                        if more and plan.last_piece[u] == s - 1:
                            w_of(h + 1, (b + 1) % 3, u, last_piece(items, u))
            heads(dve, period)
            part(H - 1, N - 1)
            for i, (x, n, d) in enumerate(tail(plan)):
                dve.wait_ge(o_made, NG * (H - 1) + x[1])
                output(x, n, d, plan.buffer(H - 1, len(plan.present(H - 1)) + i))
                share_out(H - 1, x, d)

        @block.scalar
        def _(act):
            def exponentials(h, b, s):
                u, g, k = plan.slots[s]
                c = masked_columns(g, k)
                if s == 0:
                    act.wait_ge(spos_made, h + 1)
                before = back(h, s, plan.RAW, N)
                if exists(before[0]):
                    low_ready(act, *before)
                at = k - QG * g + DELTAS - QG
                act.wait_ge(st_done, N * h + s + 1)
                act.activation(pt[s % plan.RAW][:, c:], p_t[s % 2][:, c:], ACT.Exp, bias=spos[b][:, at:at + 1]).then_inc(exp_done, 1)

            def high(h, s):
                if not exists(h) or plan.high[s] != "A":
                    return
                u, g, k = plan.slots[s]
                c = masked_columns(g, k)
                r = s % plan.RING
                before = back(h, s, plan.RING, N)
                after(act, pv_done, N * before[0] + before[1] + 1)
                act.wait_ge(exp_done, N * h + s + 1)
                act.activation(pt_h[r][:, c:], pt[s % plan.RAW][:, c:], ACT.Copy).then_inc(high_a, 1)

            def copy_out(h, u):
                if not exists(h):
                    return
                act.wait_ge(pv_done, N * h + plan.ends[u] + 1)
                after(act, o_made, NG * h + u - 1)
                act.activation(ot[u % 2][:], p_o[u % 2][0:VC, :], ACT.Copy).then_inc(ot_copied, 1)

            def shift(h, b, x, n, buf):
                g = plan.groups[x[1]]
                act.wait_ge(item_done, n + 1)
                act.activation(qs[b][ROWS:ROWS + 2, g * HALF:(g + 1) * HALF], p_s[buf][0:2, 0:HALF], ACT.Copy).then_inc(shift_used, 1)

            for _, x, n, _ in plan.period(-1):
                if x[0] == "shift":
                    shift(0, 0, x, n, n % 2)

            def period(h, b):
                items = plan.period(h)
                for s in range(N):
                    exponentials(h, b, s)
                    high(*back(h, s, 1, N))
                    for i, (t, x, n, _) in enumerate(items):
                        if t == s and x[0] == "shift":
                            shift(h + 1, (b + 1) % 3, x, n, plan.buffer(h, i))
                    for u in range(NG):
                        at = plan.ends[u] + plan.LAG
                        if at % N == s:
                            copy_out(h - at // N, u)
            heads(act, period)
            high(H - 1, N - 1)
            for u in range(NG):
                if plan.ends[u] + plan.LAG >= N:
                    copy_out(H - 1, u)

        @block.tensor
        def _(pe):
            passed = nc.alloc_semaphore("passed_pe")
            pe.wait_ge(tables_made, 1)

            def score(h, b, x, buf):
                _, u, q, c0 = x
                end = min(c0 + CHUNK, plan.width(x))
                base = plan.width(x) - P
                if x == plan.ahead[0]:
                    pe.wait_ge(stack_in[b], (h - b) * 48 + 144)
                for c in range(c0, end, HALF):
                    n = min(HALF, end - c)
                    last = pe.matmul(p_s[buf][:, c - c0:c - c0 + n], qs[b][0:ROWS + 4, base:base + P], ks[b][0:ROWS + 4, c:c + n],
                                     start=True, stop=(c + n <= base))
                if end > base:
                    last = pe.matmul(p_s[buf][:, base - c0:base - c0 + P], mask_b[:], ident_b[:], start=False, stop=True)
                return last

            def turn_shift(h, x, buf):
                u = x[1]
                pe.wait_ge(w_made, NG * h + u + 1)
                for q in range(QG):
                    last = pe.transpose(p_s[buf][0:2, q * P:(q + 1) * P], wide(w_hl[:, u, q, :]), ident[:])
                return last

            def turn_out(h, x, buf):
                u = x[1]
                after_plainly(pe, passed, ot_copied, NG * h + u + 1)
                for q in range(QG):
                    last = pe.transpose(p_s[buf][:, q * OC:q * OC + VC], ot[u % 2][:, q * P:(q + 1) * P], ident[0:VC, 0:VC])
                return last

            def free(x, d, h):
                if x[0] == "shift":
                    pe.wait_ge(shift_used, NG * (h + 1) + x[1] + 1)
                else:
                    pe.wait_ge(item_used, d + 1)

            def item(h, b, i, x, n, buf):
                if i >= 2:
                    free(plan.period(h)[i - 2][1], plan.period(h)[i - 2][3], h)
                elif exists(h):
                    free(plan.period(h - 1)[i - 2][1], plan.period(h - 1)[i - 2][3], h - 1)
                if x[0] == "score":
                    last = score(h + 1, (b + 1) % 3, x, buf)
                elif x[0] == "shift":
                    last = turn_shift(h + 1, x, buf)
                else:
                    last = turn_out(h - x[2], x, buf)
                last.then_inc(item_done, 1)

            def key_scores(h, b, s):
                u, g, k = plan.slots[s]
                c = masked_columns(g, k)
                if k == 0:
                    pe.wait_ge(shift_used, NG * h + u + 1)
                before = back(h, s, 2, N)
                if exists(before[0]):
                    after(pe, exp_done, N * before[0] + before[1] + 1)
                last = pe.matmul(p_t[s % 2][:, c:], ks[b][0:ROWS + 2, k * P:(k + 1) * P],
                                 qs[b][0:ROWS + 2, g * HALF + c:(g + 1) * HALF], start=True, stop=(k < QG * g))
                if k >= QG * g:
                    last = pe.matmul(p_t[s % 2][:, c:c + P], ident_b[:], mask_b[:], start=False, stop=True)
                last.then_inc(st_done, 1)

            def weigh(h, b, s):
                if not exists(h):
                    return
                u, g, k = plan.slots[s]
                c = masked_columns(g, k)
                r = s % plan.RING
                if s == 0:
                    pe.wait_ge(v_in[b], (h - b) * 16 + 48)
                if k == 0:
                    after(pe, ot_copied, NG * h + u - 1)
                high_ready(pe, h, s)
                pe.matmul(p_o[u % 2][0:VC, c:], vs[b][:, k, :], pt_h[r][:, c:], start=(k == 0), stop=False)
                low_ready(pe, h, s)
                pe.matmul(p_o[u % 2][0:VC, c:], vs[b][:, k, :], pt_l[r][:, c:], start=False, stop=(k == QG * g + QG - 1)
                          ).then_inc(pv_done, 1)

            pe.wait_ge(key_rows_made, 3)
            for i, (_, x, n, _) in enumerate(plan.period(-1)):
                item(-1, 2, i, x, n, n % 2)

            def period(h, b):
                items = plan.period(h)
                for s in range(N):
                    key_scores(h, b, s)
                    for i, (t, x, n, _) in enumerate(items):
                        if t == s:
                            item(h, b, i, x, n, plan.buffer(h, i))
                    weigh(back(h, s, plan.LAG, N)[0], b if s >= plan.LAG else (b + 2) % 3, back(h, s, plan.LAG, N)[1])
            heads(pe, period)
            for s in range(N - plan.LAG, N):
                weigh(H - 1, (H - 1) % 3, s)
            for i, (x, n, d) in enumerate(tail(plan)):
                held = (plan.period(H - 1) + [(0, *y) for y in tail(plan)])[len(plan.period(H - 1)) + i - 2]
                free(held[1], held[3], H - 1)
                turn_out(H - 1, x, plan.buffer(H - 1, len(plan.present(H - 1)) + i)).then_inc(item_done, 1)


def tail(plan):
    _, _, n, d = plan.period(H - 1)[-1]
    late = [x for _, x in plan.items if x[0] == "output" and x[2]]
    return [(("output", x[1], 0), n + 1 + i, d + 1 + i) for i, x in enumerate(late)]


def root_of_variance(dve, ln, act_root_ready, count, sd, rstd):
    dve.wait_ge(act_root_ready, count)
    ln.link(dve.reciprocal(sd[:, 2:3], sd[:, 1:2]))
    ln.link(dve.scalar_tensor_tensor(out=sd[:, 3:4], in0=sd[:, 2:3], scalar=sd[:, 0:1], in1=sd[:, 1:2],
                                     op0=ALU.mult, op1=ALU.add))
    return dve.reciprocal(rstd, sd[:, 3:4])


def phase_project(nc, a, o, norm, ident):
    with ExitStack() as ctx:
        sb = lambda n, s, d=F32: ctx.enter_context(nc.sbuf_tensor(n, s, d))
        ps = lambda n, s: ctx.enter_context(nc.psum_tensor(n, s, F32))
        sem = lambda n: ctx.enter_context(nc.semaphore(n))
        w_raw = [sb(f"wp_raw{k}", [P, D]) for k in range(WB)]
        w_h = sb("wp_h", [P, KT, D], F32R)
        w_l = sb("wp_l", [P, KT, D], F32R)
        bias = sb("p_bias", [P, D])
        h_in = [sb(f"h_in{b}", [P, D]) for b in range(2)]
        o_now = [sb(f"o_now{b}", [P, D]) for b in range(2)]
        a_h = [sb(f"a_h{b}", [P, KT, P], F32R) for b in range(2)]
        a_l = [sb(f"a_l{b}", [P, KT, P], F32R) for b in range(2)]
        stats = sb("stats2", [P, 2, 6])
        mv = sb("mv2", [P, 2])
        sd = sb("sd2", [P, 4])
        p_x = ps("p_x2", [P, KT, P])
        p_e = [ps(f"p_e{b}", [P, D]) for b in range(2)]

        bias_in = sem("p_bias_in")
        w_in = [sem(f"wp_in{k}") for k in range(WB)]
        w_high = sem("wp_high")
        w_split = sem("wp_split")
        h_loaded = [sem(f"h_loaded{b}") for b in range(2)]
        h_biased = sem("h_biased")
        o_copied = sem("o_copied")
        at_done = sem("at2_done")
        at_high = sem("at2_high")
        at_split = sem("at2_split")
        e_done = sem("e_done")
        h2_ready = sem("h2_ready")
        var_ready = sem("var2_ready")
        root_ready = sem("root2_ready")
        norm_ready = sem("norm_ready")
        ln_step = sem("ln2_step")
        block = ctx.enter_context(nc.Block())

        @block.sync
        def _(sp):
            for k in range(KT):
                after(sp, w_split, k - WB + 1)
                if k == 2:
                    sp.dma_start(bias[:], a["b_proj"].to_broadcast([P, D])).then_inc(bias_in, 16)
                sp.dma_start(w_raw[k % WB][:], a["w_proj"][k * P:(k + 1) * P, :]).then_inc(w_in[k % WB], 16)

            def tile(i):
                for b in range(2):
                    t = 2 * i + b
                    after(sp, h2_ready, t - 1)
                    sp.dma_start(h_in[b][:], a["h_dram"][bass.ds(t, 1)].rearrange("a p d -> (a p) d")).then_inc(h_loaded[b], 16)
            repeat(sp, NT // 2, tile)

        @block.gpsimd
        def _(pool):
            def copy(t, b):
                after(pool, at_done, t - 1)
                pool.tensor_copy(o_now[b][:], o[:, bass.ds(t, 1), :].rearrange("p a d -> p (a d)")).then_inc(o_copied, 1)
            copy(0, 0)
            pool.wait_ge(bias_in, 16)

            def tile(i):
                for b in range(2):
                    t = 2 * i + b
                    if not (isinstance(i, int) and t == NT - 1):
                        copy(t + 1, 1 - b)
                    pool.wait_ge(h_loaded[b], 16 * i + 16)
                    pool.tensor_tensor(h_in[b][:], h_in[b][:], bias[:], ALU.add).then_inc(h_biased, 1)
            repeat(pool, NT // 2, tile)

        @block.scalar
        def _(act):
            def high(t, b):
                act.wait_ge(at_done, t + 1)
                after(act, e_done, t - 1)
                act.activation(a_h[b][:], p_x[:], ACT.Copy).then_inc(at_high, 1)
            for k in range(KT):
                act.wait_ge(w_in[k % WB], 16 * (k // WB + 1))
                act.activation(w_h[:, k, :], w_raw[k % WB][:], ACT.Copy).then_inc(w_high, 1)
                if k == 0:
                    high(0, 0)

            def tile(i):
                for b in range(2):
                    t = 2 * i + b
                    if not (isinstance(i, int) and t == NT - 1):
                        high(t + 1, 1 - b)
                    act.wait_ge(var_ready, t + 1)
                    act.activation(sd[:, 1:2], sd[:, 0:1], ACT.Sqrt).then_inc(root_ready, 1)
            repeat(act, NT // 2, tile)

        @block.vector
        def _(dve):
            passed = nc.alloc_semaphore("passed6")
            ln = Chain(dve, ln_step, passed)

            def low(t, b):
                dve.wait_ge(at_high, t + 1)
                dve.tensor_tensor(a_l[b][:], p_x[:], wide(a_h[b][:]), ALU.subtract).then_inc(at_split, 1)
            for k in range(KT):
                dve.wait_ge(w_high, k + 1)
                dve.tensor_tensor(w_l[:, k, :], w_raw[k % WB][:], wide(w_h[:, k, :]), ALU.subtract).then_inc(w_split, 1)
                if k == 0:
                    low(0, 0)

            def tile(i):
                ln.begin(i)
                for b in range(2):
                    t = 2 * i + b
                    if not (isinstance(i, int) and t == NT - 1):
                        low(t + 1, 1 - b)
                    dve.wait_ge(h_biased, t + 1)
                    dve.wait_ge(e_done, t + 1)
                    dve.wait_ge(o_copied, t + 1)
                    dve.tensor_tensor(o[:, bass.ds(t, 1), :].rearrange("p a d -> p (a d)"), p_e[b][:], h_in[b][:], ALU.add
                                      ).then_inc(h2_ready, 1)
                    after_plainly(dve, passed, h2_ready, t + 1)
                    for k in range(2):
                        ins = dve.bn_stats(stats[:, k, :], o[:, bass.ds(t, 1), k * HALF:(k + 1) * HALF].rearrange("p a d -> p (a d)"))
                    ln.link(ins, plainly=True)
                    ln.link(dve.bn_aggr(mv[:], stats[:]))
                    dve.tensor_copy(norm[:, bass.ds(t, 1), 0:1].rearrange("p a k -> p (a k)"), mv[:, 0:1])
                    dve.tensor_scalar(sd[:, 0:1], mv[:, 1:2], EPS, 0.25, ALU.add, ALU.mult).then_inc(var_ready, 1)
                    root_of_variance(dve, ln, root_ready, t + 1, sd, norm[:, bass.ds(t, 1), 1:2].rearrange("p a k -> p (a k)")
                                     ).then_inc(norm_ready, 1)
            repeat(dve, NT // 2, tile)

        @block.tensor
        def _(pe):
            def turn(t, b):
                pe.wait_ge(o_copied, t + 1)
                after(pe, at_split, t)
                for k in range(KT):
                    last = pe.transpose(p_x[:, k, :], o_now[b][:, k * P:(k + 1) * P], ident[:])
                last.then_inc(at_done, 1)
            turn(0, 0)

            def tile(i):
                for b in range(2):
                    t = 2 * i + b
                    pe.wait_ge(at_split, t + 1)
                    after(pe, h2_ready, t - 1)
                    for c in range(2):
                        n = slice(c * HALF, (c + 1) * HALF)
                        for k in range(KT):
                            if isinstance(t, int) and t == 0 and c == 0:
                                pe.wait_ge(w_split, k + 1)
                            last = product3(pe, p_e[b][:, n], a_h[b][:, k, :], a_l[b][:, k, :], w_h[:, k, n], w_l[:, k, n],
                                            k == 0, k == KT - 1)
                        if c == 0 and not (isinstance(i, int) and t == NT - 1):
                            turn(t + 1, 1 - b)
                    last.then_inc(e_done, 1)
            repeat(pe, NT // 2, tile)


def phase_ffn(nc, a, o, norm, ident):
    with ExitStack() as ctx:
        sb = lambda n, s, d=F32: ctx.enter_context(nc.sbuf_tensor(n, s, d))
        ps = lambda n, s: ctx.enter_context(nc.psum_tensor(n, s, F32))
        sem = lambda n: ctx.enter_context(nc.semaphore(n))
        RAW = KT * ZW
        w_raw = [sb(f"wf_raw{k}", [P, RAW]) for k in range(WB)]
        w_h = sb("wf_h", [P, KT, D], F32R)
        w_l = sb("wf_l", [P, KT, D], F32R)
        z_hl = sb("wz_hl", [P, KT, 2, ZW], F32R)
        l_h = sb("wl_h", [P, D], F32R)
        l_l = sb("wl_l", [P, D], F32R)
        weights = ([(a["w_z"], RAW, z_hl[:, :, 0, :], z_hl[:, :, 1, :])]
                   + [(a["w_base"][k * P:(k + 1) * P, :], D, w_h[:, k, :], w_l[:, k, :]) for k in range(KT)]
                   + [(a["w_lora"], D, l_h[:], l_l[:])])
        bias = sb("f_bias", [P, D])
        r_bias = sb("r_bias", [P, NR])
        emap = sb("emap", [P, NR], I32)
        emap_f = sb("emap_f", [P, NR])
        onehot = sb("onehot", [P, E, NR])
        norm_now = [sb(f"norm_now{b}", [P, 2]) for b in range(2)]
        xn = sb("xn2", [P, D])
        x_h = [sb(f"x2_h{b}", [P, KT, P], F32R) for b in range(2)]
        x_l = [sb(f"x2_l{b}", [P, KT, P], F32R) for b in range(2)]
        rest = [sb(f"rest{b}", [P, D]) for b in range(2)]
        out = [sb(f"out{b}", [P, D]) for b in range(2)]
        z_half = sb("z_half", [P, ZW])
        z = sb("z", [P, ZW])
        logit = sb("logit", [P, NR])
        peak = sb("peak", [P, 2])
        ex = sb("ex", [P, NR])
        ex_sum = sb("ex_sum", [P, 2])
        prob = sb("prob", [P, NR])
        top8 = sb("top8", [P, 8])
        unchosen = sb("unchosen", [P, NR])
        spread = sb("spread", [P, E, NR])
        gate = sb("gate", [P, E])
        hw = sb("hw", [P, ER])
        hwt_h = sb("hwt_h", [P, P], F32R)
        hwt_l = sb("hwt_l", [P, P], F32R)
        p_x = ps("p_x3", [P, KT, P])
        p_e = [ps(f"p_f{b}", [P, D]) for b in range(2)]
        p_z = ps("p_z", [P, HALF])
        p_hw = ps("p_hw", [P, HALF])

        small_in = sem("small_in")
        bias_in = sem("f_bias_in")
        w_in = [sem(f"wf_in{k}") for k in range(WB)]
        w_high = sem("wf_high")
        w_split = sem("wf_split")
        map_step = sem("map_step")
        norm_got = sem("norm_got")
        rest_ready = sem("rest_ready")
        xn_ready = sem("xn3_ready")
        xt_done = sem("xt3_done")
        xt_high = sem("xt3_high")
        xt_split = sem("xt3_split")
        z_done = sem("z_done")
        z_read = sem("z_read")
        route = sem("route")
        logit_ready = sem("logit_ready")
        exp_ready = sem("exp_ready")
        hw_ready = sem("hw_ready")
        hwt_done = sem("hwt_done")
        hwt_high = sem("hwt_high")
        hwt_split = sem("hwt_split")
        e_done = sem("f_done")
        out_ready = sem("out_ready")
        stored = [sem(f"stored{b}") for b in range(2)]
        block = ctx.enter_context(nc.Block())

        def last_tile(i, t):
            return isinstance(i, int) and t == NT - 1

        @block.sync
        def _(sp):
            for n, (src, w, _, _) in enumerate(weights):
                after(sp, w_split, n - WB + 1)
                sp.dma_start(w_raw[n % WB][:, 0:w], src).then_inc(w_in[n % WB], 16)
                if n == 0:
                    sp.dma_start(emap[:], a["expert_map"].to_broadcast([P, NR])).then_inc(small_in, 16)
                    sp.dma_start(r_bias[:], a["b_router"].to_broadcast([P, NR])).then_inc(small_in, 16)
                    sp.dma_start(bias[:], a["b_base"].to_broadcast([P, D])).then_inc(bias_in, 16)

            def tile(i):
                for b in range(2):
                    t = 2 * i + b
                    sp.wait_ge(out_ready, t + 1)
                    sp.dma_start(a["out"][bass.ds(t, 1)].rearrange("a p d -> (a p) d"), out[b][:]).then_inc(stored[b], 16)
            repeat(sp, NT // 2, tile)
            for b in range(2):
                sp.wait_ge(stored[b], 16 * NT // 2)

        @block.gpsimd
        def _(pool):
            def tile(i):
                for b in range(2):
                    t = 2 * i + b
                    after(pool, xn_ready, t - 1)
                    pool.tensor_copy(norm_now[b][:], norm[:, bass.ds(t, 1), :].rearrange("p a k -> p (a k)")).then_inc(norm_got, 1)
                    if isinstance(t, int) and t == 0:
                        pool.wait_ge(bias_in, 16)
                    after(pool, out_ready, t - 1)
                    pool.tensor_tensor(rest[b][:], o[:, bass.ds(t, 1), :].rearrange("p a d -> p (a d)"), bias[:], ALU.add
                                       ).then_inc(rest_ready, 1)
            repeat(pool, NT // 2, tile)

        @block.scalar
        def _(act):
            def high(t, b):
                act.wait_ge(xt_done, t + 1)
                after(act, e_done, t - 1)
                act.activation(x_h[b][:], p_x[:], ACT.Copy).then_inc(xt_high, 1)
            for n, (_, w, wh, _) in enumerate(weights):
                act.wait_ge(w_in[n % WB], 16 * (n // WB + 1))
                raw = w_raw[n % WB][:, 0:w]
                act.activation(wh, raw.rearrange("p (k n) -> p k n", k=KT) if n == 0 else raw, ACT.Copy).then_inc(w_high, 1)
                if n == 0:
                    high(0, 0)

            def tile(i):
                for b in range(2):
                    t = 2 * i + b
                    act.wait_ge(logit_ready, t + 1)
                    act.activation(ex[:], logit[:], ACT.Exp, bias=peak[:, 1:2], accum_out=ex_sum[:, 0:1]).then_inc(exp_ready, 1)
                    if not last_tile(i, t):
                        high(t + 1, 1 - b)
                    act.wait_ge(hwt_done, t + 1)
                    after(act, e_done, t)
                    act.activation(hwt_h[:], p_hw[:, 0:P], ACT.Copy).then_inc(hwt_high, 1)
            repeat(act, NT // 2, tile)

        @block.vector
        def _(dve):
            passed = nc.alloc_semaphore("passed7")
            step = Chain(dve, map_step)

            def normalise(t, b):
                dve.wait_ge(norm_got, t + 1)
                after(dve, xt_done, t)
                dve.tensor_scalar(xn[:], o[:, bass.ds(t, 1), :].rearrange("p a d -> p (a d)"), norm_now[b][:, 0:1],
                                  norm_now[b][:, 1:2], ALU.subtract, ALU.mult).then_inc(xn_ready, 1)

            def low(t, b):
                dve.wait_ge(xt_high, t + 1)
                dve.tensor_tensor(x_l[b][:], p_x[:], wide(x_h[b][:]), ALU.subtract).then_inc(xt_split, 1)
            normalise(0, 0)
            for n, (_, w, wh, wl) in enumerate(weights):
                dve.wait_ge(w_high, n + 1)
                raw = w_raw[n % WB][:, 0:w]
                dve.tensor_tensor(wl, raw.rearrange("p (k n) -> p k n", k=KT) if n == 0 else raw, wide(wh), ALU.subtract
                                  ).then_inc(w_split, 1)
                if n == 0:
                    low(0, 0)
                    dve.wait_ge(small_in, 32)
                    step.link(dve.tensor_copy(emap_f[:], emap[:]))
                    for e in range(E):
                        ins = dve.tensor_scalar(onehot[:, e, :], emap_f[:], float(e), FFN_SCALE, ALU.is_equal, ALU.mult)
                    step.link(ins)
            r = Chain(dve, route, passed)

            def tile(i):
                r.begin(i)
                for b in range(2):
                    t = 2 * i + b
                    if not last_tile(i, t):
                        normalise(t + 1, 1 - b)
                    dve.wait_ge(z_done, t + 1)
                    r.link(dve.tensor_copy(z_half[:], p_z[:, ZW:2 * ZW]))
                    dve.tensor_tensor(z[:], p_z[:, 0:ZW], z_half[:], ALU.add).then_inc(z_read, 1)
                    dve.wait_ge(z_read, t + 1)
                    r.link(dve.tensor_tensor(logit[:], z[:, ER:ER + NR], r_bias[:], ALU.add))
                    r.link(dve.tensor_reduce(peak[:, 0:1], logit[:], AX_X, ALU.max))
                    dve.tensor_scalar(peak[:, 1:2], peak[:, 0:1], -1.0, None, ALU.mult).then_inc(logit_ready, 1)
                    dve.wait_ge(exp_ready, t + 1)
                    r.link(dve.reciprocal(ex_sum[:, 1:2], ex_sum[:, 0:1]))
                    r.link(dve.tensor_scalar(prob[:], ex[:], ex_sum[:, 1:2], None, ALU.mult), plainly=True)
                    r.link(dve.max(top8[:], prob[:]), plainly=True)
                    r.link(dve.match_replace(unchosen[:], top8[:], prob[:], 0.0))
                    r.link(dve.tensor_tensor(prob[:], prob[:], unchosen[:], ALU.subtract))
                    r.link(dve.tensor_tensor(spread[:], onehot[:], prob[:].unsqueeze(1).to_broadcast([P, E, NR]), ALU.mult))
                    r.link(dve.tensor_reduce(gate[:], spread[:], AX_X, ALU.add))
                    after(dve, hwt_done, t)
                    dve.tensor_tensor(hw[:].rearrange("p (e r) -> p e r", e=E), z[:, 0:ER].rearrange("p (e r) -> p e r", e=E),
                                      gate[:].unsqueeze(2).to_broadcast([P, E, ER // E]), ALU.mult).then_inc(hw_ready, 1)
                    if not last_tile(i, t):
                        low(t + 1, 1 - b)
                    dve.wait_ge(hwt_high, t + 1)
                    dve.tensor_tensor(hwt_l[:], p_hw[:, 0:P], wide(hwt_h[:]), ALU.subtract).then_inc(hwt_split, 1)
                    dve.wait_ge(e_done, t + 1)
                    dve.wait_ge(rest_ready, t + 1)
                    after(dve, stored[b], 16 * i)
                    dve.tensor_tensor(out[b][:], p_e[b][:], rest[b][:], ALU.add).then_inc(out_ready, 1)
            repeat(dve, NT // 2, tile)

        @block.tensor
        def _(pe):
            def turn(t):
                pe.wait_ge(xn_ready, t + 1)
                after(pe, xt_split, t)
                for k in range(KT):
                    last = pe.transpose(p_x[:, k, :], xn[:, k * P:(k + 1) * P], ident[:])
                last.then_inc(xt_done, 1)
            turn(0)

            def base(t, b, c):
                n = slice(c * HALF, (c + 1) * HALF)
                for k in range(KT):
                    if isinstance(t, int) and t == 0 and c == 0:
                        pe.wait_ge(w_split, k + 2)
                    product3(pe, p_e[b][:, n], x_h[b][:, k, :], x_l[b][:, k, :], w_h[:, k, n], w_l[:, k, n], k == 0, False)

            def tile(i):
                for b in range(2):
                    t = 2 * i + b
                    pe.wait_ge(xt_split, t + 1)
                    if isinstance(t, int) and t == 0:
                        pe.wait_ge(w_split, 1)
                    after(pe, z_read, t)
                    for k in range(KT):
                        if k == KT - 1:
                            pe.matmul(p_z[:, 0:ZW], x_l[b][:, k, :], z_hl[:, k, 0, :], start=False, stop=False)
                        last = pe.matmul(p_z[:, 0:2 * ZW], x_h[b][:, k, :], z_hl[:, k, :, :].rearrange("p a n -> p (a n)"),
                                         start=(k == 0), stop=(k == KT - 1))
                        if k < KT - 1:
                            pe.matmul(p_z[:, 0:ZW], x_l[b][:, k, :], z_hl[:, k, 0, :], start=False, stop=False)
                    last.then_inc(z_done, 1)
                    after(pe, out_ready, t - 1)
                    base(t, b, 0)
                    if not last_tile(i, t):
                        turn(t + 1)
                    pe.wait_ge(hw_ready, t + 1)
                    after(pe, hwt_split, t)
                    pe.transpose(p_hw[:, 0:P], hw[:], ident[:]).then_inc(hwt_done, 1)
                    base(t, b, 1)
                    pe.wait_ge(hwt_split, t + 1)
                    if isinstance(t, int) and t == 0:
                        pe.wait_ge(w_split, len(weights))
                    for c in range(2):
                        n = slice(c * HALF, (c + 1) * HALF)
                        last = product3(pe, p_e[b][:, n], hwt_h[:], hwt_l[:], l_h[:, n], l_l[:, n], False, True)
                    last.then_inc(e_done, 1)
            repeat(pe, NT // 2, tile)


def build(nc, a):
    with ExitStack() as ctx:
        ident = ctx.enter_context(nc.sbuf_tensor("ident", [P, P], F32))
        norm = ctx.enter_context(nc.sbuf_tensor("norm", [P, NT, 2], F32))
        ident_made = ctx.enter_context(nc.semaphore("ident_made"))
        with ExitStack() as front:
            xh = front.enter_context(nc.sbuf_tensor("xh", [P, KT, T], F32R))
            xl = front.enter_context(nc.sbuf_tensor("xl", [P, KT, T], F32R))
            phase_embed(nc, a, xh, xl, ident, ident_made)
            phase_qkv(nc, a, xh, xl, ident)
        o = ctx.enter_context(nc.sbuf_tensor("o", [P, NT, D], F32))
        phase_attention(nc, a, o, ident)
        phase_project(nc, a, o, norm, ident)
        phase_ffn(nc, a, o, norm, ident)


def kernel(x, mask_BS_i1_0, mask_BS_i0_1, L0_tok_weight, L0_tok_lora_A_cl, L0_tok_lora_B_cl, L0_tok_lora_A_lm,
           L0_tok_lora_B_lm, L0_tok_lora_A_cl_prime, L0_tok_lora_B_cl_prime, L0_attn_w_attn, L0_attn_b_attn,
           L0_attn_w_proj, L0_attn_b_proj, L0_ffn_base_W, L0_ffn_base_b, L0_ffn_router_W, L0_ffn_router_b,
           L0_ffn_A, L0_ffn_B, L0_ffn_expert_map):
    import concourse.bacc as bacc
    from concourse.bass_utils import run_bass_kernel_spmd

    arr = lambda v: np.asarray(v)
    slopes = (2.0 ** (-2.0 ** -(np.log2(H) - 3))) ** np.arange(1, H + 1, dtype=np.float32)
    slopes = slopes.astype(np.float32)
    slope_h = (slopes.view(np.uint32) & 0xFFFFF000).view(np.float32)
    w_attn = arr(L0_attn_w_attn).reshape(KT, P, 3, KT, P)
    z = np.concatenate([arr(L0_ffn_A).reshape(ER, D), arr(L0_ffn_router_W), np.zeros((1, D), np.float32)])
    ins = {
        "ids": np.stack([arr(m).reshape(NT, P) for m in (x, mask_BS_i1_0, mask_BS_i0_1)]).transpose(2, 0, 1).reshape(P, 3 * NT),
        "tok_w": arr(L0_tok_weight),
        "tok_a1": arr(L0_tok_lora_A_cl),
        "tok_a2": np.concatenate([arr(L0_tok_lora_A_lm), arr(L0_tok_lora_A_cl_prime)], 1),
        "lora_b": np.stack([arr(m) for m in (L0_tok_lora_B_cl, L0_tok_lora_B_lm, L0_tok_lora_B_cl_prime)], 1),
        "w_qkv": w_attn.transpose(3, 2, 1, 0, 4).reshape(3 * KT, P, KT * P),
        "b_qkv": arr(L0_attn_b_attn).reshape(3, KT, P).transpose(2, 0, 1),
        "query_rows": np.broadcast_to(np.stack([0 * slopes, 0 * slopes, slope_h, slopes - slope_h], 1).reshape(4 * H, 1), (4 * H, HALF)),
        "key_rows": np.stack([np.ones(T), np.ones(T), np.arange(T), np.arange(T)]).astype(np.float32),
        "slopes": np.broadcast_to(slopes, (P, H)),
        "w_proj": arr(L0_attn_w_proj),
        "b_proj": arr(L0_attn_b_proj).reshape(1, D),
        "w_base": arr(L0_ffn_base_W).T,
        "b_base": arr(L0_ffn_base_b).reshape(1, D),
        "w_z": z.T.reshape(KT, P, ZW).transpose(1, 0, 2).reshape(P, KT * ZW),
        "b_router": arr(L0_ffn_router_b).reshape(1, NR),
        "w_lora": arr(L0_ffn_B).transpose(0, 2, 1).reshape(ER, D),
        "expert_map": arr(L0_ffn_expert_map).reshape(1, NR),
    }
    nc = bacc.Bacc("TRN2", target_bir_lowering=False, num_devices=1)
    arrays, a = {}, {}
    for name, v in ins.items():
        v = np.ascontiguousarray(v)
        arrays["in_" + name] = v
        a[name] = nc.dram_tensor("in_" + name, v.shape, mybir.dt.from_np(v.dtype), kind="ExternalInput").ap()
    for name in ("qh", "ql", "kh", "kl"):
        a[name] = nc.dram_tensor(name + "_scratch", (D, T), F32, kind="Internal").ap()
    a["v_dram"] = nc.dram_tensor("v_scratch", (H, P, NT, VC), F32, kind="Internal").ap()
    a["rows_dram"] = nc.dram_tensor("rows_scratch", (4 * H, HALF), F32, kind="Internal").ap()
    a["h_dram"] = nc.dram_tensor("h_scratch", (NT, P, D), F32, kind="Internal").ap()
    a["out"] = nc.dram_tensor("out_dram", (NT, P, D), F32, kind="ExternalOutput").ap()
    build(nc, a)
    r = run_bass_kernel_spmd(nc, [arrays], core_ids=[0])
    return r.results[0]["out_dram"].reshape(1, T, D)
```
